# Optimizing a Trainium2 kernel written in Bass

```python
import numpy as np
import jax
import jax.numpy as jnp

def _softmax(x, axis=-1):
    return jax.nn.softmax(x, axis=axis)

def _gelu(x):
    return jax.nn.gelu(x, approximate=True)

def _silu(x):
    return jax.nn.silu(x)

def _sigmoid(x):
    return jax.nn.sigmoid(x)

def _layernorm(x, axis=-1, eps=1e-05):
    m = jnp.mean(x, axis=axis, keepdims=True)
    v = jnp.var(x, axis=axis, keepdims=True)
    return (x - m) / jnp.sqrt(v + eps)

def _scatter_add(tgt, idx, src, axis=0):
    return tgt.at[idx].add(src)

def _segment_sum(src, seg, n):
    return jax.ops.segment_sum(src, seg, n)
kernel_name = 'mk_gnn_preln_d4_gnn_r8_d6eeb2'

def setup_inputs(seed: int=0):
    np.random.seed(seed)
    _w = jnp.asarray

    def _rec_inputs():
        import jax
        import jax.numpy as jnp
        _gk = jax.random.key(seed)
        x = -8.776e-05 + 1 * jax.random.normal(jax.random.fold_in(_gk, 1), (1250, 512), jnp.float32)
        _s = jax.random.randint(jax.random.fold_in(_gk, 2), (10000,), 0, 1250, jnp.int32)
        _d = jax.random.randint(jax.random.fold_in(_gk, 3), (10000,), 0, 1250, jnp.int32)
        _loop = jnp.arange(1250, dtype=jnp.int32)
        src = jnp.concatenate([_s, _d, _loop])
        dst = jnp.concatenate([_d, _s, _loop])
        _o = jnp.argsort(dst, stable=True)
        src = src[_o]
        dst = dst[_o]
        edge_attr_128 = 0.000283511 + 1.00007 * jax.random.normal(jax.random.fold_in(_gk, 13), (21250, 128), jnp.float32)
        edge_weight = jax.random.uniform(jax.random.fold_in(_gk, 15), (21250,), jnp.float32, 0.0, 0.999998)
        edge_weight1 = jax.random.uniform(jax.random.fold_in(_gk, 16), (21250, 1), jnp.float32, 0.0, 0.999994)
        return (x, src, dst, edge_attr_128, edge_weight, edge_weight1)
    x, src, dst, edge_attr_128, edge_weight, edge_weight1 = _rec_inputs()

    def _L0_gnn_setup():
        import jax, jax.numpy as jnp
        import numpy as np
        N_NODES = 1250
        N_EDGES = 20000
        IN_DIM = 512
        OUT_DIM = 512
        LN_EPS = 1e-05
        key = jax.random.key(seed)
        k_x, k_src, k_ws, k_wn = jax.random.split(key, 4)
        x = jax.random.normal(k_x, (N_NODES, IN_DIM), dtype=jnp.float32)
        edge_src = jax.random.randint(k_src, (N_EDGES,), 0, N_NODES, dtype=jnp.int32)
        edge_dst = jnp.repeat(jnp.arange(N_NODES, dtype=jnp.int32), N_EDGES // N_NODES)
        deg = jnp.full((N_NODES,), float(N_EDGES // N_NODES), dtype=jnp.float32)
        scale = 1.0 / np.sqrt(IN_DIM)
        W_self = jax.random.normal(k_ws, (OUT_DIM, IN_DIM), dtype=jnp.float32) * scale
        W_neigh = jax.random.normal(k_wn, (OUT_DIM, IN_DIM), dtype=jnp.float32) * scale
        bias = jnp.zeros((OUT_DIM,), dtype=jnp.float32)
        gamma = jnp.ones((OUT_DIM,), dtype=jnp.float32)
        beta = jnp.zeros((OUT_DIM,), dtype=jnp.float32)
        return {'x': x, 'edge_src': edge_src, 'edge_dst': edge_dst, 'deg': deg, 'W_self': W_self, 'W_neigh': W_neigh, 'bias': bias, 'gamma': gamma, 'beta': beta}
    _L0_gnn_all = _L0_gnn_setup()
    _L0_gnn_in = {k: v for k, v in _L0_gnn_all.items() if k in ('W_self', 'W_neigh', 'bias', 'gamma', 'beta')}
    del _L0_gnn_all

    def _L1_gnn_setup():
        import jax, jax.numpy as jnp
        import numpy as np
        EPS = 1e-12

        def _gcn_conv(x, W, b, src, dst, w, n_nodes):
            h = x @ W
            deg = jax.ops.segment_sum(w, dst, num_segments=n_nodes)
            dinv = jnp.where(deg > 0, jax.lax.rsqrt(deg), 0.0)
            norm = dinv[src] * w * dinv[dst]
            out = jax.ops.segment_sum(h[src] * norm[:, None], dst, num_segments=n_nodes)
            return out + b
        key = jax.random.key(seed)
        ks = jax.random.split(key, 6)
        N, E, F_in, F_hid, F_out = (6250, 50000, 512, 256, 512)
        node_features = jax.random.normal(ks[0], (N, F_in), dtype=jnp.float32)
        node_features = node_features / jnp.linalg.norm(node_features, axis=-1, keepdims=True)
        edge_index = jax.random.randint(ks[1], (2, E), 0, N, dtype=jnp.int64)
        edge_weight = jax.random.uniform(ks[2], (E,), dtype=jnp.float32)
        W1 = jax.random.normal(ks[3], (F_in, F_hid), dtype=jnp.float32) / np.sqrt(F_in)
        b1 = jnp.zeros((F_hid,), dtype=jnp.float32)
        W2 = jax.random.normal(ks[4], (F_hid, F_out), dtype=jnp.float32) / np.sqrt(F_hid)
        b2 = jnp.zeros((F_out,), dtype=jnp.float32)
        return {'node_features': node_features, 'edge_index': edge_index, 'edge_weight': edge_weight, 'W1': W1, 'b1': b1, 'W2': W2, 'b2': b2}
    _L1_gnn_all = _L1_gnn_setup()
    _L1_gnn_in = {k: v for k, v in _L1_gnn_all.items() if k in ('W1', 'b1', 'W2', 'b2')}
    del _L1_gnn_all

    def _L2_gnn_setup():
        import jax, jax.numpy as jnp
        import numpy as np
        N, E = (1250, 18750)
        HD, ED = (512, 128)
        BN_EPS = 1e-05
        key = jax.random.key(seed)
        ks = jax.random.split(key, 16)
        s = 0.02
        return {'h': jax.random.normal(ks[0], (N, HD), jnp.float32), 'edge_index': jax.random.randint(ks[1], (2, E), 0, N, jnp.int32), 'edge_attr': jax.random.normal(ks[2], (E, ED), jnp.float32), 'W1': jax.random.normal(ks[3], (HD, HD + ED), jnp.float32) * s, 'b1': jnp.zeros((HD,), jnp.float32), 'W2': jax.random.normal(ks[4], (HD, HD), jnp.float32) * s, 'b2': jnp.zeros((HD,), jnp.float32), 'W_ih': jax.random.normal(ks[5], (3 * HD, HD), jnp.float32) * s, 'W_hh': jax.random.normal(ks[6], (3 * HD, HD), jnp.float32) * s, 'b_ih': jnp.zeros((3 * HD,), jnp.float32), 'b_hh': jnp.zeros((3 * HD,), jnp.float32), 'gamma': jnp.ones((HD,), jnp.float32), 'beta': jnp.zeros((HD,), jnp.float32), 'run_mean': jnp.zeros((HD,), jnp.float32), 'run_var': jnp.ones((HD,), jnp.float32)}
    _L2_gnn_all = _L2_gnn_setup()
    _L2_gnn_in = {k: v for k, v in _L2_gnn_all.items() if k in ('W1', 'b1', 'W2', 'b2', 'W_ih', 'W_hh', 'b_ih', 'b_hh', 'gamma', 'beta', 'run_mean', 'run_var')}
    del _L2_gnn_all

    def _L3_gnn_setup():
        import jax, jax.numpy as jnp
        import numpy as np
        N_NODES = 6250
        N_EDGES = 20000
        D_IN = 512
        D_OUT = 512
        key = jax.random.key(seed)
        k1, k2, k3, k4, k5, k6 = jax.random.split(key, 6)
        feature = jax.random.normal(k1, (N_NODES, D_IN), dtype=jnp.float32)
        edge_w = jax.random.uniform(k2, (N_EDGES, 1), dtype=jnp.float32)
        W = jax.random.normal(k3, (D_OUT, D_IN), dtype=jnp.float32) / np.sqrt(D_IN)
        b = jax.random.normal(k4, (D_OUT,), dtype=jnp.float32) * 0.01
        src = jax.random.randint(k5, (N_EDGES,), 0, N_NODES, dtype=jnp.int32)
        dst = jax.random.randint(k6, (N_EDGES,), 0, N_NODES, dtype=jnp.int32)
        return {'feature': feature, 'edge_w': edge_w, 'W': W, 'b': b, 'src': src, 'dst': dst}
    _L3_gnn_all = _L3_gnn_setup()
    _L3_gnn_in = {k: v for k, v in _L3_gnn_all.items() if k in ('W', 'b')}
    del _L3_gnn_all
    return {'x': x, 'src': src, 'dst': dst, 'edge_attr_128': edge_attr_128, 'edge_weight': edge_weight, 'edge_weight1': edge_weight1, 'L0_gnn_W_self': _L0_gnn_in['W_self'], 'L0_gnn_W_neigh': _L0_gnn_in['W_neigh'], 'L0_gnn_bias': _L0_gnn_in['bias'], 'L0_gnn_gamma': _L0_gnn_in['gamma'], 'L0_gnn_beta': _L0_gnn_in['beta'], 'L1_gnn_W1': _L1_gnn_in['W1'], 'L1_gnn_b1': _L1_gnn_in['b1'], 'L1_gnn_W2': _L1_gnn_in['W2'], 'L1_gnn_b2': _L1_gnn_in['b2'], 'L2_gnn_W1': _L2_gnn_in['W1'], 'L2_gnn_b1': _L2_gnn_in['b1'], 'L2_gnn_W2': _L2_gnn_in['W2'], 'L2_gnn_b2': _L2_gnn_in['b2'], 'L2_gnn_W_ih': _L2_gnn_in['W_ih'], 'L2_gnn_W_hh': _L2_gnn_in['W_hh'], 'L2_gnn_b_ih': _L2_gnn_in['b_ih'], 'L2_gnn_b_hh': _L2_gnn_in['b_hh'], 'L2_gnn_gamma': _L2_gnn_in['gamma'], 'L2_gnn_beta': _L2_gnn_in['beta'], 'L2_gnn_run_mean': _L2_gnn_in['run_mean'], 'L2_gnn_run_var': _L2_gnn_in['run_var'], 'L3_gnn_W': _L3_gnn_in['W'], 'L3_gnn_b': _L3_gnn_in['b']}

def reference(x, src, dst, edge_attr_128, edge_weight, edge_weight1, L0_gnn_W_self, L0_gnn_W_neigh, L0_gnn_bias, L0_gnn_gamma, L0_gnn_beta, L1_gnn_W1, L1_gnn_b1, L1_gnn_W2, L1_gnn_b2, L2_gnn_W1, L2_gnn_b1, L2_gnn_W2, L2_gnn_b2, L2_gnn_W_ih, L2_gnn_W_hh, L2_gnn_b_ih, L2_gnn_b_hh, L2_gnn_gamma, L2_gnn_beta, L2_gnn_run_mean, L2_gnn_run_var, L3_gnn_W, L3_gnn_b):
    import jax
    import jax.numpy as jnp

    def _L0_gnn_ref(x, edge_src, edge_dst, deg, W_self, W_neigh, bias, gamma, beta):
        import jax, jax.numpy as jnp
        import numpy as np
        N_NODES = 1250
        N_EDGES = 20000
        IN_DIM = 512
        OUT_DIM = 512
        LN_EPS = 1e-05
        n = x.shape[0]
        h_self = jnp.einsum('nd,od->no', x, W_self)
        neigh_sum = jax.ops.segment_sum(x[edge_src], edge_dst, num_segments=n)
        neigh_mean = neigh_sum / jnp.maximum(deg, 1.0)[:, None]
        h_neigh = jnp.einsum('nd,od->no', neigh_mean, W_neigh)
        h = h_self + h_neigh + bias
        mu = jnp.mean(h, axis=-1, keepdims=True)
        var = jnp.mean(jnp.square(h - mu), axis=-1, keepdims=True)
        h = (h - mu) * jax.lax.rsqrt(var + LN_EPS)
        return h * gamma + beta

    def _L1_gnn_ref(node_features, edge_index, edge_weight, W1, b1, W2, b2):
        import jax, jax.numpy as jnp
        import numpy as np
        EPS = 1e-12

        def _gcn_conv(x, W, b, src, dst, w, n_nodes):
            h = x @ W
            deg = jax.ops.segment_sum(w, dst, num_segments=n_nodes)
            dinv = jnp.where(deg > 0, jax.lax.rsqrt(deg), 0.0)
            norm = dinv[src] * w * dinv[dst]
            out = jax.ops.segment_sum(h[src] * norm[:, None], dst, num_segments=n_nodes)
            return out + b
        N = node_features.shape[0]
        loop = jnp.arange(N, dtype=edge_index.dtype)
        src = jnp.concatenate([edge_index[0], loop])
        dst = jnp.concatenate([edge_index[1], loop])
        w = jnp.concatenate([edge_weight, jnp.ones((N,), dtype=edge_weight.dtype)])
        x = _gcn_conv(node_features, W1, b1, src, dst, w, N)
        x = jax.nn.relu(x)
        x = _gcn_conv(x, W2, b2, src, dst, w, N)
        nrm = jnp.linalg.norm(x, axis=-1, keepdims=True)
        return x / jnp.maximum(nrm, EPS)

    def _L2_gnn_ref(h, edge_index, edge_attr, W1, b1, W2, b2, W_ih, W_hh, b_ih, b_hh, gamma, beta, run_mean, run_var):
        import jax, jax.numpy as jnp
        import numpy as np
        N, E = (1250, 18750)
        HD, ED = (512, 128)
        BN_EPS = 1e-05
        src, dst = (edge_index[0], edge_index[1])
        m_in = jnp.concatenate([h[src], edge_attr], axis=1)
        m = jax.nn.relu(m_in @ W1.T + b1) @ W2.T + b2
        agg = jax.ops.segment_sum(m, dst, num_segments=h.shape[0])
        gi = agg @ W_ih.T + b_ih
        gh = h @ W_hh.T + b_hh
        i_r, i_z, i_n = jnp.split(gi, 3, axis=1)
        h_r, h_z, h_n = jnp.split(gh, 3, axis=1)
        r = jax.nn.sigmoid(i_r + h_r)
        z = jax.nn.sigmoid(i_z + h_z)
        n = jnp.tanh(i_n + r * h_n)
        h_new = (1.0 - z) * n + z * h
        bn = gamma * (h_new - run_mean) * jax.lax.rsqrt(run_var + BN_EPS) + beta
        return h + bn

    def _L3_gnn_ref(feature, edge_w, W, b, src, dst):
        import jax, jax.numpy as jnp
        import numpy as np
        N_NODES = 6250
        N_EDGES = 20000
        D_IN = 512
        D_OUT = 512
        m = feature[src] * edge_w
        agg = jax.ops.segment_sum(m, dst, num_segments=feature.shape[0])
        return agg @ W.T + b
    edge_index = jnp.stack([src, dst])
    deg = jnp.maximum(jax.ops.segment_sum(jnp.ones(dst.shape, jnp.float32), dst, num_segments=1250), 1.0)
    h = jnp.maximum(_layernorm(x, axis=-1), 0.0)
    x = x + _L0_gnn_ref(h, src, dst, deg, L0_gnn_W_self, L0_gnn_W_neigh, L0_gnn_bias, L0_gnn_gamma, L0_gnn_beta)
    h = jnp.maximum(_layernorm(x, axis=-1), 0.0)
    x = x + _L1_gnn_ref(h, edge_index, edge_weight, L1_gnn_W1, L1_gnn_b1, L1_gnn_W2, L1_gnn_b2)
    h = jnp.maximum(_layernorm(x, axis=-1), 0.0)
    x = x + _L2_gnn_ref(h, edge_index, edge_attr_128, L2_gnn_W1, L2_gnn_b1, L2_gnn_W2, L2_gnn_b2, L2_gnn_W_ih, L2_gnn_W_hh, L2_gnn_b_ih, L2_gnn_b_hh, L2_gnn_gamma, L2_gnn_beta, L2_gnn_run_mean, L2_gnn_run_var)
    h = jnp.maximum(_layernorm(x, axis=-1), 0.0)
    x = x + _L3_gnn_ref(h, edge_weight1, L3_gnn_W, L3_gnn_b, src, dst)
    return x

_drawn_inputs = setup_inputs


def setup_inputs(seed=0):
    import zlib

    import numpy as np

    out = dict(_drawn_inputs(seed))
    spreads = {'L0_gnn_bias': (0.0, 0.1),
     'L0_gnn_gamma': (1.0, 0.2),
     'L0_gnn_beta': (0.0, 0.1),
     'L1_gnn_b1': (0.0, 2.0),
     'L1_gnn_b2': (0.0, 2.0),
     'L2_gnn_b1': (0.0, 0.287),
     'L2_gnn_b2': (0.0, 0.1),
     'L2_gnn_b_ih': (0.0, 0.462),
     'L2_gnn_b_hh': (0.0, 0.746),
     'L2_gnn_gamma': (1.0, 0.2),
     'L2_gnn_beta': (0.0, 0.1),
     'L2_gnn_run_mean': (0.0, 0.1),
     'L2_gnn_run_var': (1.0, 0.562)}
    factors = {'edge_attr_128': 4.786,
     'edge_weight': 64.0,
     'L3_gnn_b': 34.344,
     'L1_gnn_W1': 6.128,
     'L1_gnn_W2': 2.891}
    for name, (base, spread) in spreads.items():
        noise = np.random.default_rng([zlib.crc32(name.encode()), seed]).standard_normal(out[name].shape)
        drawn = base * np.exp(spread * noise) if base else spread * noise
        out[name] = jnp.asarray(drawn.astype(out[name].dtype))
    for name, factor in factors.items():
        out[name] = (out[name] * factor).astype(out[name].dtype)
    return out
```

```python
from contextlib import ExitStack

import numpy as np
import concourse.bass as bass
from concourse import mybir

F32 = mybir.dt.float32
I32 = mybir.dt.int32
BF16 = mybir.dt.bfloat16
ALU = mybir.AluOpType
ACT = mybir.ActivationFunctionType
AX_X = mybir.AxisListType.X

P = 128
N = 1250
E = 21250
D = 512
DH = 256
DE = 128
NT = -(-N // P)
KT = D // P
LAST = N - (NT - 1) * P
JV = E // P
REST = E - JV * P
COL = 8
J = -(-(JV + 1) // COL) * COL
PAIR = 2 * P
CELLS = NT * NT
CELL_PAIRS = (E + CELLS * (PAIR - 1)) // PAIR
CELL_PAIRS = -(-CELL_PAIRS // 4) * 4
CELL_CHUNKS = 2 * CELL_PAIRS
DST_PAIRS = -(-((E + NT * (PAIR - 1)) // PAIR) // 4) * 4
DST_CHUNKS = 2 * DST_PAIRS
SPARE = 2
EW = DE + 4
LN_EPS = 1e-5
BN_EPS = 1e-5
GROUP = 8


def at_least(eng, semaphore, value):
    if not isinstance(value, int) or value > 0:
        eng.wait_ge(semaphore, value)


def numbered(names):
    return {name: n for n, name in enumerate(names)}


def build_gnn(nc, x_in, src_in, dst_in, attr_in, w_in, w1_in, w_self, w_neigh, b0, gamma0, beta0,
              w1_1, b1_1, w2_1, b2_1, w1_2, b1_2, w2_2, b2_2, w_ih, w_hh, b_ih, b_hh,
              gamma2, beta2, mean2, var2, w_3, b_3, out):
    cell_rows = nc.dram_tensor("cell_rows", (P * (CELL_CHUNKS + SPARE), 4), F32, kind="Internal").ap()
    dst_rows = nc.dram_tensor("dst_rows", (P * (DST_CHUNKS + SPARE), EW), F32, kind="Internal").ap()
    p_rows = nc.dram_tensor("p_rows", (NT * P, D), F32, kind="Internal").ap()
    wt_names = ["w1h", "w2", "ih0", "ih1", "ih2", "hh0", "hh1", "hh2", "w3"]
    wt_dram = {n: nc.dram_tensor("wt_" + n, (P, KT * D), F32, kind="Internal").ap() for n in wt_names}
    w1e_dram = nc.dram_tensor("wt_w1e", (P, D), F32, kind="Internal").ap()

    with ExitStack() as ctx:
        def sb(name, shape, dt=F32):
            return ctx.enter_context(nc.sbuf_tensor(name, shape, dt))

        def sem(name):
            return ctx.enter_context(nc.semaphore(name))

        xs = sb("xs", [P, NT, D])
        h = sb("h", [P, NT, D])
        g = sb("g", [P, NT * D])
        adj = sb("adj", [P, 2 * CELLS * P])
        ws = sb("ws", [P, 2, KT, D])
        tiles = sb("tiles", [P, 4, D])
        vec = sb("vec", [P, 3, D])
        cellm = sb("cellm", [P, CELL_CHUNKS, 4])
        pay1 = sb("pay1", [P, J, 4])
        idx1 = sb("idx1", [P, J], I32)
        idx2 = sb("idx2", [P, J], I32)
        pay2 = sb("pay2", [P, J, 2])
        ident = sb("ident", [P, P])
        iota1 = sb("iota1", [P, P])
        ones = sb("ones", [P, 1])
        stats = sb("stats", [P, 6])
        mv = sb("mv", [P, NT, 2])
        rstd = sb("rstd", [P, NT])
        deg = sb("deg", [P, 2 * NT])
        invc = sb("invc", [P, NT])
        dinv = sb("dinv", [P, NT])
        dmask = sb("dmask", [P, NT])
        tabf = sb("tabf", [P, 4])
        places_at = sb("places_at", [1, CELL_PAIRS + DST_PAIRS], I32)
        cell_at = places_at[:, 0:CELL_PAIRS]
        dst_at = places_at[:, CELL_PAIRS:]
        gidx = sb("gidx", [P, GROUP], I32)
        cring = sb("cring", [P, 4, 4])
        pb = [ctx.enter_context(nc.psum_tensor(f"pb{n}", [P, 512], F32)) for n in range(8)]

        adj3 = adj[:].rearrange("p (m c d) -> p m c d", m=2, c=CELLS)
        adj_flat = adj[:].rearrange("p (m f) -> p m f", m=2)
        wst = g[:, 0:2 * KT * 640].rearrange("p (b k f) -> p b k f", b=2, k=KT)

        B1 = CELLS + 1
        B2 = NT + 1
        half = -(-B1 // 2)
        SW = B1 * J // 2
        oh = adj[:, 0:SW].bitcast(BF16).rearrange("p (b j) -> p b j", b=B1)
        cs = adj[:, SW:2 * SW].bitcast(BF16).rearrange("p (b j) -> p b j", b=B1)
        sel = adj[:, 2 * SW:2 * SW + half * J].rearrange("p (b j) -> p b j", b=half)
        assert 2 * SW + half * J <= 2 * CELLS * P

        xf = xs[:].rearrange("p t d -> p (t d)")
        cursor = [0]

        def temp(words, dt=F32):
            a = xf[:, cursor[0]:cursor[0] + words]
            cursor[0] += words
            return a if dt is F32 else a.bitcast(dt)

        srci, dsti = temp(J, I32), temp(J, I32)
        t_i = temp(J, I32)
        t_j = temp(J, I32)
        st_f, dt_f, cell_f = temp(J), temp(J), temp(J)
        cell_b = temp(J // 2).bitcast(BF16)
        dt_b = temp(J // 2).bitcast(BF16)
        wt_t, w1t_t = temp(J), temp(J)
        sum_a, sum_b = temp(J), temp(J)
        iob = temp(52).bitcast(BF16)
        iob_f = temp(104)
        tri = temp(P)
        onesq = temp(P)
        ptot = temp(B1)
        pcum = temp(B1)
        cnts = temp(B1)
        cnti = temp(B1, I32)
        nsup = temp(B1)
        endp = temp(B1)
        offs = temp(B1)
        pidx = temp(2)
        cmp_t = temp(B1)
        assert cursor[0] <= NT * D

        ohs = g[:, 0:GROUP * P].rearrange("p (c s) -> p c s", c=GROUP)
        ohd = g[:, GROUP * P:(GROUP + 8) * P].rearrange("p (c m d) -> p c m d", c=4, m=2)
        ohs3 = adj[:, CELLS * P:(CELLS + GROUP) * P].rearrange("p (c s) -> p c s", c=GROUP)
        ohd3 = adj[:, (CELLS + GROUP) * P:(CELLS + GROUP + 4) * P].rearrange("p (c d) -> p c d", c=4)
        agg0 = g[:, 2048:2048 + 2 * D].rearrange("p (b f) -> p b f", b=2)
        aggT0 = g[:, 3072:3072 + 2 * D].rearrange("p (b k n) -> p b k n", b=2, k=KT)
        y0 = g[:, 4096:4096 + 2 * D].rearrange("p (b f) -> p b f", b=2)
        hT = tiles[:, 0:2].rearrange("p b (k n) -> p b k n", k=KT)
        g1 = g[:, 0:NT * DH].rearrange("p (t f) -> p t f", t=NT)
        x1 = g[:, NT * DH:2 * NT * DH].rearrange("p (t f) -> p t f", t=NT)
        a1 = tiles[:, 2, :].rearrange("p (b f) -> p b f", b=2)
        a1T = tiles[:, 3, :].rearrange("p (b k n) -> p b k n", b=2, k=2)
        y1 = tiles[:, 0:2]
        w1_sb = ws[:, 0].rearrange("p k f -> p (k f)")[:, 0:KT * DH].rearrange("p (k f) -> p k f", k=KT)
        w2_sb = ws[:, 0].rearrange("p k f -> p (k f)")[:, KT * DH:KT * DH + 2 * D].rearrange("p (k f) -> p k f", k=2)
        r2 = g[:].rearrange("p (t f) -> p t f", t=NT)
        gru_w = adj[:, 0:6 * KT * D].rearrange("p (b k f) -> p b k f", b=6, k=KT)
        acur = [6 * KT * D]

        def adj_part(words):
            a = adj[:, acur[0]:acur[0] + words]
            acur[0] += words
            return a

        rows = adj_part(GROUP * D).rearrange("p (c f) -> p c f", c=GROUP)
        erow = adj_part(GROUP * EW).rearrange("p (c f) -> p c f", c=GROUP)
        erow_i = erow.bitcast(I32)
        erowT = adj_part(4 * P).rearrange("p (c f) -> p c f", c=4)
        ohe = adj_part(GROUP * P).rearrange("p (c f) -> p c f", c=GROUP)
        w1e_sb = adj_part(D)
        gates = rows
        vec2 = adj_part(8 * D).rearrange("p (v f) -> p v f", v=8)
        assert acur[0] <= 2 * CELLS * P
        b1_v, b2_v, bx_v, by_v, bz_v, bw_v, sc_v, sh_v = (vec2[:, k] for k in range(8))
        scratch_v = vec
        ering = sb("ering", [P, COL, EW])
        ering_i = ering[:].bitcast(I32)

        loaded = sem("loaded")
        edges_loaded = sem("edges_loaded")
        raw_loaded = [sem(f"raw_loaded{k}") for k in range(2)]
        wt_stored = [sem(f"wt_stored{k}") for k in range(2)]
        vec_loaded = sem("vec_loaded")
        const_ready = sem("const_ready")
        zero_ready = sem("zero_ready")
        zeroed = sem("zeroed")
        step = sem("step")
        totals_ready = sem("totals_ready")
        order_ready = [sem(f"order_ready{k}") for k in range(2)]
        vec_folded = sem("vec_folded")
        x1_ready = sem("x1_ready")
        square_ready, root_ready = sem("square_ready"), sem("root_ready")
        sums_clear = sem("sums_clear")
        for_act, act_read = sem("for_act"), sem("act_read")
        for_dve, dve_read = sem("for_dve"), sem("dve_read")
        c_ready = sem("c_ready")
        pool_passed = sem("pool_passed")
        c_scattered = [sem(f"c_scattered{k}") for k in range(4)]
        cells_loaded = sem("cells_loaded")
        e_loaded = [sem(f"e_loaded{k}") for k in range(2)]
        e_ready = sem("e_ready")
        e_scattered = [sem(f"e_scattered{k}") for k in range(COL)]
        x_free = sem("x_free")
        builds = []
        for k in range(2):
            builds.append(dict(dist=sem(f"src_distance{k}"), src=sem(f"src_hot{k}"), dst=sem(f"dst_hot{k}"), mm=sem(f"block_done{k}"), add=sem(f"block_added{k}")))
        h_ready = sem("h_ready")
        w_loaded = sem("w_loaded")
        p_stored = [sem(f"p_stored{k}") for k in range(2)]
        g_ready = sem("g_ready")
        g_landed = [sem(f"g_landed{k}") for k in range(GROUP)]
        erow_landed = [sem(f"erow_landed{k}") for k in range(2)]
        turned, turned_read = sem("turned"), sem("turned_read")
        edge_mm, msg_added, msg_ready = sem("edge_mm"), sem("msg_added"), sem("msg_ready")
        hot_ready, summed, sums_added = sem("hot_ready"), sem("summed"), sem("sums_added")
        gru_loaded = sem("gru_loaded")
        w1e_loaded = sem("w1e_loaded")
        vec2_loaded = sem("vec2_loaded")
        gate_in, gate_out = sem("gate_in"), sem("gate_out")
        x_done = sem("x_done")
        stored = sem("stored")

        blocks = [("w1h", 0), ("w2", 0), ("ih0", 0), ("ih1", 1), ("ih2", 2), ("hh0", 0), ("hh1", 1), ("hh2", 2),
                  ("w3", 0), ("self", 0), ("neigh", 0)]
        act_jobs = [("w", n, k) for n in range(len(blocks)) for k in range(5 if n == 0 else KT)]
        act_jobs += [(kind, t) for t in range(NT) for kind in ("h0T", "agg0T")]
        act_jobs += [("h1T", t) for t in range(NT)] + [("a1T", t) for t in range(NT)]
        act_jobs += [("h2T", t) for t in range(NT)]
        act_jobs += [("r2T", 0), ("hgT", 0)]
        for t in range(NT):
            act_jobs += [("agg2T", t)] + ([("r2T", t + 1), ("hgT", t + 1)] if t + 1 < NT else [])
        act_jobs += [("agg3T", t) for t in range(NT)]
        A = numbered(act_jobs)
        dve_jobs = ["prefix1", "prefix2", "tables", "deg", ("agg0", 0)]
        for t in range(NT):
            dve_jobs += ([("agg0", t + 1)] if t + 1 < NT else []) + [("y0", t)]
        dve_jobs += [("g1", t) for t in range(NT)] + [("x1", t) for t in range(NT)] + [("a1", 0)]
        for t in range(NT):
            dve_jobs += ([("a1", t + 1)] if t + 1 < NT else []) + [("y1", t)]
        dve_jobs += [("p2", t) for t in range(NT)]
        for t in range(NT):
            dve_jobs += [("agg2", t), ("r", t), ("z", t), ("hn", t), ("in", t)]
        dve_jobs += [("agg3", 0)]
        for t in range(NT):
            dve_jobs += ([("agg3", t + 1)] if t + 1 < NT else []) + [("y3", t)]
        V = numbered(dve_jobs)
        root_jobs = ["h0", "dinv"] + [("y0", t) for t in range(NT)] + ["h1"]
        root_jobs += [(kind, t) for t in range(NT) for kind in ("n1", "h2")] + ["bn", "h3"]
        ROOT = numbered(root_jobs)
        wj = {b: A[("w", b, KT - 1 if b else 4)] + 1 for b in range(len(blocks))}
        raw_src = {"w1h": w1_2, "w2": w2_2, "ih0": w_ih, "ih1": w_ih, "ih2": w_ih, "hh0": w_hh, "hh1": w_hh,
                   "hh2": w_hh, "w3": w_3, "self": w_self, "neigh": w_neigh}

        def act_bank(job):
            return pb[A[job] % 4]

        def dve_bank(job):
            return pb[4 + V[job] % 4]

        block = ctx.enter_context(nc.Block())

        def store_weights(sp, n):
            sp.wait_ge(act_read, wj[n])
            if n == 0:
                sp.dma_start(w1e_dram, tiles[:, 0]).then_inc(wt_stored[0], 16)
            sp.dma_start(wt_dram[blocks[n][0]], ws[:, n % 2].rearrange("p k f -> p (k f)")).then_inc(wt_stored[n % 2], 16)

        @block.sync
        def _(sp):
            def column(dst, src1d):
                sp.dma_start(dst[:, 0:JV], src1d[0:JV * P].rearrange("(p j) -> p j", j=JV)).then_inc(edges_loaded, 16)
                sp.dma_start(dst[0:REST, JV:JV + 1], src1d[JV * P:E].rearrange("(p j) -> p j", j=1)).then_inc(edges_loaded, 16)

            sp.wait_ge(const_ready, 1)
            column(srci, src_in)
            column(dsti, dst_in)
            column(wt_t, w_in)
            column(w1t_t, w1_in.rearrange("e a -> (e a)"))
            sp.wait_ge(zero_ready, 1)
            zc = (CELL_CHUNKS + SPARE) * 4
            sp.dma_start(cell_rows.rearrange("(p c) w -> p (c w)", p=P), h[:].rearrange("p t d -> p (t d)")[:, 0:zc]).then_inc(zeroed, 16)
            zd = (DST_CHUNKS + SPARE) * EW
            part = zd // 6
            dz = dst_rows.rearrange("(p c) w -> p (c w)", p=P)
            for k in range(6):
                sp.dma_start(dz[:, k * part:(k + 1) * part], h[:].rearrange("p t d -> p (t d)")[:, 0:part]).then_inc(zeroed, 16)
            for n, (name, third) in enumerate(blocks):
                if n >= 2:
                    sp.wait_ge(for_act, wj[n - 2])
                wide = DE + D if name == "w1h" else D
                raw = raw_src[name]
                sp.dma_start(wst[:, n % 2, :, 0:wide],
                             raw[third * D:(third + 1) * D, :].rearrange("(o p) f -> p o f", p=P)).then_inc(raw_loaded[n % 2], 16)
                if n >= 1 and n - 1 < len(wt_names):
                    store_weights(sp, n - 1)
            for k, v in enumerate((b0, gamma0, beta0)):
                sp.dma_start(vec[:, k], v.rearrange("(a f) -> a f", a=1).to_broadcast([P, D])).then_inc(vec_loaded, 16)
            sp.wait_ge(x_free, 1)
            for t in range(NT - 1):
                sp.dma_start(xs[:, t], x_in[t * P:(t + 1) * P, :]).then_inc(loaded, 16)
            sp.dma_start(xs[0:LAST, NT - 1], x_in[(NT - 1) * P:N, :]).then_inc(loaded, 16)
            for k in range(4):
                sp.wait_ge(c_scattered[k], 16 * (J // 4))
            sp.dma_start(cellm[:].rearrange("p c w -> p (c w)"),
                         cell_rows.rearrange("(p c) w -> p (c w)", p=P)[:, 0:CELL_CHUNKS * 4]).then_inc(cells_loaded, 16)
            edge_v = attr_in[0:JV * P, :].rearrange("(p j) f -> p j f", j=JV)
            for q in range(2):
                sp.dma_start(ering[:, 4 * q:4 * q + 4, 0:DE], edge_v[:, 4 * q:4 * q + 4, :]).then_inc(e_loaded[q], 16)
            turns = J // COL

            def edge_turn(i, last):
                for q in range(2):
                    for k in range(4 * q, 4 * q + 4):
                        sp.wait_ge(e_scattered[k], 16 * i)
                    if not last or q == 0:
                        sp.dma_start(ering[:, 4 * q:4 * q + 4, 0:DE],
                                     edge_v[:, bass.ds(COL * i + 4 * q, 4), :]).then_inc(e_loaded[q], 16)
                    else:
                        k = JV - COL * i
                        sp.dma_start(ering[:, 4:k, 0:DE], edge_v[:, COL * i + 4:JV, :]).then_inc(e_loaded[q], 16)
                        sp.dma_start(ering[0:REST, k, 0:DE], attr_in[JV * P:E, :]).then_inc(e_loaded[q], 16)

            with sp.Fori(1, turns - 1) as i:
                edge_turn(i, False)
            edge_turn(turns - 1, True)
            sp.wait_ge(wt_stored[0], 16 * 6)
            sp.wait_ge(wt_stored[1], 16 * 4)
            sp.wait_ge(h_ready, 2 * NT)
            sp.dma_start(w1_sb, w1_1.rearrange("(k p) f -> p k f", p=P)).then_inc(w_loaded, 16)
            sp.dma_start(w2_sb, w2_1.rearrange("(k p) f -> p k f", p=P)).then_inc(w_loaded, 16)
            sp.dma_start(ws[:, 1].rearrange("p k f -> p (k f)"), wt_dram["w1h"]).then_inc(w_loaded, 16)
            sp.dma_start(vec[:, 0, 0:DH], b1_1.rearrange("(a f) -> a f", a=1).to_broadcast([P, DH])).then_inc(vec_loaded, 16)
            sp.dma_start(vec[:, 1], b2_1.rearrange("(a f) -> a f", a=1).to_broadcast([P, D])).then_inc(vec_loaded, 16)
            sp.wait_ge(h_ready, 3 * NT)
            sp.dma_start(ws[:, 0].rearrange("p k f -> p (k f)"), wt_dram["w2"]).then_inc(w_loaded, 16)
            for k, v in enumerate((b1_2, b2_2, b_ih[0:D], b_ih[D:2 * D], b_ih[2 * D:3 * D], b_hh[2 * D:3 * D], gamma2, beta2)):
                sp.dma_start(vec2[:, k], v.rearrange("(a f) -> a f", a=1).to_broadcast([P, D])).then_inc(vec2_loaded, 16)
            sp.dma_start(vec[:, 0], b_hh[0:D].rearrange("(a f) -> a f", a=1).to_broadcast([P, D])).then_inc(vec2_loaded, 16)
            sp.dma_start(vec[:, 1], b_hh[D:2 * D].rearrange("(a f) -> a f", a=1).to_broadcast([P, D])).then_inc(vec2_loaded, 16)
            sp.dma_start(w1e_sb, w1e_dram).then_inc(w1e_loaded, 16)
            for k, name in enumerate(wt_names[2:8]):
                sp.dma_start(gru_w[:, k].rearrange("p k f -> p (k f)"), wt_dram[name]).then_inc(gru_loaded, 16)
            for t in range(NT):
                sp.wait_ge(dve_read, V[("p2", t)] + 1)
                sp.dma_start(p_rows[t * P:(t + 1) * P, :], tiles[:, 2 + t % 2]).then_inc(p_stored[t % 2], 16)
            for k in range(COL):
                sp.wait_ge(e_scattered[k], 16 * turns)
            edge_t = dst_rows.rearrange("(p c) w -> p c w", p=P)

            def rows_turn(i):
                for q in range(2):
                    at_least(sp, summed, GROUP * i + 4 * q - 4)
                    sp.dma_start(erow[:, 4 * q:4 * q + 4], edge_t[:, bass.ds(GROUP * i + 4 * q, 4), :]).then_inc(erow_landed[q], 16)

            rows_turn(0)
            with sp.Fori(1, DST_CHUNKS // GROUP) as i:
                rows_turn(i)
            sp.wait_ge(vec_folded, 1)
            sp.dma_start(vec[:, 0], mean2.rearrange("(a f) -> a f", a=1).to_broadcast([P, D])).then_inc(vec2_loaded, 16)
            sp.dma_start(vec[:, 1], var2.rearrange("(a f) -> a f", a=1).to_broadcast([P, D])).then_inc(vec2_loaded, 16)
            sp.dma_start(vec[:, 2], b_3.rearrange("(a f) -> a f", a=1).to_broadcast([P, D])).then_inc(vec_loaded, 16)
            sp.dma_start(ws[:, 1].rearrange("p k f -> p (k f)"), wt_dram["w3"]).then_inc(w_loaded, 16)
            for t in range(NT):
                n = P if t + 1 < NT else LAST
                sp.wait_ge(x_done, t + 1)
                sp.dma_start(out[t * P:t * P + n, :], xs[0:n, t]).then_inc(stored, 16)
            sp.wait_ge(stored, 16 * NT)

        @block.gpsimd
        def _(pool):
            def passed():
                pool.sem_inc(pool_passed, 1)

            nc.gpsimd.memset(srci, 0)
            nc.gpsimd.memset(dsti, NT * P)
            nc.gpsimd.memset(wt_t, 0.0)
            nc.gpsimd.memset(w1t_t, 0.0).then_inc(const_ready, 1)
            nc.gpsimd.memset(h[:], 0.0).then_inc(zero_ready, 1)
            nc.gpsimd.memset(ident[:], 1.0).then_inc(const_ready, 1)
            nc.gpsimd.memset(tri, 1.0).then_inc(const_ready, 1)
            pool.wait_ge(const_ready, 3)
            nc.gpsimd.affine_select(out=ident[:], in_=ident[:], compare_op=ALU.is_equal, fill=0.0, base=0,
                                    pattern=[[1, P]], channel_multiplier=-1).then_inc(const_ready, 1)
            nc.gpsimd.affine_select(out=tri, in_=tri, compare_op=ALU.is_gt, fill=0.0, base=0,
                                    pattern=[[1, P]], channel_multiplier=-1).then_inc(const_ready, 1)
            nc.gpsimd.iota(iota1[:], [[1, P]], base=1, channel_multiplier=0,
                           allow_small_or_imprecise_dtypes=True).then_inc(const_ready, 1)
            nc.gpsimd.iota(iob_f, [[1, 104]], base=0, channel_multiplier=0,
                           allow_small_or_imprecise_dtypes=True).then_inc(const_ready, 1)
            nc.gpsimd.iota(pidx, [[P, 2]], base=0, channel_multiplier=1,
                           allow_small_or_imprecise_dtypes=True).then_inc(const_ready, 1)
            nc.gpsimd.memset(onesq, 1.0).then_inc(const_ready, 1)
            nc.gpsimd.memset(ones[:], 1.0).then_inc(const_ready, 1)
            pool.wait_ge(zeroed, 16 * 7)
            pool.wait_ge(order_ready[0], 1)

            def cell_turn(i):
                for k in range(4):
                    at_least(pool, c_scattered[k], 16 * i)
                passed()
                nc.gpsimd.tensor_copy(cring[:], pay1[:, bass.ds(4 * i, 4), :]).then_inc(c_ready, 1)
                nc.gpsimd.tensor_copy(gidx[:, 0:4], idx1[:, bass.ds(4 * i, 4)]).then_inc(c_ready, 1)
                pool.wait_ge(c_ready, 2 * i + 2)
                passed()
                for k in range(4):
                    nc.gpsimd.indirect_dma_start(cell_rows[:, :], bass.IndirectOffsetOnAxis(gidx[:, k:k + 1], 0),
                                                 cring[:, k, :], None).then_inc(c_scattered[k], 16)

            cell_turn(0)
            with pool.Fori(1, J // 4) as i:
                cell_turn(i)

            pool.wait_ge(cells_loaded, 16)
            pool.wait_ge(order_ready[1], 1)
            turns = J // COL

            nc.gpsimd.memset(ering[:, :, DE + 2:EW], 0.0).then_inc(e_ready, 1)

            def edge_turn(i, last):
                for q in range(2):
                    c = slice(4 * q, 4 * q + 4)
                    for k in range(4 * q, 4 * q + 4):
                        at_least(pool, e_scattered[k], 16 * i)
                    passed()
                    nc.gpsimd.tensor_copy(ering[:, c, DE:DE + 2], pay2[:, bass.ds(COL * i + 4 * q, 4), :]).then_inc(e_ready, 1)
                    nc.gpsimd.tensor_copy(gidx[:, c], idx2[:, bass.ds(COL * i + 4 * q, 4)]).then_inc(e_ready, 1)
                    pool.wait_ge(e_ready, 4 * i + 2 * q + 3)
                    passed()
                    pool.wait_ge(e_loaded[q], 16 * i + (32 if last and q else 16))
                    passed()
                    for k in range(4 * q, 4 * q + 4):
                        nc.gpsimd.indirect_dma_start(dst_rows[:, :], bass.IndirectOffsetOnAxis(gidx[:, k:k + 1], 0),
                                                     ering[:, k, :], None).then_inc(e_scattered[k], 16)

            edge_turn(0, False)
            with pool.Fori(1, turns - 1) as i:
                edge_turn(i, False)
            edge_turn(turns - 1, True)
            pool.wait_ge(h_ready, 3 * NT)
            nc.gpsimd.memset(g[:], 0.0).then_inc(sums_clear, 1)
            for k in range(2):
                pool.wait_ge(p_stored[k], 16 * (NT // 2))

            def gather_turn(i):
                for q in range(2):
                    at_least(pool, summed, GROUP * i + 4 * q - 4)
                    pool.wait_ge(erow_landed[q], 16 * i + 16)
                    passed()
                    nc.gpsimd.tensor_copy(gidx[:, 4 * q:4 * q + 4], erow_i[:, 4 * q:4 * q + 4, DE]).then_inc(g_ready, 1)
                    pool.wait_ge(g_ready, 2 * i + q + 1)
                    passed()
                    for k in range(4 * q, 4 * q + 4):
                        nc.gpsimd.indirect_dma_start(rows[:, k, :], None, p_rows[:, :],
                                                     bass.IndirectOffsetOnAxis(gidx[:, k:k + 1], 0)).then_inc(g_landed[k], 16)

            gather_turn(0)
            with pool.Fori(1, DST_CHUNKS // GROUP) as i:
                gather_turn(i)

        @block.scalar
        def _(act):
            def copy_job(job, dst, src=None):
                act.wait_ge(for_act, A[job] + 1)
                b = act_bank(job)
                nc.scalar.copy(dst, b[:, 0:src] if src else b[:]).then_inc(act_read, 1)

            for n in range(len(blocks)):
                if n >= 2:
                    m = n - 2
                    act.wait_ge(wt_stored[m % 2], 16 * (m // 2 + 1) + (16 if m % 2 == 0 else 0))
                for k in range(KT):
                    copy_job(("w", n, k), ws[:, n % 2, k])
                if n == 0:
                    copy_job(("w", 0, 4), tiles[:, 0])

            def flat(t4):
                return t4.rearrange("p k n -> p (k n)")

            def one_hot_sources(b):
                s = builds[b]
                hot = ohs3 if b else ohs

                def turn(i):
                    for q in range(2):
                        at_least(act, s["mm"], GROUP * i + 4 * q - 4)
                        for k in range(4 * q, 4 * q + 4):
                            ins = nc.scalar.activation(hot[:, k], iota1[:], ACT.Abs,
                                                       bias=cellm[:, bass.ds(GROUP * i + k, 1), 0:1].rearrange("p a w -> p (a w)"))
                        ins.then_inc(s["dist"], 1)
                        act.wait_ge(s["dist"], 2 * i + q + 1)
                        four = hot[:, 4 * q:4 * q + 4].rearrange("p c s -> p (c s)")
                        nc.scalar.activation(four, four, ACT.Relu, bias=1.0, scale=-1.0).then_inc(s["src"], 1)

                turn(0)
                with act.Fori(1, CELL_CHUNKS // GROUP) as i:
                    turn(i)

            def root(job, ap):
                act.wait_ge(square_ready, ROOT[job] + 1)
                nc.scalar.activation(ap, ap, ACT.Sqrt).then_inc(root_ready, 1)

            root("h0", rstd[:])
            act.wait_ge(for_act, wj[len(blocks) - 1])
            act.wait_ge(cells_loaded, 16)
            one_hot_sources(0)
            root("dinv", dinv[:])
            act.wait_ge(wt_stored[0], 32)
            for t in range(NT):
                if t >= 2:
                    act.wait_ge(for_dve, V[("y0", t - 2)] + 1)
                copy_job(("h0T", t), flat(hT[:, t % 2]))
                copy_job(("agg0T", t), flat(aggT0[:, t % 2]))
                root(("y0", t), rstd[:, 0:1])
            root("h1", rstd[:])
            for t in range(NT):
                if t >= 2:
                    act.wait_ge(for_dve, V[("g1", t - 2)] + 1)
                else:
                    act.wait_ge(for_dve, V[("y0", NT - 2 + t)] + 1)
                copy_job(("h1T", t), flat(hT[:, t % 2]))
            for t in range(NT):
                if t >= 2:
                    act.wait_ge(for_dve, V[("y1", t - 2)] + 1)
                copy_job(("a1T", t), flat(a1T[:, t % 2]), DH)
                root(("n1", t), rstd[:, 0:1])
                root(("h2", t), rstd[:, 0:1])
            for t in range(NT):
                act.wait_ge(for_dve, V[("p2", t - 2)] + 1 if t >= 2 else 1)
                if t < 2:
                    act.wait_ge(h_ready, 3 * NT)
                copy_job(("h2T", t), flat(hT[:, t % 2]))
            def turned_copy(c, k):
                act.wait_ge(turned, c + 1)
                at_least(act, edge_mm, c - 3)
                nc.scalar.copy(erowT[:, k % 4], pb[k % 2][:, 0:P]).then_inc(turned_read, 1)

            def relu(c, k):
                act.wait_ge(msg_added, c + 1)
                nc.scalar.activation(rows[:, k % GROUP], rows[:, k % GROUP], ACT.Relu).then_inc(msg_ready, 1)

            turned_copy(0, 0)
            turned_copy(1, 1)
            relu(0, 0)

            def turn(i, last):
                for k in range(GROUP):
                    c = GROUP * i + k
                    if not last or k < GROUP - 2:
                        turned_copy(c + 2, k + 2)
                    if not last or k < GROUP - 1:
                        relu(c + 1, k + 1)

            turn(0, False)
            with act.Fori(1, DST_CHUNKS // GROUP - 1) as i:
                turn(i, False)
            turn(DST_CHUNKS // GROUP - 1, True)
            root("bn", vec[:, 1])
            copy_job(("r2T", 0), flat(hT[:, 0]))
            copy_job(("hgT", 0), flat(hT[:, 1]))
            for t in range(NT):
                copy_job(("agg2T", t), tiles[:, 3])
                for k, gate in enumerate(("r", "z")):
                    act.wait_ge(dve_read, V[(gate, t)] + 1)
                    nc.scalar.activation(gates[:, k], gates[:, k], ACT.Sigmoid).then_inc(gate_out, 1)
                if t + 1 < NT:
                    act.wait_ge(for_dve, V[("hn", t)] + 1)
                    copy_job(("r2T", t + 1), flat(hT[:, 0]))
                    copy_job(("hgT", t + 1), flat(hT[:, 1]))
                act.wait_ge(gate_in, t + 1)
                nc.scalar.activation(gates[:, 2], gates[:, 2], ACT.Tanh).then_inc(gate_out, 1)
            root("h3", rstd[:])
            one_hot_sources(1)
            for t in range(NT):
                if t >= 2:
                    act.wait_ge(for_dve, V[("y3", t - 2)] + 1)
                copy_job(("agg3T", t), flat(hT[:, t % 2]))

        @block.tensor
        def _(pe):
            def to_act(job):
                at_least(pe, act_read, A[job] - 3)
                return act_bank(job)

            def to_dve(job):
                at_least(pe, dve_read, V[job] - 3)
                return dve_bank(job)

            def turn_tile(job, tile):
                b = to_act(job)
                k = tile.shape[-1] // P
                for q in range(k):
                    ins = nc.tensor.transpose(b[:, q * P:(q + 1) * P], tile[:, q * P:(q + 1) * P], ident[:])
                ins.then_inc(for_act, 1)

            def sort_products(job, cols):
                b = to_dve(job)
                nc.tensor.matmul(b[:, 0:cols], tri, ptot[:, 0:cols], start=True, stop=True)
                nc.tensor.matmul(b[:, 128:128 + cols], onesq, ptot[:, 0:cols], start=True, stop=True).then_inc(for_dve, 1)

            def turn_weights(n):
                pe.wait_ge(raw_loaded[n % 2], 16 * (n // 2 + 1))
                for k in range(5 if n == 0 else KT):
                    b = to_act(("w", n, k))
                    f = (k * P) % 640
                    for o in range(KT):
                        ins = nc.tensor.transpose(b[:, o * P:(o + 1) * P], wst[:, n % 2, o, f:f + P], ident[:])
                    ins.then_inc(for_act, 1)

            pe.wait_ge(const_ready, 10)
            for n in range(3):
                turn_weights(n)
            pe.wait_ge(totals_ready, 1)
            sort_products("prefix1", B1)
            pe.wait_ge(totals_ready, 2)
            sort_products("prefix2", B2)
            for n in range(3, len(blocks)):
                turn_weights(n)
            pe.wait_ge(order_ready[1], 1)
            b = to_dve("tables")
            nc.tensor.matmul(b[0:1, 0:P], tabf[:, 0:1], ident[:], start=True, stop=True)
            nc.tensor.matmul(b[0:1, P:2 * P], tabf[:, 1:2], ident[:], start=True, stop=True)
            nc.tensor.matmul(b[0:1, 2 * P:3 * P], tabf[:, 2:3], ident[:], start=True, stop=True).then_inc(for_dve, 1)

            def build_blocks(b):
                s = builds[b]
                wide = 2 * P if b == 0 else P

                def turn(i):
                    for k in range(GROUP):
                        pair = k // 2
                        if k % 2 == 0:
                            at_least(pe, s["add"], GROUP // 2 * i + pair - 3)
                        if k % 4 == 0:
                            pe.wait_ge(s["src"], 2 * i + k // 4 + 1)
                        pe.wait_ge(s["dst"], GROUP * i + k + 1)
                        rhs = ohd[:, k % 4].rearrange("p m d -> p (m d)") if b == 0 else ohd3[:, k % 4]
                        nc.tensor.matmul(pb[pair][:, 0:wide], (ohs3 if b else ohs)[:, k], rhs,
                                         start=k % 2 == 0, stop=k % 2 == 1).then_inc(s["mm"], 1)

                turn(0)
                with pe.Fori(1, CELL_CHUNKS // GROUP) as i:
                    turn(i)

            pe.wait_ge(act_read, wj[len(blocks) - 1])
            build_blocks(0)
            pe.wait_ge(builds[0]["add"], CELL_PAIRS)
            b = to_dve("deg")
            for m in range(2):
                for t in range(NT):
                    for s in range(NT):
                        ins = nc.tensor.matmul(b[:, m * NT + t:m * NT + t + 1], adj3[:, m, t * NT + s], ones[:],
                                               start=s == 0, stop=s == NT - 1)
            ins.then_inc(for_dve, 1)

            def sum_neighbours(job, m, rows_of, wide):
                b = to_dve(job)
                t = job[1]
                for s in range(NT):
                    ins = nc.tensor.matmul(b[:, 0:wide], adj3[:, m, t * NT + s], rows_of[:, s, 0:wide],
                                           start=s == 0, stop=s == NT - 1)
                ins.then_inc(for_dve, 1)

            def linear(job, parts, wide):
                b = to_dve(job)
                n = sum(x.shape[1] for x, _ in parts)
                m = 0
                for x, w in parts:
                    for k in range(x.shape[1]):
                        ins = nc.tensor.matmul(b[:, 0:wide], x[:, k], w[:, k], start=m == 0, stop=m == n - 1)
                        m += 1
                ins.then_inc(for_dve, 1)

            pe.wait_ge(h_ready, NT)
            sum_neighbours(("agg0", 0), 0, h, D)
            for t in range(NT):
                turn_tile(("h0T", t), h[:, t])
                if t + 1 < NT:
                    sum_neighbours(("agg0", t + 1), 0, h, D)
                pe.wait_ge(dve_read, V[("agg0", t)] + 1)
                turn_tile(("agg0T", t), agg0[:, t % 2])
                pe.wait_ge(act_read, A[("agg0T", t)] + 1)
                linear(("y0", t), [(hT[:, t % 2], ws[:, 1]), (aggT0[:, t % 2], ws[:, 0])], D)
            pe.wait_ge(w_loaded, 48)
            for t in range(NT):
                pe.wait_ge(h_ready, NT + t + 1)
                turn_tile(("h1T", t), h[:, t])
                if t:
                    pe.wait_ge(act_read, A[("h1T", t - 1)] + 1)
                    linear(("g1", t - 1), [(hT[:, (t - 1) % 2], w1_sb)], DH)
            pe.wait_ge(act_read, A[("h1T", NT - 1)] + 1)
            linear(("g1", NT - 1), [(hT[:, (NT - 1) % 2], w1_sb)], DH)
            pe.wait_ge(dve_read, V[("g1", NT - 1)] + 1)
            for t in range(NT):
                sum_neighbours(("x1", t), 1, g1, DH)
            pe.wait_ge(x1_ready, NT)
            sum_neighbours(("a1", 0), 1, x1, DH)
            for t in range(NT):
                if t + 1 < NT:
                    sum_neighbours(("a1", t + 1), 1, x1, DH)
                pe.wait_ge(dve_read, V[("a1", t)] + 1)
                turn_tile(("a1T", t), a1[:, t % 2])
                pe.wait_ge(act_read, A[("a1T", t)] + 1)
                linear(("y1", t), [(a1T[:, t % 2], w2_sb)], D)
            for t in range(NT):
                pe.wait_ge(h_ready, 2 * NT + t + 1)
                turn_tile(("h2T", t), h[:, t])
                if t:
                    pe.wait_ge(act_read, A[("h2T", t - 1)] + 1)
                    linear(("p2", t - 1), [(hT[:, (t - 1) % 2], ws[:, 1])], D)
            pe.wait_ge(act_read, A[("h2T", NT - 1)] + 1)
            linear(("p2", NT - 1), [(hT[:, (NT - 1) % 2], ws[:, 1])], D)
            pe.wait_ge(w1e_loaded, 16)
            pe.wait_ge(dve_read, V[("p2", NT - 1)] + 1)

            def t_edges(i, k):
                c = GROUP * i + k
                pe.wait_ge(erow_landed[k // 4], 16 * i + 16)
                at_least(pe, turned_read, c - 1)
                nc.tensor.transpose(pb[k % 2][:, 0:P], erow[:, k, 0:DE], ident[:]).then_inc(turned, 1)

            def m_edges(i, k):
                c = GROUP * i + k
                pe.wait_ge(turned_read, c + 1)
                at_least(pe, msg_added, c - 1)
                nc.tensor.matmul(pb[2 + k % 2][:], erowT[:, k % 4], w1e_sb, start=True, stop=True).then_inc(edge_mm, 1)

            def s_edges(i, k):
                c = GROUP * i + k
                pe.wait_ge(msg_ready, c + 1)
                pe.wait_ge(hot_ready, c + 1)
                if k % 2 == 0:
                    at_least(pe, sums_added, GROUP // 2 * i + k // 2 - 1)
                nc.tensor.matmul(pb[4 + (k // 2) % 2][:], ohe[:, k], rows[:, k], start=k % 2 == 0,
                                 stop=k % 2 == 1).then_inc(summed, 1)

            t_edges(0, 0)
            t_edges(0, 1)
            m_edges(0, 0)

            def turn(i, first, last):
                for k in range(GROUP):
                    if not last or k < GROUP - 2:
                        t_edges(i + (k + 2) // GROUP, (k + 2) % GROUP)
                    if not last or k < GROUP - 1:
                        m_edges(i + (k + 1) // GROUP, (k + 1) % GROUP)
                    if not (first and k == 0):
                        s_edges(i if k else i - 1, (k - 1) % GROUP)

            turns = DST_CHUNKS // GROUP
            turn(0, True, False)
            with pe.Fori(1, turns - 1) as i:
                turn(i, False, False)
            turn(turns - 1, False, True)
            s_edges(turns - 1, GROUP - 1)
            pe.wait_ge(gru_loaded, 16 * 6)
            pe.wait_ge(w_loaded, 64)
            pe.wait_ge(sums_added, DST_PAIRS)
            turn_tile(("r2T", 0), r2[:, 0])
            turn_tile(("hgT", 0), h[:, 0])
            for t in range(NT):
                pe.wait_ge(act_read, A[("r2T", t)] + 1)
                linear(("agg2", t), [(hT[:, 0], ws[:, 0])], D)
                pe.wait_ge(dve_read, V[("agg2", t)] + 1)
                turn_tile(("agg2T", t), tiles[:, 2])
                pe.wait_ge(act_read, A[("agg2T", t)] + 1)
                at = tiles[:, 3].rearrange("p (k n) -> p k n", k=KT)
                linear(("r", t), [(hT[:, 1], gru_w[:, 3]), (at, gru_w[:, 0])], D)
                linear(("z", t), [(hT[:, 1], gru_w[:, 4]), (at, gru_w[:, 1])], D)
                linear(("hn", t), [(hT[:, 1], gru_w[:, 5])], D)
                if t + 1 < NT:
                    turn_tile(("r2T", t + 1), r2[:, t + 1])
                    turn_tile(("hgT", t + 1), h[:, t + 1])
                linear(("in", t), [(at, gru_w[:, 2])], D)
            build_blocks(1)
            pe.wait_ge(builds[1]["add"], CELL_PAIRS)
            pe.wait_ge(w_loaded, 80)
            sum_neighbours(("agg3", 0), 0, h, D)
            for t in range(NT):
                if t + 1 < NT:
                    sum_neighbours(("agg3", t + 1), 0, h, D)
                pe.wait_ge(dve_read, V[("agg3", t)] + 1)
                turn_tile(("agg3T", t), tiles[:, 2 + t % 2])
                pe.wait_ge(act_read, A[("agg3T", t)] + 1)
                linear(("y3", t), [(hT[:, t % 2], ws[:, 1])], D)

        @block.vector
        def _(dve):
            chain = [0]

            def link(ins):
                chain[0] += 1
                ins.then_inc(step, 1)
                dve.wait_ge(step, chain[0])

            vts, vtt, vstt = nc.vector.tensor_scalar, nc.vector.tensor_tensor, nc.vector.scalar_tensor_tensor

            dve.wait_ge(const_ready, 10)
            dve.wait_ge(edges_loaded, 16 * 8)
            link(nc.vector.tensor_copy(iob, iob_f))
            link(vts(t_i, srci, 7, None, ALU.arith_shift_right))
            link(nc.vector.tensor_copy(st_f, t_i))
            link(vts(t_j, dsti, 7, None, ALU.arith_shift_right))
            link(nc.vector.tensor_copy(dt_f, t_j))
            link(nc.vector.tensor_copy(dt_b, dt_f))
            link(vstt(cell_f, dt_f, float(NT), st_f, ALU.mult, ALU.add))
            link(nc.vector.tensor_copy(cell_b, cell_f))
            link(vts(t_i, srci, P - 1, None, ALU.bitwise_and))
            link(nc.vector.tensor_copy(st_f, t_i))
            link(vts(pay1[:, :, 0], st_f, 1.0, -1.0, ALU.add, ALU.mult))
            link(vts(t_j, dsti, P - 1, None, ALU.bitwise_and))
            link(nc.vector.tensor_copy(dt_f, t_j))
            link(vts(pay1[:, :, 1], dt_f, 1.0, None, ALU.add))
            nc.vector.tensor_copy(pay1[:, :, 2], wt_t)
            nc.vector.tensor_copy(pay1[:, :, 3], w1t_t)
            nc.vector.tensor_copy(pay2[:].bitcast(I32)[:, :, 0], srci)
            link(vts(pay2[:, :, 1], dt_f, 1.0, None, ALU.add))

            def places(buckets, bucket_of, chunks, job, idx, tab_cols):
                ohb, csb = oh[:, 0:buckets], cs[:, 0:buckets]
                link(vtt(ohb, iob[:, 0:buckets].unsqueeze(2).to_broadcast([P, buckets, J]),
                         bucket_of.unsqueeze(1).to_broadcast([P, buckets, J]), ALU.is_equal))
                flat_oh = ohb.rearrange("p b j -> p (b j)")
                flat_cs = csb.rearrange("p b j -> p (b j)")
                link(nc.vector.tensor_tensor_scan(flat_cs, flat_oh, flat_oh, 0.0, ALU.add, ALU.max))
                link(nc.vector.tensor_copy(pcum[:, 0:buckets], csb[:, :, J - 1]))
                nc.vector.tensor_copy(ptot[:, 0:1], pcum[:, 0:1])
                vtt(ptot[:, 1:buckets], pcum[:, 1:buckets], pcum[:, 0:buckets - 1],
                    ALU.subtract).then_inc(totals_ready, 1)
                b = dve_bank(job)
                dve.wait_ge(for_dve, V[job] + 1)
                link(vts(cnts[:, 0:buckets], b[:, 128:128 + buckets], float(PAIR - 1), None, ALU.add))
                link(nc.vector.tensor_copy(cnti[:, 0:buckets], cnts[:, 0:buckets]))
                link(vts(cnti[:, 0:buckets], cnti[:, 0:buckets], 8, None, ALU.arith_shift_right))
                link(nc.vector.tensor_copy(nsup[:, 0:buckets], cnti[:, 0:buckets]))
                link(nc.vector.tensor_tensor_scan(endp[:, 0:buckets], nsup[:, 0:buckets], nsup[:, 0:buckets], 0.0,
                                                  ALU.add, ALU.max))
                link(vtt(offs[:, 0:buckets], endp[:, 0:buckets], nsup[:, 0:buckets], ALU.subtract))
                link(vts(offs[:, 0:buckets], offs[:, 0:buckets], float(PAIR), None, ALU.mult))
                link(nc.vector.memset(offs[:, buckets - 1:buckets], float(chunks * P)))
                link(vtt(offs[:, 0:buckets], offs[:, 0:buckets], b[:, 0:buckets], ALU.add))
                link(vtt(offs[:, 0:buckets], offs[:, 0:buckets], pcum[:, 0:buckets], ALU.subtract))
                link(vtt(offs[:, 0:buckets], offs[:, 0:buckets], ptot[:, 0:buckets], ALU.add))
                ins = vts(offs[:, 0:buckets], offs[:, 0:buckets], -1.0, None, ALU.add)
                ins.then_inc(dve_read, 1)
                dve.wait_ge(dve_read, V[job] + 1)
                lo = 0
                out_sum = sum_a
                while lo < buckets:
                    hi = min(lo + half, buckets)
                    for q in range(lo, hi):
                        ins = vstt(sel[:, q - lo], csb[:, q], offs[:, q:q + 1], ohb[:, q], ALU.add, ALU.mult)
                    link(ins)
                    link(nc.vector.tensor_reduce(out_sum, sel[:, 0:hi - lo].rearrange("p b j -> p j b"), AX_X, ALU.add))
                    if out_sum is sum_b:
                        link(vtt(sum_a, sum_a, sum_b, ALU.add))
                    out_sum = sum_b
                    lo = hi
                link(nc.vector.tensor_copy(t_i, sum_a))
                link(vts(t_j, t_i, 7, None, ALU.arith_shift_right))
                link(vts(t_i, t_i, P - 1, None, ALU.bitwise_and))
                link(nc.vector.tensor_copy(sum_a, t_i))
                link(nc.vector.tensor_copy(sum_b, t_j))
                link(vstt(sum_a, sum_a, float(chunks + SPARE), sum_b, ALU.mult, ALU.add))
                link(nc.vector.tensor_copy(idx[:], sum_a))
                for n, col in enumerate(tab_cols):
                    link(vts(cmp_t[:, 0:buckets - 1], endp[:, 0:buckets - 1], pidx[:, n:n + 1], None, ALU.is_le))
                    link(nc.vector.tensor_reduce(tabf[:, col:col + 1], cmp_t[:, 0:buckets - 1], AX_X, ALU.add))

            places(B1, cell_b, CELL_CHUNKS, "prefix1", idx1, [0, 1])
            vts(tabf[:, 0:2], tabf[:, 0:2], float(CELLS - 1), float(P), ALU.min, ALU.mult).then_inc(order_ready[0], 1)
            places(B2, dt_b, DST_CHUNKS, "prefix2", idx2, [2])
            vts(tabf[:, 2:3], tabf[:, 2:3], float(NT - 1), float(D), ALU.min, ALU.mult).then_inc(order_ready[1], 1)
            nc.vector.memset(xs[:, NT - 1], 0.0).then_inc(x_free, 1)
            b = dve_bank("tables")
            dve.wait_ge(for_dve, V["tables"] + 1)
            nc.vector.tensor_copy(cell_at, b[0:1, 0:CELL_PAIRS])
            link(nc.vector.tensor_copy(dst_at, b[0:1, 2 * P:2 * P + DST_PAIRS]))
            nc.vector.memset(adj[:], 0.0).then_inc(dve_read, 1)
            dve.wait_ge(dve_read, V["tables"] + 1)

            def inverse_root(job, ap, square):
                square.then_inc(square_ready, 1)
                dve.wait_ge(root_ready, ROOT[job] + 1)
                link(nc.vector.reciprocal(ap, ap))

            def layernorm(job, dst, src):
                link(nc.vector.bn_stats(stats[:], src))
                link(nc.vector.bn_aggr(mv[:, 0], stats[:]))
                inverse_root(job, rstd[:, 0:1], vts(rstd[:, 0:1], mv[:, 0, 1:2], LN_EPS, None, ALU.add))
                link(vts(dst, src, mv[:, 0, 0:1], rstd[:, 0:1], ALU.subtract, ALU.mult))

            def moments(t):
                link(nc.vector.bn_stats(stats[:], xs[:, t]))
                link(nc.vector.bn_aggr(mv[:, t], stats[:]))

            def relu_norm_all(job):
                inverse_root(job, rstd[:], vts(rstd[:], mv[:, :, 1], LN_EPS, None, ALU.add))
                for t in range(NT):
                    link(vts(h[:, t], xs[:, t], mv[:, t, 0:1], rstd[:, t:t + 1], ALU.subtract, ALU.mult))
                    vts(h[:, t], h[:, t], 0.0, None, ALU.max).then_inc(h_ready, 1)

            def read(job, emit):
                dve.wait_ge(for_dve, V[job] + 1)
                emit(dve_bank(job)).then_inc(dve_read, 1)
                dve.wait_ge(dve_read, V[job] + 1)

            dve.wait_ge(loaded, 16 * NT)
            dve.wait_ge(zeroed, 16 * 7)
            for t in range(NT):
                moments(t)
            relu_norm_all("h0")

            def build(b):
                s = builds[b]

                def hots(i, q):
                    for k in (2 * q, 2 * q + 1):
                        c = GROUP * i + k
                        at_least(dve, s["mm"], c - 3)
                        local = cellm[:, bass.ds(c, 1), 1:2].rearrange("p a w -> p (a w)")
                        if b == 0:
                            vts(ohd[:, k % 4, 0], iota1[:], local, None, ALU.is_equal)
                        weight = cellm[:, bass.ds(c, 1), 2 + b:3 + b].rearrange("p a w -> p (a w)")
                        vts(ohd3[:, k % 4] if b else ohd[:, k % 4, 1], iota1[:], local, weight, ALU.is_equal,
                            ALU.mult).then_inc(s["dst"], 1)

                def add(i, q):
                    n = GROUP // 2 * i + q
                    at = dve.value_load(cell_at[0:1, bass.ds(n, 1)], min_val=0, max_val=(CELLS - 1) * P)
                    dve.wait_ge(s["mm"], 2 * n + 2)
                    at_least(dve, s["add"], n)
                    if b == 0:
                        cell = adj_flat[:, :, bass.ds(at, P)]
                        vtt(cell, pb[q][:, 0:2 * P].rearrange("p (m d) -> p m d", m=2), cell, ALU.add).then_inc(s["add"], 1)
                    else:
                        cell = adj[:, bass.ds(at, P)]
                        vtt(cell, pb[q][:, 0:P], cell, ALU.add).then_inc(s["add"], 1)

                def turn(i, last):
                    for q in range(4):
                        if not last or q < 3:
                            hots(i + (q + 1) // 4, (q + 1) % 4)
                        add(i, q)

                turns = CELL_CHUNKS // GROUP
                hots(0, 0)
                turn(0, False)
                with dve.Fori(1, turns - 1) as i:
                    turn(i, False)
                turn(turns - 1, True)
                dve.wait_ge(s["add"], CELL_PAIRS)

            dve.wait_ge(cells_loaded, 16)
            dve.wait_ge(for_act, wj[len(blocks) - 1])
            build(0)
            read("deg", lambda b: nc.vector.tensor_copy(deg[:], b[:, 0:2 * NT]))
            link(vts(invc[:], deg[:, 0:NT], 1.0, None, ALU.max))
            link(nc.vector.reciprocal(invc[:], invc[:]))
            link(vts(dmask[:], deg[:, NT:2 * NT], 1.0, None, ALU.add))
            inverse_root("dinv", dinv[:], vts(dinv[:], dmask[:], 2.0 ** -116, None, ALU.max))
            link(vts(dmask[:], dmask[:], 0.0, None, ALU.is_gt))
            link(vtt(dinv[:], dinv[:], dmask[:], ALU.mult))
            dve.wait_ge(vec_loaded, 48)

            def mean0(t):
                if t >= 2:
                    dve.wait_ge(for_act, A[("agg0T", t - 2)] + 1)
                read(("agg0", t), lambda b: vts(agg0[:, t % 2], b[:], invc[:, t:t + 1], None, ALU.mult))

            mean0(0)
            for t in range(NT):
                if t + 1 < NT:
                    mean0(t + 1)
                y = y0[:, t % 2]
                read(("y0", t), lambda b: vtt(y, b[:], vec[:, 0], ALU.add))
                layernorm(("y0", t), y, y)
                link(vtt(y, y, vec[:, 1], ALU.mult))
                link(vtt(y, y, vec[:, 2], ALU.add))
                link(vtt(xs[:, t], xs[:, t], y, ALU.add))
            for t in range(NT):
                moments(t)
            relu_norm_all("h1")
            for t in range(NT):
                read(("g1", t), lambda b: vts(g1[:, t], b[:, 0:DH], dinv[:, t:t + 1], None, ALU.mult))
            dve.wait_ge(vec_loaded, 80)
            for t in range(NT):
                x = x1[:, t]
                read(("x1", t), lambda b: vtt(x, b[:, 0:DH], g1[:, t], ALU.add))
                link(vstt(x, x, dinv[:, t:t + 1], vec[:, 0, 0:DH], ALU.mult, ALU.add))
                vts(x, x, 0.0, dinv[:, t:t + 1], ALU.max, ALU.mult).then_inc(x1_ready, 1)
            dve.wait_ge(x1_ready, NT)

            def sum1(t):
                if t >= 2:
                    dve.wait_ge(for_act, A[("a1T", t - 2)] + 1)
                read(("a1", t), lambda b: vtt(a1[:, t % 2], b[:, 0:DH], x1[:, t], ALU.add))

            sum1(0)
            for t in range(NT):
                if t + 1 < NT:
                    sum1(t + 1)
                y = y1[:, t % 2]
                read(("y1", t), lambda b: vstt(y, b[:], dinv[:, t:t + 1], vec[:, 1], ALU.mult, ALU.add))
                link(nc.vector.tensor_tensor_reduce(h[:, t], y, y, 1.0, 0.0, ALU.mult, ALU.add, rstd[:, 0:1]))
                inverse_root(("n1", t), rstd[:, 0:1], vts(rstd[:, 0:1], rstd[:, 0:1], 1e-24, None, ALU.max))
                link(vstt(xs[:, t], y, rstd[:, 0:1], xs[:, t], ALU.mult, ALU.add))
                layernorm(("h2", t), h[:, t], xs[:, t])
                vts(h[:, t], h[:, t], 0.0, None, ALU.max).then_inc(h_ready, 1)
            dve.wait_ge(vec2_loaded, 16 * 10)
            link(vtt(bx_v, bx_v, vec[:, 0], ALU.add))
            vtt(by_v, by_v, vec[:, 1], ALU.add).then_inc(vec_folded, 1)
            for t in range(NT):
                if t >= 2:
                    dve.wait_ge(p_stored[t % 2], 16 * (t // 2))
                read(("p2", t), lambda b: vtt(tiles[:, 2 + t % 2], b[:], b1_v, ALU.add))
            dve.wait_ge(sums_clear, 1)

            def hot(i, k):
                at_least(dve, summed, GROUP * i + k - GROUP + 1)
                dve.wait_ge(erow_landed[k // 4], 16 * i + 16)
                vts(ohe[:, k], iota1[:], erow[:, k, DE + 1:DE + 2], None, ALU.is_equal).then_inc(hot_ready, 1)

            def message(i, k):
                dve.wait_ge(edge_mm, GROUP * i + k + 1)
                dve.wait_ge(g_landed[k], 16 * i + 16)
                vtt(rows[:, k], pb[2 + k % 2][:], rows[:, k], ALU.add).then_inc(msg_added, 1)

            def add_sums(i, q):
                n = GROUP // 2 * i + q
                at = dve.value_load(dst_at[0:1, bass.ds(n, 1)], min_val=0, max_val=(NT - 1) * D)
                dve.wait_ge(summed, 2 * n + 2)
                at_least(dve, sums_added, n)
                tile = g[:, bass.ds(at, D)]
                vtt(tile, pb[4 + q % 2][:], tile, ALU.add).then_inc(sums_added, 1)

            def turn(i, first, last):
                for k in range(GROUP):
                    if not last or k < GROUP - 2:
                        hot(i + (k + 2) // GROUP, (k + 2) % GROUP)
                    if not last or k < GROUP - 1:
                        message(i + (k + 1) // GROUP, (k + 1) % GROUP)
                    if k % 2 == 0 and not (first and k == 0):
                        add_sums(i if k else i - 1, (k // 2 - 1) % 4)

            turns = DST_CHUNKS // GROUP
            hot(0, 0)
            hot(0, 1)
            message(0, 0)
            turn(0, True, False)
            with dve.Fori(1, turns - 1) as i:
                turn(i, False, False)
            turn(turns - 1, False, True)
            add_sums(turns - 1, 3)
            dve.wait_ge(vec2_loaded, 16 * 12)
            inverse_root("bn", vec[:, 1], vts(vec[:, 1], vec[:, 1], BN_EPS, None, ALU.add))
            link(vtt(sc_v, sc_v, vec[:, 1], ALU.mult))
            link(vtt(vec[:, 0], vec[:, 0], sc_v, ALU.mult))
            link(vtt(sh_v, sh_v, vec[:, 0], ALU.subtract))
            dve.wait_ge(sums_added, DST_PAIRS)
            for t in range(NT):
                read(("agg2", t), lambda b: vstt(tiles[:, 2], b2_v, deg[:, t:t + 1], b[:], ALU.mult, ALU.add))
                r, z, n, m = (gates[:, k] for k in range(4))
                read(("r", t), lambda b: vtt(r, b[:], bx_v, ALU.add))
                read(("z", t), lambda b: vtt(z, b[:], by_v, ALU.add))
                read(("hn", t), lambda b: vtt(n, b[:], bw_v, ALU.add))
                dve.wait_ge(gate_out, 3 * t + 1)
                link(vtt(n, n, r, ALU.mult))
                read(("in", t), lambda b: vtt(m, b[:], bz_v, ALU.add))
                vtt(n, n, m, ALU.add).then_inc(gate_in, 1)
                link(vtt(xs[:, t], xs[:, t], h[:, t], ALU.add))
                dve.wait_ge(gate_out, 3 * t + 3)
                link(vtt(m, h[:, t], n, ALU.subtract))
                link(vtt(m, m, z, ALU.mult))
                link(vtt(m, m, n, ALU.add))
                link(vtt(m, m, sc_v, ALU.mult))
                link(vtt(m, m, sh_v, ALU.add))
                link(vtt(xs[:, t], xs[:, t], m, ALU.add))
                moments(t)
            relu_norm_all("h3")
            dve.wait_ge(for_dve, V[("in", NT - 1)] + 1)
            link(nc.vector.memset(adj[:, 0:CELLS * P], 0.0))
            build(1)
            dve.wait_ge(vec_loaded, 96)

            def sum3(t):
                if t >= 2:
                    dve.wait_ge(for_act, A[("agg3T", t - 2)] + 1)
                read(("agg3", t), lambda b: nc.vector.tensor_copy(tiles[:, 2 + t % 2], b[:]))

            sum3(0)
            for t in range(NT):
                if t + 1 < NT:
                    sum3(t + 1)
                read(("y3", t), lambda b: vtt(xs[:, t], b[:], xs[:, t], ALU.add))
                vtt(xs[:, t], xs[:, t], vec[:, 2], ALU.add).then_inc(x_done, 1)


_INS = ["x", "src", "dst", "edge_attr_128", "edge_weight", "edge_weight1", "L0_gnn_W_self", "L0_gnn_W_neigh",
        "L0_gnn_bias", "L0_gnn_gamma", "L0_gnn_beta", "L1_gnn_W1", "L1_gnn_b1", "L1_gnn_W2", "L1_gnn_b2",
        "L2_gnn_W1", "L2_gnn_b1", "L2_gnn_W2", "L2_gnn_b2", "L2_gnn_W_ih", "L2_gnn_W_hh", "L2_gnn_b_ih",
        "L2_gnn_b_hh", "L2_gnn_gamma", "L2_gnn_beta", "L2_gnn_run_mean", "L2_gnn_run_var", "L3_gnn_W", "L3_gnn_b"]


def kernel(**inputs):
    import numpy as _np
    import concourse.bacc as _bacc
    from concourse import mybir as _mybir
    from concourse.bass_utils import run_bass_kernel_spmd as _run

    nc = _bacc.Bacc("TRN2", target_bir_lowering=False, num_devices=1)
    arrays, args = {}, []
    for name in _INS:
        a = _np.ascontiguousarray(inputs[name])
        arrays[f"in_{name}_dram"] = a
        args.append(nc.dram_tensor(f"in_{name}_dram", a.shape, _mybir.dt.from_np(a.dtype), kind="ExternalInput").ap())
    args.append(nc.dram_tensor("out_0_dram", (N, D), _mybir.dt.float32, kind="ExternalOutput").ap())
    build_gnn(nc, *args)
    r = _run(nc, [arrays], core_ids=[0])
    return r.results[0]["out_0_dram"]
```

```python
from contextlib import ExitStack

import numpy as np
import concourse.bass as bass
from concourse import mybir

F32 = mybir.dt.float32
I32 = mybir.dt.int32
F32R = mybir.dt.float32r
BF16 = mybir.dt.bfloat16
ALU = mybir.AluOpType
ACT = mybir.ActivationFunctionType
AX_X = mybir.AxisListType.X

P = 128
N = 1250
E = 21250
D = 512
DH = 256
DE = 128
NT = -(-N // P)
KT = D // P
LAST = N - (NT - 1) * P
JV = E // P
REST = E - JV * P
COL = 8
J = -(-(JV + 1) // COL) * COL
PAIR = 2 * P
CELLS = NT * NT
CELL_PAIRS = (E + CELLS * (PAIR - 1)) // PAIR
CELL_PAIRS = -(-CELL_PAIRS // 4) * 4
CELL_CHUNKS = 2 * CELL_PAIRS
DST_PAIRS = -(-((E + NT * (PAIR - 1)) // PAIR) // 4) * 4
DST_CHUNKS = 2 * DST_PAIRS
AW = CELLS * P
SPARE = 2
EW = DE + 4
LN_EPS = 1e-5
BN_EPS = 1e-5
GROUP = 8


def at_least(eng, semaphore, value):
    if not isinstance(value, int) or value > 0:
        eng.wait_ge(semaphore, value)


def numbered(names):
    return {name: n for n, name in enumerate(names)}


def build_gnn(nc, x_in, src_in, dst_in, attr_in, w_in, w1_in, w_self, w_neigh, b0, gamma0, beta0,
              w1_1, b1_1, w2_1, b2_1, w1_2, b1_2, w2_2, b2_2, w_ih, w_hh, b_ih, b_hh,
              gamma2, beta2, mean2, var2, w_3, b_3, out):
    cell_rows = nc.dram_tensor("cell_rows", (P * (CELL_CHUNKS + SPARE), 4), F32, kind="Internal").ap()
    dst_rows = nc.dram_tensor("dst_rows", (P * (DST_CHUNKS + SPARE), EW), F32, kind="Internal").ap()
    p_rows = nc.dram_tensor("p_rows", (NT * P, D), F32, kind="Internal").ap()
    wt_names = ["w1h", "w2", "ih0", "ih1", "ih2", "hh0", "hh1", "hh2", "w3"]
    wt_dram = {n: nc.dram_tensor("wt_" + n, (P, KT * D), F32, kind="Internal").ap() for n in wt_names}
    adj3_dram = nc.dram_tensor("adj3", (P, AW), F32, kind="Internal").ap()
    w1e_dram = nc.dram_tensor("wt_w1e", (P, D), F32, kind="Internal").ap()

    with ExitStack() as ctx:
        def sb(name, shape, dt=F32):
            return ctx.enter_context(nc.sbuf_tensor(name, shape, dt))

        def sem(name):
            return ctx.enter_context(nc.semaphore(name))

        def sb_under(name, shape, dt):
            with nc.sbuf_tensor(name, shape, dt) as tensor:
                return tensor

        low = sb_under("low", [P, 4 * D + 4 * P], F32R)
        hot_dst = low[:, 4 * D:].rearrange("p (c f) -> p c f", c=4)
        low_part = low[:, 0:4 * D].rearrange("p (c f) -> p c f", c=4)
        arena = sb("arena", [P, 2 * AW + 3 * NT * D])
        adj = arena[:, 0:2 * AW]
        matrices = arena[:, 0:3 * AW].rearrange("p (m f) -> p m f", m=3)
        nodes = arena[:, 2 * AW:].rearrange("p (a t d) -> p a t d", a=3, t=NT)
        xs = nodes[:, 0]
        h = nodes[:, 1]
        g = arena[:, 2 * AW + 2 * NT * D:]
        ws = sb("ws", [P, 2, KT, D])
        high = sb_under("high", [P, 4, D], F32R)
        tiles = sb("tiles", [P, 4, D])
        vec = sb("vec", [P, 3, D])
        cellm = sb("cellm", [P, CELL_CHUNKS, 4])
        pay1 = sb("pay1", [P, J, 4])
        idx1 = sb("idx1", [P, J], I32)
        idx2 = sb("idx2", [P, J], I32)
        pay2 = sb("pay2", [P, J, 2])
        ident = sb("ident", [P, P])
        iota1 = sb("iota1", [P, P])
        ones = sb("ones", [P, 1])
        stats = sb("stats", [P, 6])
        mv = sb("mv", [P, NT, 2])
        rstd = sb("rstd", [P, NT])
        one_mv = sb("one_mv", [P, 2])
        one_rstd = sb("one_rstd", [P, 1])
        deg = sb("deg", [P, 2 * NT])
        invc = sb("invc", [P, NT])
        dinv = sb("dinv", [P, NT])
        dmask = sb("dmask", [P, NT])
        tabf = sb("tabf", [P, 4])
        places_at = sb("places_at", [1, CELL_PAIRS + DST_PAIRS], I32)
        cell_at = places_at[:, 0:CELL_PAIRS]
        dst_at = places_at[:, CELL_PAIRS:]
        gidx = sb("gidx", [P, GROUP], I32)
        cring = tiles[:, 3, 0:COL * 4].rearrange("p (c w) -> p c w", c=COL)
        pb = [ctx.enter_context(nc.psum_tensor(f"pb{n}", [P, 512], F32)) for n in range(8)]

        adj3 = adj.rearrange("p (m c d) -> p m c d", m=2, c=CELLS)
        wst = g[:, 0:2 * KT * 640].rearrange("p (b k f) -> p b k f", b=2, k=KT)

        B1 = CELLS + 1
        B2 = NT + 1
        half = -(-B1 // 2)
        SW = B1 * J // 2
        oh = adj[:, 0:SW].bitcast(BF16).rearrange("p (b j) -> p b j", b=B1)
        cs = adj[:, SW:2 * SW].bitcast(BF16).rearrange("p (b j) -> p b j", b=B1)
        sel = adj[:, 2 * SW:2 * SW + half * J].rearrange("p (b j) -> p b j", b=half)
        assert 2 * SW + half * J <= 2 * CELLS * P

        xf = xs.rearrange("p t d -> p (t d)")
        cursor = [0]

        def temp(words, dt=F32):
            a = xf[:, cursor[0]:cursor[0] + words]
            cursor[0] += words
            return a if dt is F32 else a.bitcast(dt)

        srci, dsti = temp(J, I32), temp(J, I32)
        t_i = temp(J, I32)
        t_j = temp(J, I32)
        st_f, dt_f, cell_f = temp(J), temp(J), temp(J)
        cell_b = temp(J // 2).bitcast(BF16)
        dt_b = temp(J // 2).bitcast(BF16)
        wt_t, w1t_t = temp(J), temp(J)
        sum_a, sum_b = temp(J), temp(J)
        iob = temp(52).bitcast(BF16)
        iob_f = temp(104)
        tri = temp(P)
        onesq = temp(P)
        ptot = temp(B1)
        pcum = temp(B1)
        cnts = temp(B1)
        cnti = temp(B1, I32)
        nsup = temp(B1)
        endp = temp(B1)
        offs = temp(B1)
        pidx = temp(2)
        cmp_t = temp(B1)
        assert cursor[0] <= NT * D

        assert GROUP * P + GROUP // 2 * 3 * P <= arena.shape[1] - 3 * AW
        spare = arena[:, 3 * AW:]
        ohs = spare[:, 0:GROUP * P].rearrange("p (c s) -> p c s", c=GROUP)
        ohd_a = spare[:, GROUP * P:(GROUP + 12) * P].rearrange("p (c m d) -> p c m d", c=4, m=3)
        ohd_b = tiles[:].rearrange("p b f -> p (b f)")[:, 0:12 * P].rearrange("p (c m d) -> p c m d", c=4, m=3)
        deg_parts = spare[:, 0:2 * NT * P].rearrange("p (m t d) -> p m t d", m=2, t=NT)

        def ohd(k, n):
            return ohd_a[:, k:k + n] if k < 4 else ohd_b[:, k - 4:k - 4 + n]

        agg0 = g[:, 2048:2048 + 2 * D].rearrange("p (b f) -> p b f", b=2)
        aggT0 = g[:, 3072:3072 + 2 * D].rearrange("p (b k n) -> p b k n", b=2, k=KT)
        y0 = g[:, 4096:4096 + 2 * D].rearrange("p (b f) -> p b f", b=2)
        hT = tiles[:, 0:2].rearrange("p b (k n) -> p b k n", k=KT)
        g1 = g[:, 0:NT * DH].rearrange("p (t f) -> p t f", t=NT)
        x1 = g[:, NT * DH:2 * NT * DH].rearrange("p (t f) -> p t f", t=NT)
        a1 = tiles[:, 2, :].rearrange("p (b f) -> p b f", b=2)
        a1T = tiles[:, 3, :].rearrange("p (b k n) -> p b k n", b=2, k=2)
        y1 = tiles[:, 0:2]
        w1_sb = ws[:, 0].rearrange("p k f -> p (k f)")[:, 0:KT * DH].rearrange("p (k f) -> p k f", k=KT)
        w2_sb = ws[:, 0].rearrange("p k f -> p (k f)")[:, KT * DH:KT * DH + 2 * D].rearrange("p (k f) -> p k f", k=2)
        r2 = g.rearrange("p (t f) -> p t f", t=NT)
        gru_w = adj[:, 4 * (D + P):4 * (D + P) + 6 * KT * D].rearrange("p (b k f) -> p b k f", b=6, k=KT)
        acur = [4 * (D + P) + 6 * KT * D]

        def adj_part(words):
            a = adj[:, acur[0]:acur[0] + words]
            acur[0] += words
            return a

        rows = adj_part(GROUP * D).rearrange("p (c f) -> p c f", c=GROUP)
        erow = adj_part(GROUP * EW).rearrange("p (c f) -> p c f", c=GROUP)
        erow_i = erow.bitcast(I32)
        erowT = adj_part(4 * P).rearrange("p (c f) -> p c f", c=4)
        w1e_sb = adj_part(D)
        hot_far = adj_part(2 * P).rearrange("p (c f) -> p c f", c=2)
        gates = rows[:, 0:4]
        hgT = [tiles[:, 1], rows[:, 4]]
        aggT2 = [tiles[:, 3], rows[:, 5]]
        vec2 = adj_part(8 * D).rearrange("p (v f) -> p v f", v=8)
        assert acur[0] <= 2 * CELLS * P
        adj_part3 = adj[:, 0:2 * NT * P].rearrange("p (b s d) -> p b s d", b=2, s=NT)
        b1_v, b2_v, bx_v, by_v, bz_v, bw_v, sc_v, sh_v = (vec2[:, k] for k in range(8))
        ering = sb("ering", [P, COL, EW])
        ering_i = ering[:].bitcast(I32)

        loaded = sem("loaded")
        edges_loaded = sem("edges_loaded")
        raw_loaded = [sem(f"raw_loaded{k}") for k in range(2)]
        wt_stored = [sem(f"wt_stored{k}") for k in range(2)]
        vec_loaded = sem("vec_loaded")
        const_ready = sem("const_ready")
        zero_ready = sem("zero_ready")
        zeroed = sem("zeroed")
        step = sem("step")
        totals_ready = sem("totals_ready")
        order_ready = [sem(f"order_ready{k}") for k in range(2)]
        vec_folded = sem("vec_folded")
        x1_ready = sem("x1_ready")
        square_ready, root_ready = sem("square_ready"), sem("root_ready")
        sums_clear = sem("sums_clear")
        for_act, act_read = sem("for_act"), sem("act_read")
        for_dve, dve_read = sem("for_dve"), sem("dve_read")
        c_ready = sem("c_ready")
        pool_passed = sem("pool_passed")
        c_scattered = [sem(f"c_scattered{k}") for k in range(COL)]
        cells_loaded = sem("cells_loaded")
        e_loaded = [sem(f"e_loaded{k}") for k in range(2)]
        e_ready = sem("e_ready")
        e_scattered = [sem(f"e_scattered{k}") for k in range(COL)]
        x_free = sem("x_free")
        src_distance, src_hot = sem("src_distance"), sem("src_hot")
        dst_hot, weighted = sem("dst_hot"), sem("weighted")
        block_done, block_added = sem("block_done"), sem("block_added")
        adj3_stored = [sem(f"adj3_stored{k}") for k in range(3)]
        adj3_loaded = [sem(f"adj3_loaded{k}") for k in range(2)]
        deg_ready = sem("deg_ready")
        h_ready = sem("h_ready")
        w_loaded = sem("w_loaded")
        p_stored = [sem(f"p_stored{k}") for k in range(2)]
        g_ready = sem("g_ready")
        g_landed = [sem(f"g_landed{k}") for k in range(GROUP)]
        erow_landed = [sem(f"erow_landed{k}") for k in range(2)]
        turned, turned_read = sem("turned"), sem("turned_read")
        hot_distance = sem("hot_distance")
        edge_mm, msg_added, high_ready, msg_ready = sem("edge_mm"), sem("msg_added"), sem("high_ready"), sem("msg_ready")
        hot_ready, summed, sums_added = sem("hot_ready"), sem("summed"), sem("sums_added")
        gru_loaded = sem("gru_loaded")
        w1e_loaded = sem("w1e_loaded")
        vec2_loaded = sem("vec2_loaded")
        gate_in, gate_out = sem("gate_in"), sem("gate_out")
        x_done = sem("x_done")
        stored = sem("stored")

        blocks = [("w1h", 0), ("w2", 0), ("ih0", 0), ("ih1", 1), ("ih2", 2), ("hh0", 0), ("hh1", 1), ("hh2", 2),
                  ("w3", 0), ("self", 0), ("neigh", 0)]
        act_jobs = [("w", n, k) for n in range(len(blocks)) for k in range(5 if n == 0 else KT)]
        act_jobs += [(kind, t) for t in range(NT) for kind in ("h0T", "agg0T")]
        act_jobs += [("h1T", t) for t in range(NT)] + [("a1T", t) for t in range(NT)]
        act_jobs += [("h2T", t) for t in range(NT)]
        act_jobs += [("r2T", 0), ("hgT", 0), ("agg2T", 0), ("r2T", 1)]
        for t in range(1, NT):
            act_jobs += [("hgT", t), ("agg2T", t)] + ([("r2T", t + 1)] if t + 1 < NT else [])
        act_jobs += [("agg3T", t) for t in range(NT)]
        A = numbered(act_jobs)
        dve_jobs = ["prefix1", "prefix2", "tables", "deg", ("agg0", 0)]
        for t in range(NT):
            dve_jobs += ([("agg0", t + 1)] if t + 1 < NT else []) + [("y0", t)]
        dve_jobs += [("g1", t) for t in range(NT)] + [("x1", t) for t in range(NT)] + [("a1", 0)]
        for t in range(NT):
            dve_jobs += ([("a1", t + 1)] if t + 1 < NT else []) + [("y1", t)]
        dve_jobs += [("p2", t) for t in range(NT)]
        dve_jobs += [("agg2", 0)]
        for t in range(NT):
            dve_jobs += ([("agg2", t + 1)] if t + 1 < NT else []) + [("r", t), ("z", t), ("hn", t), ("in", t)]
        dve_jobs += [("agg3", 0)]
        for t in range(NT):
            dve_jobs += ([("agg3", t + 1)] if t + 1 < NT else []) + [("y3", t)]
        V = numbered(dve_jobs)
        root_jobs = ["h0", "dinv"] + [("y0", t) for t in range(NT)] + ["h1"]
        root_jobs += [(kind, t) for t in range(NT) for kind in ("n1", "h2")] + ["bn"] + [("h3", t) for t in range(NT)]
        ROOT = numbered(root_jobs)
        wj = {b: A[("w", b, KT - 1 if b else 4)] + 1 for b in range(len(blocks))}
        raw_src = {"w1h": w1_2, "w2": w2_2, "ih0": w_ih, "ih1": w_ih, "ih2": w_ih, "hh0": w_hh, "hh1": w_hh,
                   "hh2": w_hh, "w3": w_3, "self": w_self, "neigh": w_neigh}

        def act_bank(job):
            return pb[A[job] % 4]

        def dve_bank(job):
            return pb[4 + V[job] % 4]

        def e_bank(k):
            return pb[(2, 3, 6, 7)[k % 4]]

        block = ctx.enter_context(nc.Block())

        def store_weights(sp, n):
            sp.wait_ge(act_read, wj[n])
            if n == 0:
                sp.dma_start(w1e_dram, tiles[:, 0]).then_inc(wt_stored[0], 16)
            sp.dma_start(wt_dram[blocks[n][0]], ws[:, n % 2].rearrange("p k f -> p (k f)")).then_inc(wt_stored[n % 2], 16)

        @block.sync
        def _(sp):
            def column(dst, src1d):
                sp.dma_start(dst[:, 0:JV], src1d[0:JV * P].rearrange("(p j) -> p j", j=JV)).then_inc(edges_loaded, 16)
                sp.dma_start(dst[0:REST, JV:JV + 1], src1d[JV * P:E].rearrange("(p j) -> p j", j=1)).then_inc(edges_loaded, 16)

            sp.wait_ge(const_ready, 1)
            column(srci, src_in)
            column(dsti, dst_in)
            column(wt_t, w_in)
            column(w1t_t, w1_in.rearrange("e a -> (e a)"))
            sp.wait_ge(zero_ready, 1)
            zc = (CELL_CHUNKS + SPARE) * 4
            sp.dma_start(cell_rows.rearrange("(p c) w -> p (c w)", p=P), h.rearrange("p t d -> p (t d)")[:, 0:zc]).then_inc(zeroed, 16)
            zd = (DST_CHUNKS + SPARE) * EW
            part = zd // 6
            dz = dst_rows.rearrange("(p c) w -> p (c w)", p=P)
            for k in range(6):
                sp.dma_start(dz[:, k * part:(k + 1) * part], h.rearrange("p t d -> p (t d)")[:, 0:part]).then_inc(zeroed, 16)
            for n, (name, third) in enumerate(blocks):
                if n >= 2:
                    sp.wait_ge(for_act, wj[n - 2])
                wide = DE + D if name == "w1h" else D
                raw = raw_src[name]
                sp.dma_start(wst[:, n % 2, :, 0:wide],
                             raw[third * D:(third + 1) * D, :].rearrange("(o p) f -> p o f", p=P)).then_inc(raw_loaded[n % 2], 16)
                if n >= 1 and n - 1 < len(wt_names):
                    store_weights(sp, n - 1)
            for k, v in enumerate((b0, gamma0, beta0)):
                sp.dma_start(vec[:, k], v.rearrange("(a f) -> a f", a=1).to_broadcast([P, D])).then_inc(vec_loaded, 16)
            for k in range(COL):
                sp.wait_ge(c_scattered[k], 16 * (J // COL))
            sp.dma_start(cellm[:].rearrange("p c w -> p (c w)"),
                         cell_rows.rearrange("(p c) w -> p (c w)", p=P)[:, 0:CELL_CHUNKS * 4]).then_inc(cells_loaded, 16)
            edge_v = attr_in[0:JV * P, :].rearrange("(p j) f -> p j f", j=JV)
            for q in range(2):
                sp.dma_start(ering[:, 4 * q:4 * q + 4, 0:DE], edge_v[:, 4 * q:4 * q + 4, :]).then_inc(e_loaded[q], 16)
            sp.wait_ge(block_added, CELL_PAIRS)
            edges3 = [0, NT * D, 2 * NT * D, AW]
            for k in range(3):
                part3 = slice(edges3[k], edges3[k + 1])
                sp.dma_start(adj3_dram[:, part3], matrices[:, 2, part3]).then_inc(adj3_stored[k], 16)
            sp.wait_ge(x_free, 1)
            for t in range(NT - 1):
                if t == 0:
                    sp.wait_ge(adj3_stored[0], 16)
                sp.dma_start(xs[:, t], x_in[t * P:(t + 1) * P, :]).then_inc(loaded, 16)
            sp.dma_start(xs[0:LAST, NT - 1], x_in[(NT - 1) * P:N, :]).then_inc(loaded, 16)
            turns = J // COL

            def edge_turn(i, last):
                for q in range(2):
                    for k in range(4 * q, 4 * q + 4):
                        sp.wait_ge(e_scattered[k], 16 * i)
                    if not last or q == 0:
                        sp.dma_start(ering[:, 4 * q:4 * q + 4, 0:DE],
                                     edge_v[:, bass.ds(COL * i + 4 * q, 4), :]).then_inc(e_loaded[q], 16)
                    else:
                        k = JV - COL * i
                        sp.dma_start(ering[:, 4:k, 0:DE], edge_v[:, COL * i + 4:JV, :]).then_inc(e_loaded[q], 16)
                        sp.dma_start(ering[0:REST, k, 0:DE], attr_in[JV * P:E, :]).then_inc(e_loaded[q], 16)

            with sp.Fori(1, turns - 1) as i:
                edge_turn(i, False)
            edge_turn(turns - 1, True)
            sp.wait_ge(wt_stored[0], 16 * 6)
            sp.wait_ge(wt_stored[1], 16 * 4)
            sp.wait_ge(h_ready, 2 * NT)
            sp.dma_start(w1_sb, w1_1.rearrange("(k p) f -> p k f", p=P)).then_inc(w_loaded, 16)
            sp.dma_start(w2_sb, w2_1.rearrange("(k p) f -> p k f", p=P)).then_inc(w_loaded, 16)
            sp.dma_start(ws[:, 1].rearrange("p k f -> p (k f)"), wt_dram["w1h"]).then_inc(w_loaded, 16)
            sp.dma_start(vec[:, 0, 0:DH], b1_1.rearrange("(a f) -> a f", a=1).to_broadcast([P, DH])).then_inc(vec_loaded, 16)
            sp.dma_start(vec[:, 1], b2_1.rearrange("(a f) -> a f", a=1).to_broadcast([P, D])).then_inc(vec_loaded, 16)
            sp.wait_ge(h_ready, 3 * NT)
            sp.dma_start(ws[:, 0].rearrange("p k f -> p (k f)"), wt_dram["w2"]).then_inc(w_loaded, 16)
            for k, v in enumerate((b1_2, b2_2, b_ih[0:D], b_ih[D:2 * D], b_ih[2 * D:3 * D], b_hh[2 * D:3 * D], gamma2, beta2)):
                sp.dma_start(vec2[:, k], v.rearrange("(a f) -> a f", a=1).to_broadcast([P, D])).then_inc(vec2_loaded, 16)
            sp.dma_start(vec[:, 0], b_hh[0:D].rearrange("(a f) -> a f", a=1).to_broadcast([P, D])).then_inc(vec2_loaded, 16)
            sp.dma_start(vec[:, 1], b_hh[D:2 * D].rearrange("(a f) -> a f", a=1).to_broadcast([P, D])).then_inc(vec2_loaded, 16)
            sp.dma_start(w1e_sb, w1e_dram).then_inc(w1e_loaded, 16)
            for k, name in enumerate(wt_names[2:8]):
                sp.dma_start(gru_w[:, k].rearrange("p k f -> p (k f)"), wt_dram[name]).then_inc(gru_loaded, 16)
            for t in range(NT):
                sp.wait_ge(dve_read, V[("p2", t)] + 1)
                sp.dma_start(p_rows[t * P:(t + 1) * P, :], tiles[:, 2 + t % 2]).then_inc(p_stored[t % 2], 16)
            for k in range(COL):
                sp.wait_ge(e_scattered[k], 16 * turns)
            edge_t = dst_rows.rearrange("(p c) w -> p c w", p=P)

            def rows_turn(i):
                for q in range(2):
                    at_least(sp, turned, GROUP * i + 4 * q - 4)
                    at_least(sp, g_ready, 4 * i + 2 * q - 2)
                    at_least(sp, hot_ready, GROUP * i + 4 * q - 4)
                    sp.dma_start(erow[:, 4 * q:4 * q + 4], edge_t[:, bass.ds(GROUP * i + 4 * q, 4), :]).then_inc(erow_landed[q], 16)

            rows_turn(0)
            with sp.Fori(1, DST_CHUNKS // GROUP) as i:
                rows_turn(i)
            sp.wait_ge(vec_folded, 1)
            sp.dma_start(vec[:, 0], mean2.rearrange("(a f) -> a f", a=1).to_broadcast([P, D])).then_inc(vec2_loaded, 16)
            sp.dma_start(vec[:, 1], var2.rearrange("(a f) -> a f", a=1).to_broadcast([P, D])).then_inc(vec2_loaded, 16)
            sp.dma_start(vec[:, 2], b_3.rearrange("(a f) -> a f", a=1).to_broadcast([P, D])).then_inc(vec_loaded, 16)
            sp.dma_start(ws[:, 1].rearrange("p k f -> p (k f)"), wt_dram["w3"]).then_inc(w_loaded, 16)
            sp.wait_ge(for_dve, V[("in", NT - 1)] + 1)

            def load_adj3(t):
                sp.dma_start(adj_part3[:, t % 2], adj3_dram.rearrange("p (t s d) -> p t s d", t=NT, s=NT)[:, t]
                             ).then_inc(adj3_loaded[t % 2], 16)

            load_adj3(0)
            load_adj3(1)
            for t in range(2, NT):
                sp.wait_ge(for_dve, V[("agg3", t - 2)] + 1)
                load_adj3(t)
            for t in range(NT):
                n = P if t + 1 < NT else LAST
                sp.wait_ge(x_done, t + 1)
                sp.dma_start(out[t * P:t * P + n, :], xs[0:n, t]).then_inc(stored, 16)
            sp.wait_ge(stored, 16 * NT)

        @block.gpsimd
        def _(pool):
            def passed():
                pool.sem_inc(pool_passed, 1)

            nc.gpsimd.memset(srci, 0)
            nc.gpsimd.memset(dsti, NT * P)
            nc.gpsimd.memset(wt_t, 0.0)
            nc.gpsimd.memset(w1t_t, 0.0).then_inc(const_ready, 1)
            nc.gpsimd.memset(h, 0.0).then_inc(zero_ready, 1)
            nc.gpsimd.memset(ident[:], 1.0).then_inc(const_ready, 1)
            nc.gpsimd.memset(tri, 1.0).then_inc(const_ready, 1)
            pool.wait_ge(const_ready, 3)
            nc.gpsimd.affine_select(out=ident[:], in_=ident[:], compare_op=ALU.is_equal, fill=0.0, base=0,
                                    pattern=[[1, P]], channel_multiplier=-1).then_inc(const_ready, 1)
            nc.gpsimd.affine_select(out=tri, in_=tri, compare_op=ALU.is_gt, fill=0.0, base=0,
                                    pattern=[[1, P]], channel_multiplier=-1).then_inc(const_ready, 1)
            nc.gpsimd.iota(iota1[:], [[1, P]], base=1, channel_multiplier=0,
                           allow_small_or_imprecise_dtypes=True).then_inc(const_ready, 1)
            nc.gpsimd.iota(iob_f, [[1, 104]], base=0, channel_multiplier=0,
                           allow_small_or_imprecise_dtypes=True).then_inc(const_ready, 1)
            nc.gpsimd.iota(pidx, [[P, 2]], base=0, channel_multiplier=1,
                           allow_small_or_imprecise_dtypes=True).then_inc(const_ready, 1)
            nc.gpsimd.memset(onesq, 1.0).then_inc(const_ready, 1)
            nc.gpsimd.memset(ones[:], 1.0).then_inc(const_ready, 1)
            pool.wait_ge(zeroed, 16 * 7)
            pool.wait_ge(order_ready[0], 1)

            def cell_turn(i):
                for q in range(2):
                    c = slice(4 * q, 4 * q + 4)
                    for k in range(4 * q, 4 * q + 4):
                        at_least(pool, c_scattered[k], 16 * i)
                    passed()
                    nc.gpsimd.tensor_copy(cring[:, c], pay1[:, bass.ds(COL * i + 4 * q, 4), :]).then_inc(c_ready, 1)
                    nc.gpsimd.tensor_copy(gidx[:, c], idx1[:, bass.ds(COL * i + 4 * q, 4)]).then_inc(c_ready, 1)
                    pool.wait_ge(c_ready, 4 * i + 2 * q + 2)
                    passed()
                    for k in range(4 * q, 4 * q + 4):
                        nc.gpsimd.indirect_dma_start(cell_rows[:, :], bass.IndirectOffsetOnAxis(gidx[:, k:k + 1], 0),
                                                     cring[:, k, :], None).then_inc(c_scattered[k], 16)

            cell_turn(0)
            with pool.Fori(1, J // COL) as i:
                cell_turn(i)

            pool.wait_ge(cells_loaded, 16)

            def weights_turn(i):
                for q in range(4):
                    pool.wait_ge(dst_hot, 4 * i + q + 1)
                    passed()
                    hot = ohd(2 * q, 2)
                    nc.gpsimd.tensor_tensor(hot[:, :, 1:3], hot[:, :, 0:1].to_broadcast([P, 2, 2, P]),
                                            cellm[:, bass.ds(GROUP * i + 2 * q, 2), 2:4].unsqueeze(3).to_broadcast([P, 2, 2, P]),
                                            ALU.mult).then_inc(weighted, 1)

            weights_turn(0)
            with pool.Fori(1, CELL_CHUNKS // GROUP) as i:
                weights_turn(i)

            pool.wait_ge(order_ready[1], 1)
            turns = J // COL

            nc.gpsimd.memset(ering[:, :, DE + 2:EW], 0.0).then_inc(e_ready, 1)

            def edge_turn(i, last):
                for q in range(2):
                    c = slice(4 * q, 4 * q + 4)
                    for k in range(4 * q, 4 * q + 4):
                        at_least(pool, e_scattered[k], 16 * i)
                    passed()
                    nc.gpsimd.tensor_copy(ering[:, c, DE:DE + 2], pay2[:, bass.ds(COL * i + 4 * q, 4), :]).then_inc(e_ready, 1)
                    nc.gpsimd.tensor_copy(gidx[:, c], idx2[:, bass.ds(COL * i + 4 * q, 4)]).then_inc(e_ready, 1)
                    pool.wait_ge(e_ready, 4 * i + 2 * q + 3)
                    passed()
                    pool.wait_ge(e_loaded[q], 16 * i + (32 if last and q else 16))
                    passed()
                    for k in range(4 * q, 4 * q + 4):
                        nc.gpsimd.indirect_dma_start(dst_rows[:, :], bass.IndirectOffsetOnAxis(gidx[:, k:k + 1], 0),
                                                     ering[:, k, :], None).then_inc(e_scattered[k], 16)

            edge_turn(0, False)
            with pool.Fori(1, turns - 1) as i:
                edge_turn(i, False)
            edge_turn(turns - 1, True)
            pool.wait_ge(h_ready, 3 * NT)
            nc.gpsimd.memset(g, 0.0).then_inc(sums_clear, 1)
            for k in range(2):
                pool.wait_ge(p_stored[k], 16 * (NT // 2))

            def gather_turn(i):
                for q in range(4):
                    at_least(pool, summed, GROUP * i + 2 * q - 6)
                    pool.wait_ge(erow_landed[q // 2], 16 * i + 16)
                    passed()
                    nc.gpsimd.tensor_copy(gidx[:, 2 * q:2 * q + 2], erow_i[:, 2 * q:2 * q + 2, DE]).then_inc(g_ready, 1)
                    pool.wait_ge(g_ready, 4 * i + q + 1)
                    passed()
                    for k in (2 * q, 2 * q + 1):
                        nc.gpsimd.indirect_dma_start(rows[:, k, :], None, p_rows[:, :],
                                                     bass.IndirectOffsetOnAxis(gidx[:, k:k + 1], 0)).then_inc(g_landed[k], 16)

            gather_turn(0)
            with pool.Fori(1, DST_CHUNKS // GROUP) as i:
                gather_turn(i)

        @block.scalar
        def _(act):
            def copy_job(job, dst, src=None):
                act.wait_ge(for_act, A[job] + 1)
                b = act_bank(job)
                nc.scalar.copy(dst, b[:, 0:src] if src else b[:]).then_inc(act_read, 1)

            for n in range(len(blocks)):
                if n >= 2:
                    m = n - 2
                    act.wait_ge(wt_stored[m % 2], 16 * (m // 2 + 1) + (16 if m % 2 == 0 else 0))
                for k in range(KT):
                    copy_job(("w", n, k), ws[:, n % 2, k])
                if n == 0:
                    copy_job(("w", 0, 4), tiles[:, 0])

            def flat(t4):
                return t4.rearrange("p k n -> p (k n)")

            def one_hot_sources():
                def turn(i):
                    for q in range(4):
                        at_least(act, block_done, 4 * i + q - 3)
                        for k in (2 * q, 2 * q + 1):
                            ins = nc.scalar.activation(ohs[:, k], iota1[:], ACT.Abs,
                                                       bias=cellm[:, bass.ds(GROUP * i + k, 1), 0:1].rearrange("p a w -> p (a w)"))
                        ins.then_inc(src_distance, 1)
                        act.wait_ge(src_distance, 4 * i + q + 1)
                        two = ohs[:, 2 * q:2 * q + 2].rearrange("p c s -> p (c s)")
                        nc.scalar.activation(two, two, ACT.Relu, bias=1.0, scale=-1.0).then_inc(src_hot, 1)

                turn(0)
                with act.Fori(1, CELL_CHUNKS // GROUP) as i:
                    turn(i)

            def root(job, ap):
                act.wait_ge(square_ready, ROOT[job] + 1)
                nc.scalar.activation(ap, ap, ACT.Sqrt).then_inc(root_ready, 1)

            act.wait_ge(for_act, wj[len(blocks) - 1])
            act.wait_ge(cells_loaded, 16)
            one_hot_sources()
            root("h0", rstd[:])
            root("dinv", dinv[:])
            for t in range(NT):
                if t >= 2:
                    act.wait_ge(for_dve, V[("y0", t - 2)] + 1)
                copy_job(("h0T", t), flat(hT[:, t % 2]))
                copy_job(("agg0T", t), flat(aggT0[:, t % 2]))
                root(("y0", t), one_rstd[:])
            root("h1", rstd[:])
            for t in range(NT):
                if t >= 2:
                    act.wait_ge(for_dve, V[("g1", t - 2)] + 1)
                else:
                    act.wait_ge(for_dve, V[("y0", NT - 2 + t)] + 1)
                copy_job(("h1T", t), flat(hT[:, t % 2]))
            for t in range(NT):
                if t >= 2:
                    act.wait_ge(for_dve, V[("y1", t - 2)] + 1)
                copy_job(("a1T", t), flat(a1T[:, t % 2]), DH)
                root(("n1", t), one_rstd[:])
                root(("h2", t), one_rstd[:])
            for t in range(NT):
                act.wait_ge(for_dve, V[("p2", t - 2)] + 1 if t >= 2 else 1)
                if t < 2:
                    act.wait_ge(h_ready, 3 * NT)
                copy_job(("h2T", t), flat(hT[:, t % 2]))
            def turned_copy(c, k):
                act.wait_ge(turned, c + 1)
                at_least(act, edge_mm, c - 3)
                nc.scalar.copy(erowT[:, k % 4], pb[k % 2][:, 0:P]).then_inc(turned_read, 1)

            def relu(c, k):
                act.wait_ge(msg_added, c + 1)
                at_least(act, summed, c - 3)
                nc.scalar.activation(high[:, k % 4], rows[:, k % GROUP], ACT.Relu).then_inc(high_ready, 1)

            def hot(c, k):
                act.wait_ge(turned, c + 1)
                nc.scalar.activation(hot_far[:, k % 2], iota1[:], ACT.Abs, bias=erow[:, k % GROUP, DE + 1:DE + 2]).then_inc(hot_distance, 1)
                at_least(act, summed, c - 3)
                act.wait_ge(hot_distance, c + 1)
                nc.scalar.activation(hot_dst[:, k % 4], hot_far[:, k % 2], ACT.Relu, bias=1.0, scale=-1.0).then_inc(hot_ready, 1)

            for c in range(3):
                turned_copy(c, c)
            hot(0, 0)
            relu(0, 0)

            def turn(i, last):
                for k in range(GROUP):
                    c = GROUP * i + k
                    if not last or k < GROUP - 3:
                        turned_copy(c + 3, k + 3)
                    if not last or k < GROUP - 1:
                        hot(c + 1, k + 1)
                        relu(c + 1, k + 1)

            turn(0, False)
            with act.Fori(1, DST_CHUNKS // GROUP - 1) as i:
                turn(i, False)
            turn(DST_CHUNKS // GROUP - 1, True)
            root("bn", vec[:, 1])
            def hg_copy(t):
                if t >= 2:
                    act.wait_ge(for_dve, V[("hn", t - 2)] + 1)
                copy_job(("hgT", t), hgT[t % 2])

            def agg_copy(t):
                if t >= 2:
                    act.wait_ge(for_dve, V[("in", t - 2)] + 1)
                copy_job(("agg2T", t), aggT2[t % 2])

            def r2_copy(t):
                if t >= 1:
                    act.wait_ge(for_dve, V[("agg2", t - 1)] + 1)
                copy_job(("r2T", t), flat(hT[:, 0]))

            r2_copy(0)
            hg_copy(0)
            agg_copy(0)
            r2_copy(1)
            for t in range(NT):
                if t + 1 < NT:
                    hg_copy(t + 1)
                    agg_copy(t + 1)
                    if t + 2 < NT:
                        r2_copy(t + 2)
                for k, gate in enumerate(("r", "z")):
                    act.wait_ge(dve_read, V[(gate, t)] + 1)
                    nc.scalar.activation(gates[:, k], gates[:, k], ACT.Sigmoid).then_inc(gate_out, 1)
                act.wait_ge(gate_in, t + 1)
                nc.scalar.activation(gates[:, 2], gates[:, 2], ACT.Tanh).then_inc(gate_out, 1)
                root(("h3", t), one_rstd[:])
            for t in range(NT):
                if t >= 2:
                    act.wait_ge(for_dve, V[("y3", t - 2)] + 1)
                copy_job(("agg3T", t), flat(hT[:, t % 2]))

        @block.tensor
        def _(pe):
            def to_act(job):
                at_least(pe, act_read, A[job] - 3)
                return act_bank(job)

            def to_dve(job):
                at_least(pe, dve_read, V[job] - 3)
                return dve_bank(job)

            def turn_tile(job, tile):
                b = to_act(job)
                k = tile.shape[-1] // P
                for q in range(k):
                    ins = nc.tensor.transpose(b[:, q * P:(q + 1) * P], tile[:, q * P:(q + 1) * P], ident[:])
                ins.then_inc(for_act, 1)

            def sort_products(job, cols):
                b = to_dve(job)
                nc.tensor.matmul(b[:, 0:cols], tri, ptot[:, 0:cols], start=True, stop=True)
                nc.tensor.matmul(b[:, 128:128 + cols], onesq, ptot[:, 0:cols], start=True, stop=True).then_inc(for_dve, 1)

            def turn_weights(n):
                pe.wait_ge(raw_loaded[n % 2], 16 * (n // 2 + 1))
                for k in range(5 if n == 0 else KT):
                    b = to_act(("w", n, k))
                    f = (k * P) % 640
                    for o in range(KT):
                        ins = nc.tensor.transpose(b[:, o * P:(o + 1) * P], wst[:, n % 2, o, f:f + P], ident[:])
                    ins.then_inc(for_act, 1)

            pe.wait_ge(const_ready, 10)
            pe.wait_ge(totals_ready, 1)
            sort_products("prefix1", B1)
            for n in range(4):
                turn_weights(n)
            pe.wait_ge(totals_ready, 2)
            sort_products("prefix2", B2)
            for n in range(4, len(blocks)):
                turn_weights(n)
            pe.wait_ge(order_ready[1], 1)
            b = to_dve("tables")
            nc.tensor.matmul(b[0:1, 0:P], tabf[:, 0:1], ident[:], start=True, stop=True)
            nc.tensor.matmul(b[0:1, P:2 * P], tabf[:, 1:2], ident[:], start=True, stop=True)
            nc.tensor.matmul(b[0:1, 2 * P:3 * P], tabf[:, 2:3], ident[:], start=True, stop=True).then_inc(for_dve, 1)

            def build_blocks():
                def turn(i):
                    for q in range(4):
                        n = 4 * i + q
                        at_least(pe, block_added, n - 3)
                        pe.wait_ge(src_hot, n + 1)
                        pe.wait_ge(weighted, n + 1)
                        for k in range(2):
                            ins = nc.tensor.matmul(pb[q][:, 0:3 * P], ohs[:, 2 * q + k],
                                                   ohd(2 * q + k, 1).rearrange("p a m d -> p (a m d)"), start=k == 0, stop=k == 1)
                        ins.then_inc(block_done, 1)

                turn(0)
                with pe.Fori(1, CELL_PAIRS // 4) as i:
                    turn(i)

            pe.wait_ge(act_read, wj[len(blocks) - 1])
            build_blocks()
            pe.wait_ge(deg_ready, 1)
            b = to_dve("deg")
            for m in range(2):
                for t in range(NT):
                    ins = nc.tensor.matmul(b[:, m * NT + t:m * NT + t + 1], deg_parts[:, m, t], ones[:], start=True, stop=True)
            ins.then_inc(for_dve, 1)

            def matrix(m, t):
                return adj3[:, m, t * NT:(t + 1) * NT]

            def sum_neighbours(job, blocks_of, rows_of, wide):
                b = to_dve(job)
                for s in range(NT):
                    ins = nc.tensor.matmul(b[:, 0:wide], blocks_of[:, s], rows_of[:, s, 0:wide],
                                           start=s == 0, stop=s == NT - 1)
                ins.then_inc(for_dve, 1)

            def linear(job, parts, wide):
                b = to_dve(job)
                n = sum(x.shape[1] for x, _ in parts)
                m = 0
                for x, w in parts:
                    for k in range(x.shape[1]):
                        ins = nc.tensor.matmul(b[:, 0:wide], x[:, k], w[:, k], start=m == 0, stop=m == n - 1)
                        m += 1
                ins.then_inc(for_dve, 1)

            pe.wait_ge(h_ready, NT)
            sum_neighbours(("agg0", 0), matrix(0, 0), h, D)
            for t in range(NT):
                turn_tile(("h0T", t), h[:, t])
                if t + 1 < NT:
                    sum_neighbours(("agg0", t + 1), matrix(0, t + 1), h, D)
                pe.wait_ge(dve_read, V[("agg0", t)] + 1)
                turn_tile(("agg0T", t), agg0[:, t % 2])
                pe.wait_ge(act_read, A[("agg0T", t)] + 1)
                linear(("y0", t), [(hT[:, t % 2], ws[:, 1]), (aggT0[:, t % 2], ws[:, 0])], D)
            pe.wait_ge(w_loaded, 48)
            for t in range(NT):
                pe.wait_ge(h_ready, NT + t + 1)
                turn_tile(("h1T", t), h[:, t])
                if t:
                    pe.wait_ge(act_read, A[("h1T", t - 1)] + 1)
                    linear(("g1", t - 1), [(hT[:, (t - 1) % 2], w1_sb)], DH)
            pe.wait_ge(act_read, A[("h1T", NT - 1)] + 1)
            linear(("g1", NT - 1), [(hT[:, (NT - 1) % 2], w1_sb)], DH)
            pe.wait_ge(dve_read, V[("g1", NT - 1)] + 1)
            for t in range(NT):
                sum_neighbours(("x1", t), matrix(1, t), g1, DH)
            pe.wait_ge(x1_ready, NT)
            sum_neighbours(("a1", 0), matrix(1, 0), x1, DH)
            for t in range(NT):
                if t + 1 < NT:
                    sum_neighbours(("a1", t + 1), matrix(1, t + 1), x1, DH)
                pe.wait_ge(dve_read, V[("a1", t)] + 1)
                turn_tile(("a1T", t), a1[:, t % 2])
                pe.wait_ge(act_read, A[("a1T", t)] + 1)
                linear(("y1", t), [(a1T[:, t % 2], w2_sb)], D)
            for t in range(NT):
                pe.wait_ge(h_ready, 2 * NT + t + 1)
                turn_tile(("h2T", t), h[:, t])
                if t:
                    pe.wait_ge(act_read, A[("h2T", t - 1)] + 1)
                    linear(("p2", t - 1), [(hT[:, (t - 1) % 2], ws[:, 1])], D)
            pe.wait_ge(act_read, A[("h2T", NT - 1)] + 1)
            linear(("p2", NT - 1), [(hT[:, (NT - 1) % 2], ws[:, 1])], D)
            pe.wait_ge(w1e_loaded, 16)
            pe.wait_ge(dve_read, V[("p2", NT - 1)] + 1)

            def t_edges(i, k):
                c = GROUP * i + k
                pe.wait_ge(erow_landed[k // 4], 16 * i + 16)
                at_least(pe, turned_read, c - 1)
                nc.tensor.transpose(pb[k % 2][:, 0:P], erow[:, k, 0:DE], ident[:]).then_inc(turned, 1)

            def m_edges(i, k):
                c = GROUP * i + k
                pe.wait_ge(turned_read, c + 1)
                at_least(pe, msg_added, c - 3)
                nc.tensor.matmul(e_bank(k)[:], erowT[:, k % 4], w1e_sb, start=True, stop=True).then_inc(edge_mm, 1)

            def s_edges(i, k):
                c = GROUP * i + k
                pe.wait_ge(msg_ready, c + 1)
                pe.wait_ge(hot_ready, c + 1)
                if k % 2 == 0:
                    at_least(pe, sums_added, GROUP // 2 * i + k // 2 - 1)
                sums, hot = pb[4 + (k // 2) % 2][:], hot_dst[:, k % 4]
                nc.tensor.matmul(sums, hot, high[:, k % 4], start=k % 2 == 0, stop=False)
                nc.tensor.matmul(sums, hot, low_part[:, k % 4], start=False, stop=k % 2 == 1).then_inc(summed, 1)

            for k in range(3):
                t_edges(0, k)
            m_edges(0, 0)
            m_edges(0, 1)

            def turn(i, first, last):
                for k in range(GROUP):
                    if not last or k < GROUP - 3:
                        t_edges(i + (k + 3) // GROUP, (k + 3) % GROUP)
                    if not last or k < GROUP - 2:
                        m_edges(i + (k + 2) // GROUP, (k + 2) % GROUP)
                    if not (first and k == 0):
                        s_edges(i if k else i - 1, (k - 1) % GROUP)

            turns = DST_CHUNKS // GROUP
            turn(0, True, False)
            with pe.Fori(1, turns - 1) as i:
                turn(i, False, False)
            turn(turns - 1, False, True)
            s_edges(turns - 1, GROUP - 1)
            pe.wait_ge(gru_loaded, 16 * 6)
            pe.wait_ge(w_loaded, 64)
            pe.wait_ge(sums_added, DST_PAIRS)
            def blocks4(tile):
                return tile.rearrange("p (k n) -> p k n", k=KT)

            def agg_linear(t):
                pe.wait_ge(act_read, A[("r2T", t)] + 1)
                linear(("agg2", t), [(hT[:, 0], ws[:, 0])], D)

            def agg_turn(t):
                pe.wait_ge(dve_read, V[("agg2", t)] + 1)
                turn_tile(("agg2T", t), tiles[:, 2])

            turn_tile(("r2T", 0), r2[:, 0])
            turn_tile(("hgT", 0), h[:, 0])
            agg_linear(0)
            agg_turn(0)
            turn_tile(("r2T", 1), r2[:, 1])
            for t in range(NT):
                hg, at = blocks4(hgT[t % 2]), blocks4(aggT2[t % 2])
                if t + 1 < NT:
                    agg_linear(t + 1)
                    turn_tile(("hgT", t + 1), h[:, t + 1])
                pe.wait_ge(act_read, A[("agg2T", t)] + 1)
                linear(("r", t), [(hg, gru_w[:, 3]), (at, gru_w[:, 0])], D)
                linear(("z", t), [(hg, gru_w[:, 4]), (at, gru_w[:, 1])], D)
                if t + 1 < NT:
                    agg_turn(t + 1)
                if t + 2 < NT:
                    turn_tile(("r2T", t + 2), r2[:, t + 2])
                linear(("hn", t), [(hg, gru_w[:, 5])], D)
                linear(("in", t), [(at, gru_w[:, 2])], D)
            pe.wait_ge(h_ready, 4 * NT)
            pe.wait_ge(w_loaded, 80)

            def sum_neighbours3(t):
                pe.wait_ge(adj3_loaded[t % 2], 16 * (t // 2 + 1))
                sum_neighbours(("agg3", t), adj_part3[:, t % 2], h, D)

            sum_neighbours3(0)
            for t in range(NT):
                if t + 1 < NT:
                    sum_neighbours3(t + 1)
                pe.wait_ge(dve_read, V[("agg3", t)] + 1)
                turn_tile(("agg3T", t), tiles[:, 2 + t % 2])
                pe.wait_ge(act_read, A[("agg3T", t)] + 1)
                linear(("y3", t), [(hT[:, t % 2], ws[:, 1])], D)

        @block.vector
        def _(dve):
            chain = [0]

            def link(ins):
                chain[0] += 1
                ins.then_inc(step, 1)
                dve.wait_ge(step, chain[0])

            vts, vtt, vstt = nc.vector.tensor_scalar, nc.vector.tensor_tensor, nc.vector.scalar_tensor_tensor

            dve.wait_ge(const_ready, 10)
            dve.wait_ge(edges_loaded, 16 * 8)
            link(nc.vector.tensor_copy(iob, iob_f))
            link(vts(t_i, srci, 7, None, ALU.arith_shift_right))
            link(nc.vector.tensor_copy(st_f, t_i))
            link(vts(t_j, dsti, 7, None, ALU.arith_shift_right))
            link(nc.vector.tensor_copy(dt_f, t_j))
            link(nc.vector.tensor_copy(dt_b, dt_f))
            link(vstt(cell_f, dt_f, float(NT), st_f, ALU.mult, ALU.add))
            link(nc.vector.tensor_copy(cell_b, cell_f))
            link(vts(t_i, srci, P - 1, None, ALU.bitwise_and))
            link(nc.vector.tensor_copy(st_f, t_i))
            link(vts(pay1[:, :, 0], st_f, 1.0, -1.0, ALU.add, ALU.mult))
            link(vts(t_j, dsti, P - 1, None, ALU.bitwise_and))
            link(nc.vector.tensor_copy(dt_f, t_j))
            link(vts(pay1[:, :, 1], dt_f, 1.0, None, ALU.add))
            nc.vector.tensor_copy(pay1[:, :, 2], wt_t)
            nc.vector.tensor_copy(pay1[:, :, 3], w1t_t)
            nc.vector.tensor_copy(pay2[:].bitcast(I32)[:, :, 0], srci)
            link(vts(pay2[:, :, 1], dt_f, 1.0, -1.0, ALU.add, ALU.mult))

            def places(buckets, bucket_of, chunks, job, idx, tab_cols):
                ohb, csb = oh[:, 0:buckets], cs[:, 0:buckets]
                link(vtt(ohb, iob[:, 0:buckets].unsqueeze(2).to_broadcast([P, buckets, J]),
                         bucket_of.unsqueeze(1).to_broadcast([P, buckets, J]), ALU.is_equal))
                flat_oh = ohb.rearrange("p b j -> p (b j)")
                flat_cs = csb.rearrange("p b j -> p (b j)")
                link(nc.vector.tensor_tensor_scan(flat_cs, flat_oh, flat_oh, 0.0, ALU.add, ALU.max))
                link(nc.vector.tensor_copy(pcum[:, 0:buckets], csb[:, :, J - 1]))
                nc.vector.tensor_copy(ptot[:, 0:1], pcum[:, 0:1])
                vtt(ptot[:, 1:buckets], pcum[:, 1:buckets], pcum[:, 0:buckets - 1],
                    ALU.subtract).then_inc(totals_ready, 1)
                b = dve_bank(job)
                dve.wait_ge(for_dve, V[job] + 1)
                link(vts(cnts[:, 0:buckets], b[:, 128:128 + buckets], float(PAIR - 1), None, ALU.add))
                link(nc.vector.tensor_copy(cnti[:, 0:buckets], cnts[:, 0:buckets]))
                link(vts(cnti[:, 0:buckets], cnti[:, 0:buckets], 8, None, ALU.arith_shift_right))
                link(nc.vector.tensor_copy(nsup[:, 0:buckets], cnti[:, 0:buckets]))
                link(nc.vector.tensor_tensor_scan(endp[:, 0:buckets], nsup[:, 0:buckets], nsup[:, 0:buckets], 0.0,
                                                  ALU.add, ALU.max))
                link(vtt(offs[:, 0:buckets], endp[:, 0:buckets], nsup[:, 0:buckets], ALU.subtract))
                link(vts(offs[:, 0:buckets], offs[:, 0:buckets], float(PAIR), None, ALU.mult))
                link(nc.vector.memset(offs[:, buckets - 1:buckets], float(chunks * P)))
                link(vtt(offs[:, 0:buckets], offs[:, 0:buckets], b[:, 0:buckets], ALU.add))
                link(vtt(offs[:, 0:buckets], offs[:, 0:buckets], pcum[:, 0:buckets], ALU.subtract))
                link(vtt(offs[:, 0:buckets], offs[:, 0:buckets], ptot[:, 0:buckets], ALU.add))
                ins = vts(offs[:, 0:buckets], offs[:, 0:buckets], -1.0, None, ALU.add)
                ins.then_inc(dve_read, 1)
                dve.wait_ge(dve_read, V[job] + 1)
                lo = 0
                out_sum = sum_a
                while lo < buckets:
                    hi = min(lo + half, buckets)
                    for q in range(lo, hi):
                        ins = vstt(sel[:, q - lo], csb[:, q], offs[:, q:q + 1], ohb[:, q], ALU.add, ALU.mult)
                    link(ins)
                    link(nc.vector.tensor_reduce(out_sum, sel[:, 0:hi - lo].rearrange("p b j -> p j b"), AX_X, ALU.add))
                    if out_sum is sum_b:
                        link(vtt(sum_a, sum_a, sum_b, ALU.add))
                    out_sum = sum_b
                    lo = hi
                link(nc.vector.tensor_copy(t_i, sum_a))
                link(vts(t_j, t_i, 7, None, ALU.arith_shift_right))
                link(vts(t_i, t_i, P - 1, None, ALU.bitwise_and))
                link(nc.vector.tensor_copy(sum_a, t_i))
                link(nc.vector.tensor_copy(sum_b, t_j))
                link(vstt(sum_a, sum_a, float(chunks + SPARE), sum_b, ALU.mult, ALU.add))
                link(nc.vector.tensor_copy(idx[:], sum_a))
                for n, col in enumerate(tab_cols):
                    link(vts(cmp_t[:, 0:buckets - 1], endp[:, 0:buckets - 1], pidx[:, n:n + 1], None, ALU.is_le))
                    link(nc.vector.tensor_reduce(tabf[:, col:col + 1], cmp_t[:, 0:buckets - 1], AX_X, ALU.add))

            places(B1, cell_b, CELL_CHUNKS, "prefix1", idx1, [0, 1])
            vts(tabf[:, 0:2], tabf[:, 0:2], float(CELLS - 1), float(P), ALU.min, ALU.mult).then_inc(order_ready[0], 1)
            places(B2, dt_b, DST_CHUNKS, "prefix2", idx2, [2])
            vts(tabf[:, 2:3], tabf[:, 2:3], float(NT - 1), float(D), ALU.min, ALU.mult).then_inc(order_ready[1], 1)
            b = dve_bank("tables")
            dve.wait_ge(for_dve, V["tables"] + 1)
            link(nc.vector.tensor_copy(cell_at, b[0:1, 0:CELL_PAIRS]))
            nc.vector.tensor_copy(dst_at, b[0:1, 2 * P:2 * P + DST_PAIRS]).then_inc(dve_read, 1)
            dve.wait_ge(dve_read, V["tables"] + 1)
            dve.wait_ge(zeroed, 16 * 7)
            dve.wait_ge(for_act, wj[len(blocks) - 1])
            link(nc.vector.memset(arena[:, 0:3 * AW], 0.0))

            def inverse_root(job, ap, square):
                square.then_inc(square_ready, 1)
                dve.wait_ge(root_ready, ROOT[job] + 1)
                link(nc.vector.reciprocal(ap, ap))

            def layernorm(job, dst, src):
                link(nc.vector.bn_stats(stats[:], src))
                link(nc.vector.bn_aggr(one_mv[:], stats[:]))
                inverse_root(job, one_rstd[:], vts(one_rstd[:], one_mv[:, 1:2], LN_EPS, None, ALU.add))
                link(vts(dst, src, one_mv[:, 0:1], one_rstd[:], ALU.subtract, ALU.mult))

            def moments(t):
                link(nc.vector.bn_stats(stats[:], xs[:, t]))
                link(nc.vector.bn_aggr(mv[:, t], stats[:]))

            def relu_norm_all(job):
                inverse_root(job, rstd[:], vts(rstd[:], mv[:, :, 1], LN_EPS, None, ALU.add))
                for t in range(NT):
                    link(vts(h[:, t], xs[:, t], mv[:, t, 0:1], rstd[:, t:t + 1], ALU.subtract, ALU.mult))
                    vts(h[:, t], h[:, t], 0.0, None, ALU.max).then_inc(h_ready, 1)

            def read(job, emit):
                dve.wait_ge(for_dve, V[job] + 1)
                emit(dve_bank(job)).then_inc(dve_read, 1)
                dve.wait_ge(dve_read, V[job] + 1)

            def hots(i, q):
                n = 4 * i + q
                at_least(dve, block_done, n - 3)
                vtt(ohd(2 * q, 2)[:, :, 0], iota1[:].unsqueeze(1).to_broadcast([P, 2, P]),
                    cellm[:, bass.ds(GROUP * i + 2 * q, 2), 1:2].to_broadcast([P, 2, P]), ALU.is_equal).then_inc(dst_hot, 1)

            def add_block(i, q):
                n = 4 * i + q
                at = dve.value_load(cell_at[0:1, bass.ds(n, 1)], min_val=0, max_val=(CELLS - 1) * P)
                dve.wait_ge(block_done, n + 1)
                at_least(dve, block_added, n)
                cell = matrices[:, :, bass.ds(at, P)]
                vtt(cell, pb[q][:, 0:3 * P].rearrange("p (m d) -> p m d", m=3), cell, ALU.add).then_inc(block_added, 1)

            def turn(i, last):
                for q in range(4):
                    if not last or q < 2:
                        hots(i + (q + 2) // 4, (q + 2) % 4)
                    add_block(i, q)

            dve.wait_ge(cells_loaded, 16)
            dve.wait_ge(wt_stored[0], 32)
            turns = CELL_PAIRS // 4
            hots(0, 0)
            hots(0, 1)
            turn(0, False)
            with dve.Fori(1, turns - 1) as i:
                turn(i, False)
            turn(turns - 1, True)
            dve.wait_ge(block_added, CELL_PAIRS)
            dve.wait_ge(adj3_stored[0], 16)
            nc.vector.memset(xs[:, NT - 1], 0.0).then_inc(x_free, 1)
            for m in range(2):
                for t in range(NT):
                    ins = nc.vector.tensor_reduce(deg_parts[:, m, t], adj3[:, m, t * NT:(t + 1) * NT].rearrange("p s d -> p d s"),
                                                  AX_X, ALU.add)
            ins.then_inc(deg_ready, 1)
            dve.wait_ge(loaded, 16 * NT)
            for t in range(NT):
                moments(t)
            dve.wait_ge(adj3_stored[1], 16)
            relu_norm_all("h0")
            read("deg", lambda b: nc.vector.tensor_copy(deg[:], b[:, 0:2 * NT]))
            link(vts(invc[:], deg[:, 0:NT], 1.0, None, ALU.max))
            link(nc.vector.reciprocal(invc[:], invc[:]))
            link(vts(dmask[:], deg[:, NT:2 * NT], 1.0, None, ALU.add))
            inverse_root("dinv", dinv[:], vts(dinv[:], dmask[:], 2.0 ** -116, None, ALU.max))
            link(vts(dmask[:], dmask[:], 0.0, None, ALU.is_gt))
            link(vtt(dinv[:], dinv[:], dmask[:], ALU.mult))
            dve.wait_ge(vec_loaded, 48)
            dve.wait_ge(adj3_stored[2], 16)

            def mean0(t):
                if t >= 2:
                    dve.wait_ge(for_act, A[("agg0T", t - 2)] + 1)
                read(("agg0", t), lambda b: vts(agg0[:, t % 2], b[:], invc[:, t:t + 1], None, ALU.mult))

            mean0(0)
            for t in range(NT):
                if t + 1 < NT:
                    mean0(t + 1)
                y = y0[:, t % 2]
                read(("y0", t), lambda b: vtt(y, b[:], vec[:, 0], ALU.add))
                layernorm(("y0", t), y, y)
                link(vtt(y, y, vec[:, 1], ALU.mult))
                link(vtt(y, y, vec[:, 2], ALU.add))
                link(vtt(xs[:, t], xs[:, t], y, ALU.add))
                link(nc.vector.bn_stats(stats[:], xs[:, t]))
                link(nc.vector.bn_aggr(mv[:, t], stats[:]))
            relu_norm_all("h1")
            for t in range(NT):
                read(("g1", t), lambda b: vts(g1[:, t], b[:, 0:DH], dinv[:, t:t + 1], None, ALU.mult))
            dve.wait_ge(vec_loaded, 80)
            for t in range(NT):
                x = x1[:, t]
                read(("x1", t), lambda b: vtt(x, b[:, 0:DH], g1[:, t], ALU.add))
                link(vstt(x, x, dinv[:, t:t + 1], vec[:, 0, 0:DH], ALU.mult, ALU.add))
                vts(x, x, 0.0, dinv[:, t:t + 1], ALU.max, ALU.mult).then_inc(x1_ready, 1)
            dve.wait_ge(x1_ready, NT)

            def sum1(t):
                if t >= 2:
                    dve.wait_ge(for_act, A[("a1T", t - 2)] + 1)
                read(("a1", t), lambda b: vtt(a1[:, t % 2], b[:, 0:DH], x1[:, t], ALU.add))

            sum1(0)
            for t in range(NT):
                if t + 1 < NT:
                    sum1(t + 1)
                y = y1[:, t % 2]
                read(("y1", t), lambda b: vstt(y, b[:], dinv[:, t:t + 1], vec[:, 1], ALU.mult, ALU.add))
                link(nc.vector.tensor_tensor_reduce(h[:, t], y, y, 1.0, 0.0, ALU.mult, ALU.add, one_rstd[:]))
                inverse_root(("n1", t), one_rstd[:], vts(one_rstd[:], one_rstd[:], 1e-24, None, ALU.max))
                link(vstt(xs[:, t], y, one_rstd[:], xs[:, t], ALU.mult, ALU.add))
                layernorm(("h2", t), h[:, t], xs[:, t])
                vts(h[:, t], h[:, t], 0.0, None, ALU.max).then_inc(h_ready, 1)
            dve.wait_ge(vec2_loaded, 16 * 10)
            link(vtt(bx_v, bx_v, vec[:, 0], ALU.add))
            vtt(by_v, by_v, vec[:, 1], ALU.add).then_inc(vec_folded, 1)
            for t in range(NT):
                if t >= 2:
                    dve.wait_ge(p_stored[t % 2], 16 * (t // 2))
                read(("p2", t), lambda b: vtt(tiles[:, 2 + t % 2], b[:], b1_v, ALU.add))
            dve.wait_ge(sums_clear, 1)

            def message(i, k):
                dve.wait_ge(edge_mm, GROUP * i + k + 1)
                dve.wait_ge(g_landed[k], 16 * i + 16)
                vtt(rows[:, k], e_bank(k)[:], rows[:, k], ALU.add).then_inc(msg_added, 1)

            def low(i, k):
                dve.wait_ge(high_ready, GROUP * i + k + 1)
                vstt(low_part[:, k % 4], rows[:, k], 0.0, high[:, k % 4].bitcast(F32), ALU.max, ALU.subtract).then_inc(msg_ready, 1)

            def add_sums(i, q):
                n = GROUP // 2 * i + q
                at = dve.value_load(dst_at[0:1, bass.ds(n, 1)], min_val=0, max_val=(NT - 1) * D)
                dve.wait_ge(summed, 2 * n + 2)
                at_least(dve, sums_added, n)
                tile = g[:, bass.ds(at, D)]
                vtt(tile, pb[4 + q % 2][:], tile, ALU.add).then_inc(sums_added, 1)

            def turn(i, first, last):
                for k in range(GROUP):
                    if not last or k < GROUP - 2:
                        message(i + (k + 2) // GROUP, (k + 2) % GROUP)
                    if not last or k < GROUP - 1:
                        low(i + (k + 1) // GROUP, (k + 1) % GROUP)
                    if k % 2 == 0 and not (first and k == 0):
                        add_sums(i if k else i - 1, (k // 2 - 1) % 4)

            turns = DST_CHUNKS // GROUP
            message(0, 0)
            message(0, 1)
            low(0, 0)
            turn(0, True, False)
            with dve.Fori(1, turns - 1) as i:
                turn(i, False, False)
            turn(turns - 1, False, True)
            add_sums(turns - 1, 3)
            dve.wait_ge(vec2_loaded, 16 * 12)
            inverse_root("bn", vec[:, 1], vts(vec[:, 1], vec[:, 1], BN_EPS, None, ALU.add))
            link(vtt(sc_v, sc_v, vec[:, 1], ALU.mult))
            link(vtt(vec[:, 0], vec[:, 0], sc_v, ALU.mult))
            link(vtt(sh_v, sh_v, vec[:, 0], ALU.subtract))
            dve.wait_ge(sums_added, DST_PAIRS)

            def sum2(t):
                if t >= 1:
                    dve.wait_ge(for_act, A[("agg2T", t - 1)] + 1)
                read(("agg2", t), lambda b: vstt(tiles[:, 2], b2_v, deg[:, t:t + 1], b[:], ALU.mult, ALU.add))

            sum2(0)
            for t in range(NT):
                if t + 1 < NT:
                    sum2(t + 1)
                r, z, n, m = (gates[:, k] for k in range(4))
                read(("r", t), lambda b: vtt(r, b[:], bx_v, ALU.add))
                read(("z", t), lambda b: vtt(z, b[:], by_v, ALU.add))
                read(("hn", t), lambda b: vtt(n, b[:], bw_v, ALU.add))
                dve.wait_ge(gate_out, 3 * t + 1)
                link(vtt(n, n, r, ALU.mult))
                read(("in", t), lambda b: vtt(m, b[:], bz_v, ALU.add))
                vtt(n, n, m, ALU.add).then_inc(gate_in, 1)
                link(vtt(xs[:, t], xs[:, t], h[:, t], ALU.add))
                dve.wait_ge(gate_out, 3 * t + 3)
                link(vtt(m, h[:, t], n, ALU.subtract))
                link(vtt(m, m, z, ALU.mult))
                link(vtt(m, m, n, ALU.add))
                link(vtt(m, m, sc_v, ALU.mult))
                link(vtt(m, m, sh_v, ALU.add))
                link(vtt(xs[:, t], xs[:, t], m, ALU.add))
                layernorm(("h3", t), h[:, t], xs[:, t])
                vts(h[:, t], h[:, t], 0.0, None, ALU.max).then_inc(h_ready, 1)
            dve.wait_ge(vec_loaded, 96)

            def sum3(t):
                if t >= 2:
                    dve.wait_ge(for_act, A[("agg3T", t - 2)] + 1)
                read(("agg3", t), lambda b: nc.vector.tensor_copy(tiles[:, 2 + t % 2], b[:]))

            sum3(0)
            for t in range(NT):
                if t + 1 < NT:
                    sum3(t + 1)
                read(("y3", t), lambda b: vtt(xs[:, t], b[:], xs[:, t], ALU.add))
                vtt(xs[:, t], xs[:, t], vec[:, 2], ALU.add).then_inc(x_done, 1)


_INS = ["x", "src", "dst", "edge_attr_128", "edge_weight", "edge_weight1", "L0_gnn_W_self", "L0_gnn_W_neigh",
        "L0_gnn_bias", "L0_gnn_gamma", "L0_gnn_beta", "L1_gnn_W1", "L1_gnn_b1", "L1_gnn_W2", "L1_gnn_b2",
        "L2_gnn_W1", "L2_gnn_b1", "L2_gnn_W2", "L2_gnn_b2", "L2_gnn_W_ih", "L2_gnn_W_hh", "L2_gnn_b_ih",
        "L2_gnn_b_hh", "L2_gnn_gamma", "L2_gnn_beta", "L2_gnn_run_mean", "L2_gnn_run_var", "L3_gnn_W", "L3_gnn_b"]


def kernel(**inputs):
    import numpy as _np
    import concourse.bacc as _bacc
    from concourse import mybir as _mybir
    from concourse.bass_utils import run_bass_kernel_spmd as _run

    nc = _bacc.Bacc("TRN2", target_bir_lowering=False, num_devices=1)
    arrays, args = {}, []
    for name in _INS:
        a = _np.ascontiguousarray(inputs[name])
        arrays[f"in_{name}_dram"] = a
        args.append(nc.dram_tensor(f"in_{name}_dram", a.shape, _mybir.dt.from_np(a.dtype), kind="ExternalInput").ap())
    args.append(nc.dram_tensor("out_0_dram", (N, D), _mybir.dt.float32, kind="ExternalOutput").ap())
    build_gnn(nc, *args)
    r = _run(nc, [arrays], core_ids=[0])
    return r.results[0]["out_0_dram"]
```

```python
from contextlib import ExitStack

import numpy as np
import concourse.bass as bass
from concourse import mybir

F32 = mybir.dt.float32
I32 = mybir.dt.int32
F32R = mybir.dt.float32r
BF16 = mybir.dt.bfloat16
ALU = mybir.AluOpType
ACT = mybir.ActivationFunctionType
AX_X = mybir.AxisListType.X

P = 128
N = 1250
E = 21250
D = 512
DH = 256
DE = 128
NT = -(-N // P)
KT = D // P
LAST = N - (NT - 1) * P
JV = E // P
REST = E - JV * P
COL = 8
J = -(-(JV + 1) // COL) * COL
PAIR = 2 * P
CELLS = NT * NT
CELL_PAIRS = (E + CELLS * (PAIR - 1)) // PAIR
CELL_PAIRS = -(-CELL_PAIRS // 8) * 8
CELL_CHUNKS = 2 * CELL_PAIRS
DST_PAIRS = -(-((E + NT * (PAIR - 1)) // PAIR) // 4) * 4
DST_CHUNKS = 2 * DST_PAIRS
AW = CELLS * P
SPARE = 2
EW = DE + 4
LN_EPS = 1e-5
BN_EPS = 1e-5
GROUP = 8
TURN = 8


def at_least(eng, semaphore, value):
    if not isinstance(value, int) or value > 0:
        eng.wait_ge(semaphore, value)


def numbered(names):
    return {name: n for n, name in enumerate(names)}


def build_gnn(nc, x_in, src_in, dst_in, attr_in, w_in, w1_in, w_self, w_neigh, b0, gamma0, beta0,
              w1_1, b1_1, w2_1, b2_1, w1_2, b1_2, w2_2, b2_2, w_ih, w_hh, b_ih, b_hh,
              gamma2, beta2, mean2, var2, w_3, b_3, out):
    cell_rows = nc.dram_tensor("cell_rows", (P * (CELL_CHUNKS + SPARE), 4), F32, kind="Internal").ap()
    dst_rows = nc.dram_tensor("dst_rows", (P * (DST_CHUNKS + SPARE), EW), F32, kind="Internal").ap()
    p_rows = nc.dram_tensor("p_rows", (NT * P, D), F32, kind="Internal").ap()
    stored_blocks = ["w1h", "hh0", "hh1", "hh2", "w3"]
    wt_names = stored_blocks + ["m0", "m1", "m2"]
    wt_dram = {n: nc.dram_tensor("wt_" + n, (P, KT * D), F32, kind="Internal").ap() for n in wt_names}
    c_dram = [nc.dram_tensor(f"c{k}", (P, D), F32, kind="Internal").ap() for k in range(3)]
    h0_dram = nc.dram_tensor("h0", (P, NT * D), F32, kind="Internal").ap()
    ys_dram = nc.dram_tensor("ys", (P, NT * D), F32, kind="Internal").ap()
    adj3_dram = nc.dram_tensor("adj3", (P, AW), F32, kind="Internal").ap()
    w1e_dram = nc.dram_tensor("wt_w1e", (P, D), F32, kind="Internal").ap()

    with ExitStack() as ctx:
        def sb(name, shape, dt=F32):
            return ctx.enter_context(nc.sbuf_tensor(name, shape, dt))

        def sem(name):
            return ctx.enter_context(nc.semaphore(name))

        def sb_under(name, shape, dt):
            with nc.sbuf_tensor(name, shape, dt) as tensor:
                return tensor

        low = sb_under("low", [P, 4 * D + 4 * P], F32R)
        hot_dst = low[:, 4 * D:].rearrange("p (c f) -> p c f", c=4)
        low_part = low[:, 0:4 * D].rearrange("p (c f) -> p c f", c=4)
        parts3 = sb_under("parts3", [P, 2 * NT * D + 4 * NT * P], F32R)
        h3 = parts3[:, 0:2 * NT * D].rearrange("p (a s f) -> p a s f", a=2, s=NT)
        a3 = parts3[:, 2 * NT * D:].rearrange("p (b a s d) -> p b a s d", b=2, a=2, s=NT)
        arena = sb("arena", [P, 2 * AW + 3 * NT * D])
        adj = arena[:, 0:2 * AW]
        matrices = arena[:, 0:3 * AW].rearrange("p (m f) -> p m f", m=3)
        nodes = arena[:, 2 * AW:].rearrange("p (a t d) -> p a t d", a=3, t=NT)
        xs = nodes[:, 0]
        h = nodes[:, 1]
        g = arena[:, 2 * AW + 2 * NT * D:]
        ws = sb("ws", [P, 2, KT, D])
        high = sb_under("high", [P, 4, D], F32R)
        tiles = sb("tiles", [P, 4, D])
        vec = sb("vec", [P, 3, D])
        cellm = sb("cellm", [P, CELL_CHUNKS, 4])
        pay1 = sb("pay1", [P, J, 4])
        idx1 = sb("idx1", [P, J], I32)
        idx2 = sb("idx2", [P, J], I32)
        pay2 = sb("pay2", [P, J, 2])
        ident = sb("ident", [P, P])
        iota1 = sb("iota1", [P, P])
        ones = sb("ones", [P, 1])
        stats = sb("stats", [P, 6])
        mv = sb("mv", [P, NT, 2])
        rstd = sb("rstd", [P, NT])
        one_mv = sb("one_mv", [P, 2])
        one_rstd = sb("one_rstd", [P, 1])
        deg = sb("deg", [P, 2 * NT])
        invc = sb("invc", [P, NT])
        dinv = sb("dinv", [P, NT])
        dmask = sb("dmask", [P, NT])
        tabf = sb("tabf", [P, 4])
        places_at = sb("places_at", [1, CELL_PAIRS + DST_PAIRS], I32)
        cell_at = places_at[:, 0:CELL_PAIRS]
        dst_at = places_at[:, CELL_PAIRS:]
        gidx = sb("gidx", [P, GROUP], I32)
        cring = tiles[:, 3, 0:COL * 4].rearrange("p (c w) -> p c w", c=COL)
        pb = [ctx.enter_context(nc.psum_tensor(f"pb{n}", [P, 512], F32)) for n in range(8)]

        adj3 = adj.rearrange("p (m c d) -> p m c d", m=2, c=CELLS)
        wst = g[:, 0:2 * KT * 640].rearrange("p (b k f) -> p b k f", b=2, k=KT)

        B1 = CELLS + 1
        B2 = NT + 1
        THIRD = J // 3
        assert THIRD % COL == 0
        SW = B1 * J // 2
        oh = adj[:, 0:SW].bitcast(BF16).rearrange("p (b j) -> p b j", b=B1)
        cs = adj[:, SW:2 * SW].bitcast(BF16).rearrange("p (b j) -> p b j", b=B1)
        sel = adj[:, 2 * SW:2 * SW + B1 * THIRD]
        assert 2 * SW + B1 * THIRD <= 2 * AW and B2 * J <= B1 * THIRD

        xf = xs.rearrange("p t d -> p (t d)")
        cursor = [0]

        def temp(words, dt=F32):
            a = xf[:, cursor[0]:cursor[0] + words]
            cursor[0] += words
            return a if dt is F32 else a.bitcast(dt)

        srci, dsti = temp(J, I32), temp(J, I32)
        t_i = temp(J, I32)
        t_j = temp(J, I32)
        st_f, dt_f, cell_f = temp(J), temp(J), temp(J)
        cell_b = temp(J // 2).bitcast(BF16)
        dt_b = temp(J // 2).bitcast(BF16)
        wt_t, w1t_t = temp(J), temp(J)
        sum_a, sum_b = temp(J), temp(J)
        iob = temp(52).bitcast(BF16)
        iob_f = temp(104)
        tri = temp(P)
        onesq = temp(P)
        ptot = temp(B1)
        pcum = temp(B1)
        cnts = temp(B1)
        cnti = temp(B1, I32)
        nsup = temp(B1)
        endp = temp(B1)
        offs = temp(B1)
        pidx = temp(2)
        cmp_t = temp(B1)
        assert cursor[0] <= NT * D

        assert GROUP * P + GROUP // 2 * 3 * P <= arena.shape[1] - 3 * AW
        spare = arena[:, 3 * AW:]
        ohs = spare[:, 0:GROUP * P].rearrange("p (c s) -> p c s", c=GROUP)
        ohd_a = spare[:, GROUP * P:(GROUP + 12) * P].rearrange("p (c m d) -> p c m d", c=4, m=3)
        ohd_b = tiles[:].rearrange("p b f -> p (b f)")[:, 0:12 * P].rearrange("p (c m d) -> p c m d", c=4, m=3)
        deg_parts = spare[:, 0:2 * NT * P].rearrange("p (m t d) -> p m t d", m=2, t=NT)

        def ohd(k, n):
            return ohd_a[:, k:k + n] if k < 4 else ohd_b[:, k - 4:k - 4 + n]

        hf = h.rearrange("p t d -> p (t d)")
        w2_raw = hf[:, 0:KT * D].rearrange("p (k f) -> p k f", k=KT)
        m_out = hf[:, KT * D:2 * KT * D].rearrange("p (k f) -> p k f", k=KT)
        b2_wide = hf[:, 2 * KT * D:2 * KT * D + D].rearrange("p (k f) -> p k f", k=KT)
        c_out = hf[:, 2 * KT * D + D:2 * KT * D + 2 * D]
        b2_col = vec[:, 0, 0:KT]
        early = adj[:, 0:6 * D].rearrange("p (b f) -> p b f", b=6)
        he, ye = early[:, 0:4], early[:, 4:6]
        agg0 = g[:, 2048:2048 + 2 * D].rearrange("p (b f) -> p b f", b=2)
        aggT0 = g[:, 3072:3072 + 2 * D].rearrange("p (b k n) -> p b k n", b=2, k=KT)
        y0 = g[:, 4096:4096 + 2 * D].rearrange("p (b f) -> p b f", b=2)
        hT = tiles[:, 0:2].rearrange("p b (k n) -> p b k n", k=KT)
        g1 = g[:, 0:NT * DH].rearrange("p (t f) -> p t f", t=NT)
        x1 = g[:, NT * DH:2 * NT * DH].rearrange("p (t f) -> p t f", t=NT)
        a1 = tiles[:, 2, :].rearrange("p (b f) -> p b f", b=2)
        a1T = tiles[:, 3, :].rearrange("p (b k n) -> p b k n", b=2, k=2)
        y1 = tiles[:, 0:2]
        w1_sb = ws[:, 1].rearrange("p k f -> p (k f)")[:, 0:KT * DH].rearrange("p (k f) -> p k f", k=KT)
        w2_sb = ws[:, 1].rearrange("p k f -> p (k f)")[:, KT * DH:KT * DH + 2 * D].rearrange("p (k f) -> p k f", k=2)
        r2 = g.rearrange("p (t f) -> p t f", t=NT)
        gru_w = adj[:, low.shape[1]:low.shape[1] + 6 * KT * D].rearrange("p (b k f) -> p b k f", b=6, k=KT)
        gru_end = low.shape[1] + 6 * KT * D
        acur = [gru_end]

        def adj_part(words):
            a = adj[:, acur[0]:acur[0] + words]
            acur[0] += words
            return a

        rows = adj_part(GROUP * D).rearrange("p (c f) -> p c f", c=GROUP)
        erow = adj_part(GROUP * EW).rearrange("p (c f) -> p c f", c=GROUP)
        erow_i = erow.bitcast(I32)
        erowT = adj_part(4 * P).rearrange("p (c f) -> p c f", c=4)
        w1e_sb = adj_part(D)
        free = cellm[:].rearrange("p c w -> p (c w)")
        hot_far = free[:, 2 * D:2 * D + 2 * P].rearrange("p (c f) -> p c f", c=2)
        gates = rows[:, 0:4]
        h2T = rows[:, 0:2].rearrange("p b (k n) -> p b k n", k=KT)
        hgT = [tiles[:, 1], rows[:, 4]]
        r2T = [tiles[:, 0], rows[:, 5]]
        vec2_start = acur[0]
        vec2 = adj_part(8 * D).rearrange("p (v f) -> p v f", v=8)
        assert acur[0] <= 2 * CELLS * P
        at3 = gru_end + 6 * D
        assert at3 >= parts3.shape[1] and at3 + 2 * NT * P <= vec2_start
        adj_part3 = adj[:, at3:at3 + 2 * NT * P].rearrange("p (b s d) -> p b s d", b=2, s=NT)
        b1_v, bx_v, by_v, bz_v, bw_v, cr_v, cz_v, cn_v = (vec2[:, k] for k in range(8))
        sc_v, sh_v = free[:, 0:D], free[:, D:2 * D]
        ering = sb("ering", [P, COL, EW])

        loaded = sem("loaded")
        edges_loaded = sem("edges_loaded")
        raw_loaded = [sem(f"raw_loaded{k}") for k in range(2)]
        wt_stored = [sem(f"wt_stored{k}") for k in range(2)]
        vec_loaded = sem("vec_loaded")
        const_ready = sem("const_ready")
        zero_ready = sem("zero_ready")
        zeroed = sem("zeroed")
        step = sem("step")
        totals_ready = sem("totals_ready")
        order_ready = [sem(f"order_ready{k}") for k in range(2)]
        sorted_all = sem("sorted_all")
        vec_folded = sem("vec_folded")
        x1_ready = sem("x1_ready")
        square_ready, root_ready = sem("square_ready"), sem("root_ready")
        sums_clear = sem("sums_clear")
        for_act, act_read = sem("for_act"), sem("act_read")
        for_dve, dve_read = sem("for_dve"), sem("dve_read")
        c_ready = sem("c_ready")
        pool_passed = sem("pool_passed")
        c_scattered = [sem(f"c_scattered{k}") for k in range(COL)]
        cells_loaded = sem("cells_loaded")
        e_loaded = [sem(f"e_loaded{k}") for k in range(2)]
        e_ready = sem("e_ready")
        e_scattered = [sem(f"e_scattered{k}") for k in range(COL)]
        x_free = sem("x_free")
        src_distance, src_hot = sem("src_distance"), sem("src_hot")
        dst_hot, weighted = sem("dst_hot"), sem("weighted")
        block_done, block_added = sem("block_done"), sem("block_added")
        adj3_stored = [sem(f"adj3_stored{k}") for k in range(4)]
        adj3_loaded = [sem(f"adj3_loaded{k}") for k in range(2)]
        deg_ready = sem("deg_ready")
        w2_loaded, m_stored = sem("w2_loaded"), sem("m_stored")
        b2_loaded, b2_ready = sem("b2_loaded"), sem("b2_ready")
        xe_loaded = [sem(f"xe_loaded{k}") for k in range(NT)]
        he_ready = sem("he_ready")
        he_stored = [sem(f"he_stored{k}") for k in range(4)]
        ye_stored = [sem(f"ye_stored{k}") for k in range(2)]
        h0_loaded = [sem(f"h0_loaded{k}") for k in range(2)]
        ys_loaded = [sem(f"ys_loaded{k}") for k in range(2)]
        y_used = sem("y_used")
        high3, low3 = sem("high3"), sem("low3")
        p_loaded, w3_loaded = sem("p_loaded"), sem("w3_loaded")
        h_ready = sem("h_ready")
        w_loaded = sem("w_loaded")
        p_stored = [sem(f"p_stored{k}") for k in range(2)]
        g_ready = sem("g_ready")
        g_landed = [sem(f"g_landed{k}") for k in range(GROUP)]
        erow_landed = [sem(f"erow_landed{k}") for k in range(2)]
        turned, turned_read = sem("turned"), sem("turned_read")
        hot_distance = sem("hot_distance")
        edge_mm, msg_added, high_ready, msg_ready = sem("edge_mm"), sem("msg_added"), sem("high_ready"), sem("msg_ready")
        hot_ready, summed, sums_added = sem("hot_ready"), sem("summed"), sem("sums_added")
        gru_loaded = sem("gru_loaded")
        b1_loaded = sem("b1_loaded")
        w1e_loaded = sem("w1e_loaded")
        vec2_loaded = sem("vec2_loaded")
        gate_in, gate_out = sem("gate_in"), sem("gate_out")
        x_done = sem("x_done")
        stored = sem("stored")

        blocks = [("w1h", 0), ("hh0", 0), ("hh1", 1), ("hh2", 2), ("w3", 0), ("ih0", 0), ("ih1", 1), ("ih2", 2),
                  ("neigh", 0), ("self", 0)]
        PREFIX2_AFTER = 8
        act_jobs = []
        for n, (name, third) in enumerate(blocks):
            act_jobs += [("w", n, k) for k in range(5 if n == 0 else KT)]
            if name[0:2] == "ih":
                act_jobs += [("m", third, k) for k in range(KT)] + [("c", third)]
        act_jobs += [("hsT", t) for t in range(NT)]
        act_jobs += ["deg"] + [("agg0T", t) for t in range(NT)]
        h1_jobs = [("h1T", 0)]
        for t in range(NT):
            h1_jobs += ([("h1T", t + 1)] if t + 1 < NT else []) + [("g1", t)]
        act_jobs += h1_jobs + [("a1T", t) for t in range(NT)]
        act_jobs += [("h2T", t) for t in range(NT)]
        act_jobs += [(kind, t) for t in range(NT) for kind in ("r2T", "hgT")]
        act_jobs += [("agg3T", t) for t in range(NT)]
        A = numbered(act_jobs)
        dve_jobs = ["prefix1", "prefix2", "tables"] + [("ys", t) for t in range(NT)] 

        def sums_then(a, y):
            order = [(a, 0), (a, 1)]
            for t in range(NT):
                order += ([(a, t + 2)] if t + 2 < NT else []) + [(y, t)]
            return order

        dve_jobs += sums_then("agg0", "y0")
        dve_jobs += [("x1", t) for t in range(NT)] + sums_then("a1", "y1")
        dve_jobs += [("p2", t) for t in range(NT)]
        for t in range(NT):
            dve_jobs += [("r", t), ("z", t), ("hn", t), ("in", t)]
        dve_jobs += sums_then("agg3", "y3")
        V = numbered(dve_jobs)
        root_jobs = [("he", t) for t in range(NT)] + ["dinv"] + [("y0", t) for t in range(NT - 1)] + ["h1", ("y0", NT - 1), ("h1", NT - 1)]
        root_jobs += [(kind, t) for t in range(NT) for kind in ("n1", "h2")] + ["bn"] + [("h3", t) for t in range(NT)]
        ROOT = numbered(root_jobs)
        A_LOW3 = [1] + [NT + 1 + t for t in range(1, NT)]
        wj = {b: A[("w", b, KT - 1 if b else 4)] + 1 for b in range(len(blocks))}
        raw_src = {"w1h": w1_2, "ih0": w_ih, "ih1": w_ih, "ih2": w_ih, "hh0": w_hh, "hh1": w_hh,
                   "hh2": w_hh, "w3": w_3, "self": w_self, "neigh": w_neigh}

        def act_bank(job):
            return pb[A[job] % 4]

        def dve_bank(job):
            return pb[4 + V[job] % 4]

        def e_bank(k):
            return pb[(2, 3, 6, 7)[k % 4]]

        block = ctx.enter_context(nc.Block())

        def store_weights(sp, n):
            sp.wait_ge(act_read, wj[n])
            if n == 0:
                sp.dma_start(w1e_dram, tiles[:, 0]).then_inc(wt_stored[0], 16)
            sp.dma_start(wt_dram[blocks[n][0]], ws[:, n % 2].rearrange("p k f -> p (k f)")).then_inc(wt_stored[n % 2], 16)

        @block.sync
        def _(sp):
            def column(dst, src1d):
                sp.dma_start(dst[:, 0:JV], src1d[0:JV * P].rearrange("(p j) -> p j", j=JV)).then_inc(edges_loaded, 16)
                sp.dma_start(dst[0:REST, JV:JV + 1], src1d[JV * P:E].rearrange("(p j) -> p j", j=1)).then_inc(edges_loaded, 16)

            sp.wait_ge(const_ready, 1)
            column(srci, src_in)
            column(dsti, dst_in)
            column(wt_t, w_in)
            column(w1t_t, w1_in.rearrange("e a -> (e a)"))
            for k in range(KT):
                sp.dma_start(b2_col[:, k:k + 1], b2_2[k * P:(k + 1) * P].rearrange("(p a) -> p a", a=1)).then_inc(b2_loaded, 16)
            sp.wait_ge(zero_ready, 1)
            zc = (CELL_CHUNKS + SPARE) * 4
            sp.dma_start(cell_rows.rearrange("(p c) w -> p (c w)", p=P), h.rearrange("p t d -> p (t d)")[:, 0:zc]).then_inc(zeroed, 16)
            zd = (DST_CHUNKS + SPARE) * EW
            part = zd // 6
            dz = dst_rows.rearrange("(p c) w -> p (c w)", p=P)
            for k in range(6):
                sp.dma_start(dz[:, k * part:(k + 1) * part], h.rearrange("p t d -> p (t d)")[:, 0:part]).then_inc(zeroed, 16)
            for n, (name, third) in enumerate(blocks):
                if n >= 2:
                    sp.wait_ge(for_act, wj[n - 2])
                wide = DE + D if name == "w1h" else D
                raw = raw_src[name]
                sp.dma_start(wst[:, n % 2, :, 0:wide],
                             raw[third * D:(third + 1) * D, :].rearrange("(o p) f -> p o f", p=P)).then_inc(raw_loaded[n % 2], 16)
                if n == 3:
                    sp.wait_ge(zeroed, 16 * 7)
                    sp.dma_start(w2_raw, w2_2.rearrange("(o p) f -> p o f", p=P)).then_inc(w2_loaded, 16)
                if 1 <= n <= len(stored_blocks):
                    store_weights(sp, n - 1)
                if blocks[n - 2][0][0:2] == "ih":
                    gate = blocks[n - 2][1]
                    sp.wait_ge(act_read, A[("c", gate)] + 1)
                    sp.dma_start(wt_dram[f"m{gate}"], m_out.rearrange("p k f -> p (k f)")).then_inc(m_stored, 16)
                    sp.dma_start(c_dram[gate], c_out).then_inc(m_stored, 16)
            sp.wait_ge(b2_ready, 1)
            for k, v in enumerate((b0, gamma0, beta0)):
                sp.dma_start(vec[:, k], v.rearrange("(a f) -> a f", a=1).to_broadcast([P, D])).then_inc(vec_loaded, 16)
            sp.wait_ge(sorted_all, 1)
            sp.wait_ge(x_free, 1)
            for t in range(NT):
                n = P if t + 1 < NT else LAST
                sp.dma_start(xs[0:n, t], x_in[t * P:t * P + n, :]).then_inc(xe_loaded[t], 16)
            for t in range(1, NT + 2):
                if t <= NT:
                    sp.wait_ge(he_ready, t)
                    sp.dma_start(h0_dram[:, (t - 1) * D:t * D], he[:, (t - 1) % 4]).then_inc(he_stored[(t - 1) % 4], 16)
                if t >= 2:
                    sp.wait_ge(dve_read, V[("ys", t - 2)] + 1)
                    sp.dma_start(ys_dram[:, (t - 2) * D:(t - 1) * D], ye[:, t % 2]).then_inc(ye_stored[t % 2], 16)
            sp.wait_ge(for_dve, V[("ys", NT - 1)] + 1)
            for k in range(4):
                sp.wait_ge(he_stored[k], 16 * ((NT + 3 - k) // 4))
            sp.dma_start(ws[:, 1].rearrange("p k f -> p (k f)"), h0_dram[:, 0:KT * D]).then_inc(h0_loaded[0], 16)
            for k in range(COL):
                sp.wait_ge(c_scattered[k], 16 * (J // COL))
            sp.dma_start(cellm[:].rearrange("p c w -> p (c w)"),
                         cell_rows.rearrange("(p c) w -> p (c w)", p=P)[:, 0:CELL_CHUNKS * 4]).then_inc(cells_loaded, 16)
            edge_v = attr_in[0:JV * P, :].rearrange("(p j) f -> p j f", j=JV)
            for q in range(2):
                sp.dma_start(ering[:, 4 * q:4 * q + 4, 0:DE], edge_v[:, 4 * q:4 * q + 4, :]).then_inc(e_loaded[q], 16)
            sp.wait_ge(block_added, CELL_PAIRS)
            edges3 = [0, NT * D, (NT + KT) * D, 2 * NT * D, AW]

            def store3(k):
                part3 = slice(edges3[k], edges3[k + 1])
                sp.dma_start(adj3_dram[:, part3], matrices[:, 2, part3]).then_inc(adj3_stored[k], 16)

            store3(2)
            sp.wait_ge(adj3_stored[2], 16)
            sp.dma_start(hf[:, KT * D:], h0_dram[:, KT * D:]).then_inc(h0_loaded[1], 16)
            store3(3)
            store3(1)
            store3(0)
            for k in range(2):
                sp.wait_ge(ye_stored[k], 16 * (NT // 2))
            sp.wait_ge(x_free, 2)
            for t in range(NT - 1):
                if t == 0:
                    sp.wait_ge(adj3_stored[0], 16)
                sp.dma_start(xs[:, t], x_in[t * P:(t + 1) * P, :]).then_inc(loaded, 16)
            sp.dma_start(xs[0:LAST, NT - 1], x_in[(NT - 1) * P:N, :]).then_inc(loaded, 16)
            turns = J // COL

            def edge_turn(i, last):
                for q in range(2):
                    for k in range(4 * q, 4 * q + 4):
                        sp.wait_ge(e_scattered[k], 16 * i)
                    if not last or q == 0:
                        sp.dma_start(ering[:, 4 * q:4 * q + 4, 0:DE],
                                     edge_v[:, bass.ds(COL * i + 4 * q, 4), :]).then_inc(e_loaded[q], 16)
                    else:
                        k = JV - COL * i
                        sp.dma_start(ering[:, 4:k, 0:DE], edge_v[:, COL * i + 4:JV, :]).then_inc(e_loaded[q], 16)
                        sp.dma_start(ering[0:REST, k, 0:DE], attr_in[JV * P:E, :]).then_inc(e_loaded[q], 16)

            with sp.Fori(1, turns - 1) as i:
                edge_turn(i, False)
            edge_turn(turns - 1, True)
            sp.wait_ge(wt_stored[0], 16 * 4)
            sp.wait_ge(wt_stored[1], 16 * 2)
            sp.wait_ge(m_stored, 16 * 6)
            sp.wait_ge(for_dve, V[("y0", NT - 1)] + 1)
            sp.dma_start(ws[:, 0].rearrange("p k f -> p (k f)"), wt_dram["w1h"]).then_inc(p_loaded, 16)
            sp.wait_ge(for_dve, V[("a1", NT - 1)] + 1)
            sp.dma_start(b1_v, b1_2.rearrange("(a f) -> a f", a=1).to_broadcast([P, D])).then_inc(b1_loaded, 16)
            for v, row in ((bx_v, b_ih[0:D]), (by_v, b_ih[D:2 * D]), (bz_v, b_ih[2 * D:3 * D]),
                           (bw_v, b_hh[2 * D:3 * D]), (sc_v, gamma2), (sh_v, beta2)):
                sp.dma_start(v, row.rearrange("(a f) -> a f", a=1).to_broadcast([P, D])).then_inc(vec2_loaded, 16)
            for v, k in ((cr_v, 0), (cz_v, 1), (cn_v, 2)):
                sp.dma_start(v, c_dram[k]).then_inc(vec2_loaded, 16)
            sp.dma_start(w1e_sb, w1e_dram).then_inc(w1e_loaded, 16)
            sp.wait_ge(h_ready, 2 * NT)
            sp.dma_start(vec[:, 0], b_hh[0:D].rearrange("(a f) -> a f", a=1).to_broadcast([P, D])).then_inc(vec2_loaded, 16)
            sp.dma_start(vec[:, 1], b_hh[D:2 * D].rearrange("(a f) -> a f", a=1).to_broadcast([P, D])).then_inc(vec2_loaded, 16)
            for t in range(NT):
                sp.wait_ge(dve_read, V[("p2", t)] + 1)
                sp.dma_start(p_rows[t * P:(t + 1) * P, :], tiles[:, 2 + t % 2]).then_inc(p_stored[t % 2], 16)
            for k in range(COL):
                sp.wait_ge(e_scattered[k], 16 * turns)
            edge_t = dst_rows.rearrange("(p c) w -> p c w", p=P)

            def rows_turn(i):
                for q in range(2):
                    at_least(sp, turned, GROUP * i + 4 * q - 4)
                    at_least(sp, g_ready, 4 * i + 2 * q - 2)
                    at_least(sp, hot_ready, GROUP * i + 4 * q - 4)
                    sp.dma_start(erow[:, 4 * q:4 * q + 4], edge_t[:, bass.ds(GROUP * i + 4 * q, 4), :]).then_inc(erow_landed[q], 16)

            gru_names = ["m0", "m1", "m2", "hh0", "hh1", "hh2"]
            for i, name in enumerate(gru_names):
                rows_turn(i)
                sp.dma_start(gru_w[:, i].rearrange("p k f -> p (k f)"), wt_dram[name]).then_inc(gru_loaded, 16)
            with sp.Fori(len(gru_names), DST_CHUNKS // GROUP) as i:
                rows_turn(i)
            sp.wait_ge(vec_folded, 1)
            sp.dma_start(vec[:, 0], mean2.rearrange("(a f) -> a f", a=1).to_broadcast([P, D])).then_inc(vec2_loaded, 16)
            sp.dma_start(vec[:, 1], var2.rearrange("(a f) -> a f", a=1).to_broadcast([P, D])).then_inc(vec2_loaded, 16)
            sp.dma_start(vec[:, 2], b_3.rearrange("(a f) -> a f", a=1).to_broadcast([P, D])).then_inc(vec_loaded, 16)
            sp.dma_start(ws[:, 1].rearrange("p k f -> p (k f)"), wt_dram["w3"]).then_inc(w3_loaded, 16)
            sp.wait_ge(sums_added, DST_PAIRS)

            def load_adj3(t):
                sp.dma_start(adj_part3[:, t % 2], adj3_dram.rearrange("p (t s d) -> p t s d", t=NT, s=NT)[:, t]
                             ).then_inc(adj3_loaded[t % 2], 16)

            load_adj3(0)
            load_adj3(1)
            for t in range(2, NT):
                sp.wait_ge(low3, A_LOW3[t - 2])
                load_adj3(t)
            for t in range(NT):
                n = P if t + 1 < NT else LAST
                sp.wait_ge(x_done, t + 1)
                sp.dma_start(out[t * P:t * P + n, :], xs[0:n, t]).then_inc(stored, 16)
            sp.wait_ge(stored, 16 * NT)

        @block.gpsimd
        def _(pool):
            def passed():
                pool.sem_inc(pool_passed, 1)

            nc.gpsimd.memset(srci, 0)
            nc.gpsimd.memset(dsti, NT * P)
            nc.gpsimd.memset(wt_t, 0.0)
            nc.gpsimd.memset(w1t_t, 0.0).then_inc(const_ready, 1)
            nc.gpsimd.memset(h, 0.0).then_inc(zero_ready, 1)
            nc.gpsimd.memset(ident[:], 1.0).then_inc(const_ready, 1)
            nc.gpsimd.memset(tri, 1.0).then_inc(const_ready, 1)
            pool.wait_ge(const_ready, 3)
            nc.gpsimd.affine_select(out=ident[:], in_=ident[:], compare_op=ALU.is_equal, fill=0.0, base=0,
                                    pattern=[[1, P]], channel_multiplier=-1).then_inc(const_ready, 1)
            nc.gpsimd.affine_select(out=tri, in_=tri, compare_op=ALU.is_gt, fill=0.0, base=0,
                                    pattern=[[1, P]], channel_multiplier=-1).then_inc(const_ready, 1)
            nc.gpsimd.iota(iota1[:], [[1, P]], base=1, channel_multiplier=0,
                           allow_small_or_imprecise_dtypes=True).then_inc(const_ready, 1)
            nc.gpsimd.iota(iob_f, [[1, 104]], base=0, channel_multiplier=0,
                           allow_small_or_imprecise_dtypes=True).then_inc(const_ready, 1)
            nc.gpsimd.iota(pidx, [[P, 2]], base=0, channel_multiplier=1,
                           allow_small_or_imprecise_dtypes=True).then_inc(const_ready, 1)
            nc.gpsimd.memset(onesq, 1.0).then_inc(const_ready, 1)
            nc.gpsimd.memset(ones[:], 1.0).then_inc(const_ready, 1)
            pool.wait_ge(zeroed, 16 * 7)
            pool.wait_ge(b2_loaded, 16 * KT)
            passed()
            nc.gpsimd.tensor_copy(b2_wide, b2_col.unsqueeze(2).to_broadcast([P, KT, P])).then_inc(b2_ready, 1)

            def cell_turn(i):
                for q in range(2):
                    c = slice(4 * q, 4 * q + 4)
                    for k in range(4 * q, 4 * q + 4):
                        at_least(pool, c_scattered[k], 16 * i)
                    passed()
                    nc.gpsimd.tensor_copy(cring[:, c], pay1[:, bass.ds(COL * i + 4 * q, 4), :]).then_inc(c_ready, 1)
                    nc.gpsimd.tensor_copy(gidx[:, c], idx1[:, bass.ds(COL * i + 4 * q, 4)]).then_inc(c_ready, 1)
                    pool.wait_ge(c_ready, 4 * i + 2 * q + 2)
                    passed()
                    for k in range(4 * q, 4 * q + 4):
                        nc.gpsimd.indirect_dma_start(cell_rows[:, :], bass.IndirectOffsetOnAxis(gidx[:, k:k + 1], 0),
                                                     cring[:, k, :], None).then_inc(c_scattered[k], 16)

            for part in range(3):
                pool.wait_ge(order_ready[0], part + 1)
                first = part * (THIRD // COL)
                if part == 0:
                    cell_turn(0)
                    first = 1
                with pool.Fori(first, (part + 1) * (THIRD // COL)) as i:
                    cell_turn(i)

            pool.wait_ge(cells_loaded, 16)

            def weights_turn(i):
                for q in range(TURN):
                    pool.wait_ge(dst_hot, TURN * i + q + 1)
                    passed()
                    hot = ohd(2 * (q % 4), 2)
                    nc.gpsimd.tensor_tensor(hot[:, :, 1:3], hot[:, :, 0:1].to_broadcast([P, 2, 2, P]),
                                            cellm[:, bass.ds(2 * TURN * i + 2 * q, 2), 2:4].unsqueeze(3).to_broadcast([P, 2, 2, P]),
                                            ALU.mult).then_inc(weighted, 1)

            weights_turn(0)
            with pool.Fori(1, CELL_PAIRS // TURN) as i:
                weights_turn(i)

            pool.wait_ge(order_ready[1], 1)
            turns = J // COL

            nc.gpsimd.memset(ering[:, :, DE + 2:EW], 0.0).then_inc(e_ready, 1)

            def edge_turn(i, last):
                for q in range(2):
                    c = slice(4 * q, 4 * q + 4)
                    for k in range(4 * q, 4 * q + 4):
                        at_least(pool, e_scattered[k], 16 * i)
                    passed()
                    nc.gpsimd.tensor_copy(ering[:, c, DE:DE + 2], pay2[:, bass.ds(COL * i + 4 * q, 4), :]).then_inc(e_ready, 1)
                    nc.gpsimd.tensor_copy(gidx[:, c], idx2[:, bass.ds(COL * i + 4 * q, 4)]).then_inc(e_ready, 1)
                    pool.wait_ge(e_ready, 4 * i + 2 * q + 3)
                    passed()
                    pool.wait_ge(e_loaded[q], 16 * i + (32 if last and q else 16))
                    passed()
                    for k in range(4 * q, 4 * q + 4):
                        nc.gpsimd.indirect_dma_start(dst_rows[:, :], bass.IndirectOffsetOnAxis(gidx[:, k:k + 1], 0),
                                                     ering[:, k, :], None).then_inc(e_scattered[k], 16)

            edge_turn(0, False)
            with pool.Fori(1, turns - 1) as i:
                edge_turn(i, False)
            edge_turn(turns - 1, True)
            pool.wait_ge(h_ready, 2 * NT)
            nc.gpsimd.memset(g, 0.0).then_inc(sums_clear, 1)
            for k in range(2):
                pool.wait_ge(p_stored[k], 16 * (NT // 2))

            def gather_turn(i):
                for q in range(4):
                    at_least(pool, summed, GROUP * i + 2 * q - 6)
                    pool.wait_ge(erow_landed[q // 2], 16 * i + 16)
                    passed()
                    nc.gpsimd.tensor_copy(gidx[:, 2 * q:2 * q + 2], erow_i[:, 2 * q:2 * q + 2, DE]).then_inc(g_ready, 1)
                    pool.wait_ge(g_ready, 4 * i + q + 1)
                    passed()
                    for k in (2 * q, 2 * q + 1):
                        nc.gpsimd.indirect_dma_start(rows[:, k, :], None, p_rows[:, :],
                                                     bass.IndirectOffsetOnAxis(gidx[:, k:k + 1], 0)).then_inc(g_landed[k], 16)

            gather_turn(0)
            with pool.Fori(1, DST_CHUNKS // GROUP) as i:
                gather_turn(i)

        @block.scalar
        def _(act):
            def copy_job(job, dst, src=None):
                act.wait_ge(for_act, A[job] + 1)
                b = act_bank(job)
                nc.scalar.copy(dst, b[:, 0:src] if src else b[:]).then_inc(act_read, 1)

            for n in range(len(blocks)):
                m = n - 2
                if 0 <= m < len(stored_blocks):
                    act.wait_ge(wt_stored[m % 2], 16 * (m // 2 + 1) + (16 if m % 2 == 0 else 0))
                elif m >= 0:
                    act.wait_ge(for_act, A[("c", blocks[m][1])] + 1)
                for k in range(KT):
                    copy_job(("w", n, k), ws[:, n % 2, k])
                if n == 0:
                    copy_job(("w", 0, 4), tiles[:, 0])
                if blocks[n][0][0:2] == "ih":
                    gate = blocks[n][1]
                    if gate:
                        act.wait_ge(m_stored, 32 * gate)
                    for k in range(KT):
                        copy_job(("m", gate, k), m_out[:, k])
                    copy_job(("c", gate), c_out)

            def flat(t4):
                return t4.rearrange("p k n -> p (k n)")

            def one_hot_sources():
                def turn(i):
                    for q in range(TURN):
                        at_least(act, block_done, TURN * i + q - 3)
                        for k in (2 * q, 2 * q + 1):
                            ins = nc.scalar.activation(ohs[:, k % GROUP], iota1[:], ACT.Abs,
                                                       bias=cellm[:, bass.ds(2 * TURN * i + k, 1), 0:1].rearrange("p a w -> p (a w)"))
                        ins.then_inc(src_distance, 1)
                        act.wait_ge(src_distance, TURN * i + q + 1)
                        two = ohs[:, 2 * (q % 4):2 * (q % 4) + 2].rearrange("p c s -> p (c s)")
                        nc.scalar.activation(two, two, ACT.Relu, bias=1.0, scale=-1.0).then_inc(src_hot, 1)

                turn(0)
                with act.Fori(1, CELL_PAIRS // TURN) as i:
                    turn(i)

            def root(job, ap):
                act.wait_ge(square_ready, ROOT[job] + 1)
                nc.scalar.activation(ap, ap, ACT.Sqrt).then_inc(root_ready, 1)

            act.wait_ge(wt_stored[0], 32)
            root(("he", 0), one_rstd[:])
            root(("he", 1), one_rstd[:])
            for t in range(NT):
                if t >= 2:
                    act.wait_ge(for_dve, V[("ys", t - 2)] + 1)
                copy_job(("hsT", t), flat(hT[:, t % 2]))
                if t + 2 < NT:
                    root(("he", t + 2), one_rstd[:])
            act.wait_ge(cells_loaded, 16)
            act.wait_ge(for_act, wj[len(blocks) - 1])
            one_hot_sources()
            copy_job("deg", deg[:], 2 * NT)
            root("dinv", dinv[:])
            def load_ys(t):
                nc.scalar.dma_start(y0[:, t % 2], ys_dram[:, t * D:(t + 1) * D]).then_inc(ys_loaded[t % 2], 16)

            load_ys(0)
            load_ys(1)

            def turned0(t):
                if t >= 2:
                    act.wait_ge(for_dve, V[("y0", t - 2)] + 1)
                copy_job(("agg0T", t), flat(aggT0[:, t % 2]))

            turned0(0)
            for t in range(NT):
                if t + 1 < NT:
                    turned0(t + 1)
                if t < NT - 1:
                    root(("y0", t), one_rstd[:])
                if 1 <= t < NT - 1:
                    act.wait_ge(y_used, t)
                    load_ys(t + 1)
            act.wait_ge(for_dve, V[("agg0", NT - 1)] + 1)
            nc.scalar.dma_start(w1_sb, w1_1.rearrange("(k p) f -> p k f", p=P)).then_inc(w_loaded, 16)
            nc.scalar.dma_start(w2_sb, w2_1.rearrange("(k p) f -> p k f", p=P)).then_inc(w_loaded, 16)
            root("h1", rstd[:, 0:NT - 1])
            for n, (kind, t) in enumerate(h1_jobs):
                if n == 5:
                    root(("y0", NT - 1), one_rstd[:])
                if n == 9:
                    root(("h1", NT - 1), rstd[:, NT - 1:NT])
                if n == len(h1_jobs) - 2:
                    act.wait_ge(h_ready, NT)
                    nc.scalar.dma_start(vec[:, 0, 0:DH], b1_1.rearrange("(a f) -> a f", a=1).to_broadcast([P, DH])
                                        ).then_inc(vec_loaded, 16)
                    nc.scalar.dma_start(vec[:, 1], b2_1.rearrange("(a f) -> a f", a=1).to_broadcast([P, D])
                                        ).then_inc(vec_loaded, 16)
                if kind == "g1":
                    act.wait_ge(for_act, A[("g1", t)] + 1)
                    nc.scalar.activation(g1[:, t], act_bank(("g1", t))[:, 0:DH], ACT.Copy,
                                         scale=dinv[:, t:t + 1]).then_inc(act_read, 1)
                else:
                    if t >= 2:
                        act.wait_ge(for_act, A[("g1", t - 2)] + 1)
                    copy_job(("h1T", t), flat(hT[:, t % 2]))

            def turned1(t):
                if t >= 2:
                    act.wait_ge(for_dve, V[("y1", t - 2)] + 1)
                copy_job(("a1T", t), flat(a1T[:, t % 2]), DH)

            turned1(0)
            for t in range(NT):
                if t + 1 < NT:
                    turned1(t + 1)
                if t < NT - 1:
                    root(("n1", t), one_rstd[:])
                    root(("h2", t), one_rstd[:])
            act.wait_ge(for_dve, V[("a1", NT - 1)] + 1)
            for t in range(NT):
                if t >= 2:
                    act.wait_ge(for_dve, V[("p2", t - 2)] + 1)
                copy_job(("h2T", t), flat(h2T[:, t % 2]))
                if t == 0:
                    root(("n1", NT - 1), one_rstd[:])
                if t == 2:
                    root(("h2", NT - 1), one_rstd[:])
            def turned_copy(c, k):
                act.wait_ge(turned, c + 1)
                at_least(act, edge_mm, c - 3)
                nc.scalar.copy(erowT[:, k % 4], pb[k % 2][:, 0:P]).then_inc(turned_read, 1)

            def relu(c, k):
                act.wait_ge(msg_added, c + 1)
                at_least(act, summed, c - 3)
                nc.scalar.activation(high[:, k % 4], rows[:, k % GROUP], ACT.Relu).then_inc(high_ready, 1)

            def hot(c, k):
                act.wait_ge(turned, c + 1)
                nc.scalar.activation(hot_far[:, k % 2], iota1[:], ACT.Abs, bias=erow[:, k % GROUP, DE + 1:DE + 2]).then_inc(hot_distance, 1)
                at_least(act, summed, c - 3)
                act.wait_ge(hot_distance, c + 1)
                nc.scalar.activation(hot_dst[:, k % 4], hot_far[:, k % 2], ACT.Relu, bias=1.0, scale=-1.0).then_inc(hot_ready, 1)

            for c in range(3):
                turned_copy(c, c)
            hot(0, 0)
            relu(0, 0)

            def turn(i, last):
                for k in range(GROUP):
                    c = GROUP * i + k
                    if not last or k < GROUP - 3:
                        turned_copy(c + 3, k + 3)
                    if not last or k < GROUP - 1:
                        hot(c + 1, k + 1)
                        relu(c + 1, k + 1)

            turn(0, False)
            with act.Fori(1, DST_CHUNKS // GROUP - 1) as i:
                turn(i, False)
            turn(DST_CHUNKS // GROUP - 1, True)
            root("bn", vec[:, 1])
            def copies(t):
                if t >= 2:
                    act.wait_ge(for_dve, V[("in", t - 2)] + 1)
                copy_job(("r2T", t), r2T[t % 2])
                copy_job(("hgT", t), hgT[t % 2])

            def high_matrix(t):
                act.wait_ge(adj3_loaded[t % 2], 16 * (t // 2 + 1))
                if t >= 2:
                    act.wait_ge(for_dve, V[("agg3", t - 2)] + 1)
                nc.scalar.copy(a3[:, t % 2, 0], adj_part3[:, t % 2]).then_inc(high3, 1)

            def high_rows(k):
                act.wait_ge(h_ready, 2 * NT + k + 1)
                nc.scalar.copy(h3[:, 0, k], h[:, k]).then_inc(high3, 1)

            copies(0)
            for t in range(NT):
                if t + 1 < NT:
                    copies(t + 1)
                for k in range(2):
                    act.wait_ge(gate_in, 3 * t + k + 1)
                    nc.scalar.activation(gates[:, k], gates[:, k], ACT.Sigmoid).then_inc(gate_out, 1)
                if t == NT - 1:
                    act.wait_ge(for_dve, V[("in", t)] + 1)
                    high_matrix(0)
                act.wait_ge(gate_in, 3 * t + 3)
                nc.scalar.activation(gates[:, 2], gates[:, 2], ACT.Tanh).then_inc(gate_out, 1)
                if t == NT - 1:
                    for k in range(KT):
                        high_rows(k)
                root(("h3", t), one_rstd[:])
            for k in range(KT, NT):
                high_rows(k)
            high_matrix(1)
            high_matrix(2)

            def turned3(t):
                if t >= 2:
                    act.wait_ge(for_dve, V[("y3", t - 2)] + 1)
                copy_job(("agg3T", t), flat(hT[:, t % 2]))

            turned3(0)
            for t in range(NT - 1):
                if t + 3 < NT:
                    high_matrix(t + 3)
                turned3(t + 1)

        @block.tensor
        def _(pe):
            def to_act(job):
                at_least(pe, act_read, A[job] - 3)
                return act_bank(job)

            def to_dve(job):
                at_least(pe, dve_read, V[job] - 3)
                return dve_bank(job)

            def turn_tile(job, tile):
                b = to_act(job)
                k = tile.shape[-1] // P
                for q in range(k):
                    ins = nc.tensor.transpose(b[:, q * P:(q + 1) * P], tile[:, q * P:(q + 1) * P], ident[:])
                ins.then_inc(for_act, 1)

            def sort_products(job, cols):
                b = to_dve(job)
                nc.tensor.matmul(b[:, 0:cols], tri, ptot[:, 0:cols], start=True, stop=True)
                nc.tensor.matmul(b[:, 128:128 + cols], onesq, ptot[:, 0:cols], start=True, stop=True).then_inc(for_dve, 1)

            def linear(job, parts, wide):
                b, done = (to_dve(job), for_dve) if job in V else (to_act(job), for_act)
                n = sum(x.shape[1] for x, _ in parts)
                m = 0
                for x, w in parts:
                    for k in range(x.shape[1]):
                        ins = nc.tensor.matmul(b[:, 0:wide], x[:, k], w[:, k], start=m == 0, stop=m == n - 1)
                        m += 1
                ins.then_inc(done, 1)

            def turn_weights(n):
                pe.wait_ge(raw_loaded[n % 2], 16 * (n // 2 + 1))
                for k in range(5 if n == 0 else KT):
                    b = to_act(("w", n, k))
                    f = (k * P) % 640
                    for o in range(KT):
                        ins = nc.tensor.transpose(b[:, o * P:(o + 1) * P], wst[:, n % 2, o, f:f + P], ident[:])
                    ins.then_inc(for_act, 1)

            pe.wait_ge(const_ready, 10)
            pe.wait_ge(totals_ready, 1)
            sort_products("prefix1", B1)
            for n in range(len(blocks)):
                turn_weights(n)
                if n == PREFIX2_AFTER:
                    pe.wait_ge(totals_ready, 2)
                    sort_products("prefix2", B2)
                if blocks[n][0][0:2] == "ih":
                    gate = blocks[n][1]
                    pe.wait_ge(w2_loaded, 16)
                    pe.wait_ge(b2_ready, 1)
                    pe.wait_ge(act_read, wj[n])
                    for k in range(KT + 1):
                        job = ("m", gate, k) if k < KT else ("c", gate)
                        b = to_act(job)
                        for o in range(KT):
                            left = w2_raw[:, o, k * P:(k + 1) * P] if k < KT else b2_wide[:, o]
                            ins = nc.tensor.matmul(b[:], left, ws[:, n % 2, o], start=o == 0, stop=o == KT - 1)
                        ins.then_inc(for_act, 1)
            pe.wait_ge(sorted_all, 1)
            b = to_dve("tables")
            nc.tensor.matmul(b[0:1, 0:P], tabf[:, 0:1], ident[:], start=True, stop=True)
            nc.tensor.matmul(b[0:1, P:2 * P], tabf[:, 1:2], ident[:], start=True, stop=True)
            nc.tensor.matmul(b[0:1, 2 * P:3 * P], tabf[:, 2:3], ident[:], start=True, stop=True).then_inc(for_dve, 1)

            def build_blocks():
                def turn(i):
                    for q in range(TURN):
                        n, place = TURN * i + q, q % 4
                        at_least(pe, block_added, n - 3)
                        pe.wait_ge(src_hot, n + 1)
                        pe.wait_ge(weighted, n + 1)
                        for k in range(2):
                            ins = nc.tensor.matmul(pb[place][:, 0:3 * P], ohs[:, 2 * place + k],
                                                   ohd(2 * place + k, 1).rearrange("p a m d -> p (a m d)"), start=k == 0, stop=k == 1)
                        ins.then_inc(block_done, 1)

                turn(0)
                with pe.Fori(1, CELL_PAIRS // TURN) as i:
                    turn(i)

            pe.wait_ge(he_ready, 1)
            turn_tile(("hsT", 0), he[:, 0])
            for t in range(NT):
                if t + 1 < NT:
                    pe.wait_ge(he_ready, t + 2)
                    turn_tile(("hsT", t + 1), he[:, (t + 1) % 4])
                pe.wait_ge(act_read, A[("hsT", t)] + 1)
                linear(("ys", t), [(hT[:, t % 2], ws[:, 1])], D)
            build_blocks()
            def matrix(m, t):
                return adj3[:, m, t * NT:(t + 1) * NT]

            def sum_neighbours(job, blocks_of, rows_of, wide):
                b = to_dve(job)
                for s in range(NT):
                    ins = nc.tensor.matmul(b[:, 0:wide], blocks_of[:, s], rows_of[:, s, 0:wide],
                                           start=s == 0, stop=s == NT - 1)
                ins.then_inc(for_dve, 1)

            def sum0(t, tiles_of):
                b = to_dve(("agg0", t))
                for s in tiles_of:
                    ins = nc.tensor.matmul(b[:], matrix(0, t)[:, s], ws[:, 1, s] if s < KT else h[:, s],
                                           start=s == 0, stop=s == NT - 1)
                if tiles_of[-1] == NT - 1:
                    ins.then_inc(for_dve, 1)

            pe.wait_ge(block_added, CELL_PAIRS)
            pe.wait_ge(h0_loaded[0], 16)
            for t in range(3):
                sum0(t, range(KT))
            pe.wait_ge(h0_loaded[1], 16)
            sum0(0, range(KT, NT))
            sum0(1, range(KT, NT))
            pe.wait_ge(deg_ready, 1)
            b = to_act("deg")
            for m in range(2):
                for t in range(NT):
                    ins = nc.tensor.matmul(b[:, m * NT + t:m * NT + t + 1], deg_parts[:, m, t], ones[:], start=True, stop=True)
            ins.then_inc(for_act, 1)

            def turn0(t):
                pe.wait_ge(dve_read, V[("agg0", t)] + 1)
                turn_tile(("agg0T", t), agg0[:, t % 2])

            for t in range(NT):
                if t + 2 < NT:
                    sum0(t + 2, range(KT, NT) if t == 0 else range(NT))
                if t == 0:
                    turn0(0)
                if t + 1 < NT:
                    turn0(t + 1)
                pe.wait_ge(act_read, A[("agg0T", t)] + 1)
                linear(("y0", t), [(aggT0[:, t % 2], ws[:, 0])], D)
            pe.wait_ge(w_loaded, 32)
            for t in range(NT):
                pe.wait_ge(h_ready, t + 1)
                turn_tile(("h1T", t), h[:, t])
                if t:
                    pe.wait_ge(act_read, A[("h1T", t - 1)] + 1)
                    linear(("g1", t - 1), [(hT[:, (t - 1) % 2], w1_sb)], DH)
            pe.wait_ge(act_read, A[("h1T", NT - 1)] + 1)
            linear(("g1", NT - 1), [(hT[:, (NT - 1) % 2], w1_sb)], DH)
            pe.wait_ge(act_read, A[("g1", NT - 1)] + 1)
            for t in range(NT):
                sum_neighbours(("x1", t), matrix(1, t), g1, DH)
            pe.wait_ge(x1_ready, NT)
            sum_neighbours(("a1", 0), matrix(1, 0), x1, DH)
            sum_neighbours(("a1", 1), matrix(1, 1), x1, DH)

            def turn1(t):
                pe.wait_ge(dve_read, V[("a1", t)] + 1)
                turn_tile(("a1T", t), a1[:, t % 2])

            turn1(0)
            for t in range(NT):
                if t + 2 < NT:
                    sum_neighbours(("a1", t + 2), matrix(1, t + 2), x1, DH)
                if t + 1 < NT:
                    turn1(t + 1)
                pe.wait_ge(act_read, A[("a1T", t)] + 1)
                linear(("y1", t), [(a1T[:, t % 2], w2_sb)], D)
            pe.wait_ge(p_loaded, 16)
            for t in range(NT):
                pe.wait_ge(h_ready, NT + t + 1)
                turn_tile(("h2T", t), h[:, t])
                if t:
                    pe.wait_ge(act_read, A[("h2T", t - 1)] + 1)
                    linear(("p2", t - 1), [(h2T[:, (t - 1) % 2], ws[:, 0])], D)
            pe.wait_ge(act_read, A[("h2T", NT - 1)] + 1)
            linear(("p2", NT - 1), [(h2T[:, (NT - 1) % 2], ws[:, 0])], D)
            pe.wait_ge(w1e_loaded, 16)
            pe.wait_ge(dve_read, V[("p2", NT - 1)] + 1)

            def t_edges(i, k):
                c = GROUP * i + k
                pe.wait_ge(erow_landed[k // 4], 16 * i + 16)
                at_least(pe, turned_read, c - 1)
                nc.tensor.transpose(pb[k % 2][:, 0:P], erow[:, k, 0:DE], ident[:]).then_inc(turned, 1)

            def m_edges(i, k):
                c = GROUP * i + k
                pe.wait_ge(turned_read, c + 1)
                at_least(pe, msg_added, c - 3)
                nc.tensor.matmul(e_bank(k)[:], erowT[:, k % 4], w1e_sb, start=True, stop=True).then_inc(edge_mm, 1)

            def s_edges(i, k):
                c = GROUP * i + k
                pe.wait_ge(msg_ready, c + 1)
                pe.wait_ge(hot_ready, c + 1)
                if k % 2 == 0:
                    at_least(pe, sums_added, GROUP // 2 * i + k // 2 - 1)
                sums, hot = pb[4 + (k // 2) % 2][:], hot_dst[:, k % 4]
                nc.tensor.matmul(sums, hot, high[:, k % 4], start=k % 2 == 0, stop=False)
                nc.tensor.matmul(sums, hot, low_part[:, k % 4], start=False, stop=k % 2 == 1).then_inc(summed, 1)

            for k in range(3):
                t_edges(0, k)
            m_edges(0, 0)
            m_edges(0, 1)

            def turn(i, first, last):
                for k in range(GROUP):
                    if not last or k < GROUP - 3:
                        t_edges(i + (k + 3) // GROUP, (k + 3) % GROUP)
                    if not last or k < GROUP - 2:
                        m_edges(i + (k + 2) // GROUP, (k + 2) % GROUP)
                    if not (first and k == 0):
                        s_edges(i if k else i - 1, (k - 1) % GROUP)

            turns = DST_CHUNKS // GROUP
            turn(0, True, False)
            with pe.Fori(1, turns - 1) as i:
                turn(i, False, False)
            turn(turns - 1, False, True)
            s_edges(turns - 1, GROUP - 1)
            pe.wait_ge(gru_loaded, 16 * 6)
            pe.wait_ge(sums_added, DST_PAIRS)
            def blocks4(tile):
                return tile.rearrange("p (k n) -> p k n", k=KT)

            def turns2(t):
                turn_tile(("r2T", t), r2[:, t])
                turn_tile(("hgT", t), h[:, t])

            turns2(0)
            for t in range(NT):
                if t + 1 < NT:
                    turns2(t + 1)
                pe.wait_ge(act_read, A[("hgT", t)] + 1)
                hg, at = blocks4(hgT[t % 2]), blocks4(r2T[t % 2])
                linear(("r", t), [(hg, gru_w[:, 3]), (at, gru_w[:, 0])], D)
                linear(("z", t), [(hg, gru_w[:, 4]), (at, gru_w[:, 1])], D)
                linear(("hn", t), [(hg, gru_w[:, 5])], D)
                linear(("in", t), [(at, gru_w[:, 2])], D)
            pe.wait_ge(w3_loaded, 16)

            def sum_neighbours3(t):
                b = to_dve(("agg3", t))
                pe.wait_ge(low3, A_LOW3[t])
                for k in range(NT):
                    if t == 0:
                        pe.wait_ge(low3, k + 2)
                    for left, right in ((0, 0), (0, 1), (1, 0)):
                        ins = nc.tensor.matmul(b[:], a3[:, t % 2, left, k], h3[:, right, k], start=k == 0 and left + right == 0,
                                               stop=k == NT - 1 and left == 1)
                ins.then_inc(for_dve, 1)

            def turn3(t):
                pe.wait_ge(dve_read, V[("agg3", t)] + 1)
                turn_tile(("agg3T", t), tiles[:, 2 + t % 2])

            sum_neighbours3(0)
            sum_neighbours3(1)
            turn3(0)
            for t in range(NT):
                if t + 2 < NT:
                    sum_neighbours3(t + 2)
                if t + 1 < NT:
                    turn3(t + 1)
                pe.wait_ge(act_read, A[("agg3T", t)] + 1)
                linear(("y3", t), [(hT[:, t % 2], ws[:, 1])], D)

        @block.vector
        def _(dve):
            chain = [0]

            def link(ins):
                chain[0] += 1
                ins.then_inc(step, 1)
                dve.wait_ge(step, chain[0])

            vts, vtt, vstt = nc.vector.tensor_scalar, nc.vector.tensor_tensor, nc.vector.scalar_tensor_tensor

            dve.wait_ge(const_ready, 10)
            dve.wait_ge(edges_loaded, 16 * 8)
            link(nc.vector.tensor_copy(iob, iob_f))
            link(vts(t_i, srci, 7, None, ALU.arith_shift_right))
            link(nc.vector.tensor_copy(st_f, t_i))
            link(vts(t_j, dsti, 7, None, ALU.arith_shift_right))
            link(nc.vector.tensor_copy(dt_f, t_j))
            link(nc.vector.tensor_copy(dt_b, dt_f))
            link(vstt(cell_f, dt_f, float(NT), st_f, ALU.mult, ALU.add))
            link(nc.vector.tensor_copy(cell_b, cell_f))
            link(vts(t_i, srci, P - 1, None, ALU.bitwise_and))
            link(nc.vector.tensor_copy(st_f, t_i))
            link(vts(pay1[:, :, 0], st_f, 1.0, -1.0, ALU.add, ALU.mult))
            link(vts(t_j, dsti, P - 1, None, ALU.bitwise_and))
            link(nc.vector.tensor_copy(dt_f, t_j))
            link(vts(pay1[:, :, 1], dt_f, 1.0, None, ALU.add))
            nc.vector.tensor_copy(pay1[:, :, 2], wt_t)
            nc.vector.tensor_copy(pay1[:, :, 3], w1t_t)
            nc.vector.tensor_copy(pay2[:].bitcast(I32)[:, :, 0], srci)
            link(vts(pay2[:, :, 1], dt_f, 1.0, -1.0, ALU.add, ALU.mult))

            def places(buckets, bucket_of, chunks, job, idx, tab_cols, width, ready):
                ohb, csb = oh[:, 0:buckets], cs[:, 0:buckets]
                link(vtt(ohb, iob[:, 0:buckets].unsqueeze(2).to_broadcast([P, buckets, J]),
                         bucket_of.unsqueeze(1).to_broadcast([P, buckets, J]), ALU.is_equal))
                flat_oh = ohb.rearrange("p b j -> p (b j)")
                flat_cs = csb.rearrange("p b j -> p (b j)")
                link(nc.vector.tensor_tensor_scan(flat_cs, flat_oh, flat_oh, 0.0, ALU.add, ALU.max))
                link(nc.vector.tensor_copy(pcum[:, 0:buckets], csb[:, :, J - 1]))
                nc.vector.tensor_copy(ptot[:, 0:1], pcum[:, 0:1])
                vtt(ptot[:, 1:buckets], pcum[:, 1:buckets], pcum[:, 0:buckets - 1],
                    ALU.subtract).then_inc(totals_ready, 1)
                b = dve_bank(job)
                dve.wait_ge(for_dve, V[job] + 1)
                link(vts(cnts[:, 0:buckets], b[:, 128:128 + buckets], float(PAIR - 1), None, ALU.add))
                link(nc.vector.tensor_copy(cnti[:, 0:buckets], cnts[:, 0:buckets]))
                link(vts(cnti[:, 0:buckets], cnti[:, 0:buckets], 8, None, ALU.arith_shift_right))
                link(nc.vector.tensor_copy(nsup[:, 0:buckets], cnti[:, 0:buckets]))
                link(nc.vector.tensor_tensor_scan(endp[:, 0:buckets], nsup[:, 0:buckets], nsup[:, 0:buckets], 0.0,
                                                  ALU.add, ALU.max))
                link(vtt(offs[:, 0:buckets], endp[:, 0:buckets], nsup[:, 0:buckets], ALU.subtract))
                link(vts(offs[:, 0:buckets], offs[:, 0:buckets], float(PAIR), None, ALU.mult))
                link(nc.vector.memset(offs[:, buckets - 1:buckets], float(chunks * P)))
                link(vtt(offs[:, 0:buckets], offs[:, 0:buckets], b[:, 0:buckets], ALU.add))
                link(vtt(offs[:, 0:buckets], offs[:, 0:buckets], pcum[:, 0:buckets], ALU.subtract))
                link(vtt(offs[:, 0:buckets], offs[:, 0:buckets], ptot[:, 0:buckets], ALU.add))
                ins = vts(offs[:, 0:buckets], offs[:, 0:buckets], -1.0, None, ALU.add)
                ins.then_inc(dve_read, 1)
                dve.wait_ge(dve_read, V[job] + 1)
                for lo in range(0, J, width):
                    c = slice(lo, lo + width)
                    part = sel[:, 0:buckets * width].rearrange("p (b j) -> p b j", b=buckets)
                    for q in range(buckets):
                        ins = vstt(part[:, q], csb[:, q, c], offs[:, q:q + 1], ohb[:, q, c], ALU.add, ALU.mult)
                    link(ins)
                    link(nc.vector.tensor_reduce(sum_a[:, c], part.rearrange("p b j -> p j b"), AX_X, ALU.add))
                    link(nc.vector.tensor_copy(t_i[:, c], sum_a[:, c]))
                    link(vts(t_j[:, c], t_i[:, c], 7, None, ALU.arith_shift_right))
                    link(vts(t_i[:, c], t_i[:, c], P - 1, None, ALU.bitwise_and))
                    link(nc.vector.tensor_copy(sum_a[:, c], t_i[:, c]))
                    link(nc.vector.tensor_copy(sum_b[:, c], t_j[:, c]))
                    link(vstt(sum_a[:, c], sum_a[:, c], float(chunks + SPARE), sum_b[:, c], ALU.mult, ALU.add))
                    nc.vector.tensor_copy(idx[:, c], sum_a[:, c]).then_inc(ready, 1)
                for n, col in enumerate(tab_cols):
                    link(vts(cmp_t[:, 0:buckets - 1], endp[:, 0:buckets - 1], pidx[:, n:n + 1], None, ALU.is_le))
                    link(nc.vector.tensor_reduce(tabf[:, col:col + 1], cmp_t[:, 0:buckets - 1], AX_X, ALU.add))

            places(B1, cell_b, CELL_CHUNKS, "prefix1", idx1, [0, 1], THIRD, order_ready[0])
            link(vts(tabf[:, 0:2], tabf[:, 0:2], float(CELLS - 1), float(P), ALU.min, ALU.mult))
            places(B2, dt_b, DST_CHUNKS, "prefix2", idx2, [2], J, order_ready[1])
            vts(tabf[:, 2:3], tabf[:, 2:3], float(NT - 1), float(D), ALU.min, ALU.mult).then_inc(sorted_all, 1)
            nc.vector.memset(xs[:, NT - 1], 0.0).then_inc(x_free, 1)
            nc.vector.memset(adj[:, 6 * D:], 0.0)
            b = dve_bank("tables")
            dve.wait_ge(for_dve, V["tables"] + 1)
            link(nc.vector.tensor_copy(cell_at, b[0:1, 0:CELL_PAIRS]))
            nc.vector.tensor_copy(dst_at, b[0:1, 2 * P:2 * P + DST_PAIRS]).then_inc(dve_read, 1)
            dve.wait_ge(dve_read, V["tables"] + 1)
            def inverse_root(job, ap, square):
                square.then_inc(square_ready, 1)
                dve.wait_ge(root_ready, ROOT[job] + 1)
                link(nc.vector.reciprocal(ap, ap))

            def layernorm(job, dst, src):
                link(nc.vector.bn_stats(stats[:], src))
                link(nc.vector.bn_aggr(one_mv[:], stats[:]))
                inverse_root(job, one_rstd[:], vts(one_rstd[:], one_mv[:, 1:2], LN_EPS, None, ALU.add))
                link(vts(dst, src, one_mv[:, 0:1], one_rstd[:], ALU.subtract, ALU.mult))

            def relu_norm(job, first, end):
                inverse_root(job, rstd[:, first:end], vts(rstd[:, first:end], mv[:, first:end, 1], LN_EPS, None, ALU.add))
                for t in range(first, end):
                    link(vts(h[:, t], xs[:, t], mv[:, t, 0:1], rstd[:, t:t + 1], ALU.subtract, ALU.mult))
                    vts(h[:, t], h[:, t], 0.0, None, ALU.max).then_inc(h_ready, 1)

            def read(job, emit):
                dve.wait_ge(for_dve, V[job] + 1)
                emit(dve_bank(job)).then_inc(dve_read, 1)
                dve.wait_ge(dve_read, V[job] + 1)

            dve.wait_ge(vec_loaded, 48)

            def norm0(t):
                if t >= 4:
                    dve.wait_ge(he_stored[t % 4], 16 * (t // 4))
                    dve.wait_ge(for_act, A[("hsT", t - 4)] + 1)
                dve.wait_ge(xe_loaded[t], 16)
                layernorm(("he", t), he[:, t % 4], xs[:, t])
                vts(he[:, t % 4], he[:, t % 4], 0.0, None, ALU.max).then_inc(he_ready, 1)

            norm0(0)
            norm0(1)
            for t in range(NT):
                if t + 2 < NT:
                    norm0(t + 2)
                if t >= 2:
                    dve.wait_ge(ye_stored[t % 2], 16 * (t // 2))
                read(("ys", t), lambda b: vtt(ye[:, t % 2], b[:], vec[:, 0], ALU.add))
            dve.wait_ge(for_act, A[("hsT", NT - 1)] + 1)
            dve.wait_ge(m_stored, 16 * 6)
            for k in range(4):
                dve.wait_ge(he_stored[k], 16 * ((NT + 3 - k) // 4))
            for k in range(2):
                dve.wait_ge(ye_stored[k], 16 * (NT // 2))
            nc.vector.memset(adj[:, 0:6 * D], 0.0)
            link(nc.vector.memset(arena[:, 2 * AW:3 * AW], 0.0))
            def hots(i, q):
                n = TURN * i + q
                at_least(dve, block_done, n - 3)
                vtt(ohd(2 * (q % 4), 2)[:, :, 0], iota1[:].unsqueeze(1).to_broadcast([P, 2, P]),
                    cellm[:, bass.ds(2 * TURN * i + 2 * q, 2), 1:2].to_broadcast([P, 2, P]), ALU.is_equal).then_inc(dst_hot, 1)

            def add_block(i, q):
                n = TURN * i + q
                at = dve.value_load(cell_at[0:1, bass.ds(n, 1)], min_val=0, max_val=(CELLS - 1) * P)
                dve.wait_ge(block_done, n + 1)
                at_least(dve, block_added, n)
                cell = matrices[:, :, bass.ds(at, P)]
                vtt(cell, pb[q % 4][:, 0:3 * P].rearrange("p (m d) -> p m d", m=3), cell, ALU.add).then_inc(block_added, 1)

            def turn(i, last):
                for q in range(TURN):
                    if not last or q < TURN - 3:
                        hots(i + (q + 3) // TURN, (q + 3) % TURN)
                    add_block(i, q)

            dve.wait_ge(cells_loaded, 16)
            dve.wait_ge(wt_stored[0], 32)
            turns = CELL_PAIRS // TURN
            for q in range(3):
                hots(0, q)
            turn(0, False)
            with dve.Fori(1, turns - 1) as i:
                turn(i, False)
            turn(turns - 1, True)
            dve.wait_ge(block_added, CELL_PAIRS)
            for m in range(2):
                for t in range(NT):
                    ins = nc.vector.tensor_reduce(deg_parts[:, m, t], adj3[:, m, t * NT:(t + 1) * NT].rearrange("p s d -> p d s"),
                                                  AX_X, ALU.add)
            ins.then_inc(deg_ready, 1)
            dve.wait_ge(adj3_stored[0], 16)
            nc.vector.memset(xs[:, NT - 1], 0.0).then_inc(x_free, 1)
            dve.wait_ge(act_read, A["deg"] + 1)
            link(vts(invc[:], deg[:, 0:NT], 1.0, None, ALU.max))
            link(nc.vector.reciprocal(invc[:], invc[:]))
            link(vts(dmask[:], deg[:, NT:2 * NT], 1.0, None, ALU.add))
            inverse_root("dinv", dinv[:], vts(dinv[:], dmask[:], 2.0 ** -116, None, ALU.max))
            link(vts(dmask[:], dmask[:], 0.0, None, ALU.is_gt))
            link(vtt(dinv[:], dinv[:], dmask[:], ALU.mult))
            dve.wait_ge(adj3_stored[3], 16)

            def mean0(t):
                if t >= 2:
                    dve.wait_ge(for_act, A[("agg0T", t - 2)] + 1)
                read(("agg0", t), lambda b: vts(agg0[:, t % 2], b[:], invc[:, t:t + 1], None, ALU.mult))

            mean0(0)
            mean0(1)
            for t in range(NT):
                if t + 2 < NT:
                    mean0(t + 2)
                if t == NT - 1:
                    dve.wait_ge(adj3_stored[1], 16)
                    relu_norm("h1", 0, NT - 1)
                y = y0[:, t % 2]
                dve.wait_ge(ys_loaded[t % 2], 16 * (t // 2 + 1))
                read(("y0", t), lambda b: vtt(y, b[:], y, ALU.add))
                layernorm(("y0", t), y, y)
                link(vtt(y, y, vec[:, 1], ALU.mult))
                link(vtt(y, y, vec[:, 2], ALU.add))
                if t == 0:
                    dve.wait_ge(loaded, 16 * NT)
                chain[0] += 1
                vtt(xs[:, t], xs[:, t], y, ALU.add).then_inc(step, 1)
                dve.wait_ge(step, chain[0])
                dve.sem_inc(y_used, 1)
                link(nc.vector.bn_stats(stats[:], xs[:, t]))
                link(nc.vector.bn_aggr(mv[:, t], stats[:]))
            relu_norm(("h1", NT - 1), NT - 1, NT)
            dve.wait_ge(vec_loaded, 80)
            for t in range(NT):
                x = x1[:, t]
                read(("x1", t), lambda b: vtt(x, b[:, 0:DH], g1[:, t], ALU.add))
                link(vstt(x, x, dinv[:, t:t + 1], vec[:, 0, 0:DH], ALU.mult, ALU.add))
                vts(x, x, 0.0, dinv[:, t:t + 1], ALU.max, ALU.mult).then_inc(x1_ready, 1)
            dve.wait_ge(x1_ready, NT)

            def sum1(t):
                if t >= 2:
                    dve.wait_ge(for_act, A[("a1T", t - 2)] + 1)
                read(("a1", t), lambda b: vtt(a1[:, t % 2], b[:, 0:DH], x1[:, t], ALU.add))

            sum1(0)
            sum1(1)
            for t in range(NT):
                if t + 2 < NT:
                    sum1(t + 2)
                y = y1[:, t % 2]
                read(("y1", t), lambda b: vstt(y, b[:], dinv[:, t:t + 1], vec[:, 1], ALU.mult, ALU.add))
                link(nc.vector.tensor_tensor_reduce(h[:, t], y, y, 1.0, 0.0, ALU.mult, ALU.add, one_rstd[:]))
                inverse_root(("n1", t), one_rstd[:], vts(one_rstd[:], one_rstd[:], 1e-24, None, ALU.max))
                link(vstt(xs[:, t], y, one_rstd[:], xs[:, t], ALU.mult, ALU.add))
                layernorm(("h2", t), h[:, t], xs[:, t])
                vts(h[:, t], h[:, t], 0.0, None, ALU.max).then_inc(h_ready, 1)
            dve.wait_ge(b1_loaded, 16)
            for t in range(NT):
                if t >= 2:
                    dve.wait_ge(p_stored[t % 2], 16 * (t // 2))
                read(("p2", t), lambda b: vtt(tiles[:, 2 + t % 2], b[:], b1_v, ALU.add))
            dve.wait_ge(vec2_loaded, 16 * 11)
            link(vtt(bx_v, bx_v, vec[:, 0], ALU.add))
            vtt(by_v, by_v, vec[:, 1], ALU.add).then_inc(vec_folded, 1)
            dve.wait_ge(sums_clear, 1)

            def message(i, k):
                dve.wait_ge(edge_mm, GROUP * i + k + 1)
                dve.wait_ge(g_landed[k], 16 * i + 16)
                vtt(rows[:, k], e_bank(k)[:], rows[:, k], ALU.add).then_inc(msg_added, 1)

            def low(i, k):
                dve.wait_ge(high_ready, GROUP * i + k + 1)
                vstt(low_part[:, k % 4], rows[:, k], 0.0, high[:, k % 4].bitcast(F32), ALU.max, ALU.subtract).then_inc(msg_ready, 1)

            def add_sums(i, q):
                n = GROUP // 2 * i + q
                at = dve.value_load(dst_at[0:1, bass.ds(n, 1)], min_val=0, max_val=(NT - 1) * D)
                dve.wait_ge(summed, 2 * n + 2)
                at_least(dve, sums_added, n)
                tile = g[:, bass.ds(at, D)]
                vtt(tile, pb[4 + q % 2][:], tile, ALU.add).then_inc(sums_added, 1)

            def turn(i, first, last):
                for k in range(GROUP):
                    if not last or k < GROUP - 2:
                        message(i + (k + 2) // GROUP, (k + 2) % GROUP)
                    if not last or k < GROUP - 1:
                        low(i + (k + 1) // GROUP, (k + 1) % GROUP)
                    if k % 2 == 0 and not (first and k == 0):
                        add_sums(i if k else i - 1, (k // 2 - 1) % 4)

            turns = DST_CHUNKS // GROUP
            message(0, 0)
            message(0, 1)
            low(0, 0)
            turn(0, True, False)
            with dve.Fori(1, turns - 1) as i:
                turn(i, False, False)
            turn(turns - 1, False, True)
            add_sums(turns - 1, 3)
            dve.wait_ge(vec2_loaded, 16 * 13)
            inverse_root("bn", vec[:, 1], vts(vec[:, 1], vec[:, 1], BN_EPS, None, ALU.add))
            link(vtt(sc_v, sc_v, vec[:, 1], ALU.mult))
            link(vtt(vec[:, 0], vec[:, 0], sc_v, ALU.mult))
            link(vtt(sh_v, sh_v, vec[:, 0], ALU.subtract))
            dve.wait_ge(sums_added, DST_PAIRS)

            def low_matrix(t):
                dve.wait_ge(high3, A_LOW3[t])
                vtt(a3[:, t % 2, 1], adj_part3[:, t % 2], a3[:, t % 2, 0].bitcast(F32), ALU.subtract).then_inc(low3, 1)

            def low_rows(k):
                dve.wait_ge(high3, k + 2)
                vtt(h3[:, 1, k], h[:, k], h3[:, 0, k].bitcast(F32), ALU.subtract).then_inc(low3, 1)

            for t in range(NT):
                r, z, n, m = (gates[:, k] for k in range(4))
                count = deg[:, t:t + 1]
                for gate, name, c_v, b_v in ((r, "r", cr_v, bx_v), (z, "z", cz_v, by_v)):
                    read((name, t), lambda b: vstt(gate, c_v, count, b[:], ALU.mult, ALU.add))
                    vtt(gate, gate, b_v, ALU.add).then_inc(gate_in, 1)
                read(("hn", t), lambda b: vtt(n, b[:], bw_v, ALU.add))
                dve.wait_ge(gate_out, 3 * t + 1)
                link(vtt(n, n, r, ALU.mult))
                dve.wait_ge(gate_out, 3 * t + 2)
                link(vtt(z, z, sc_v, ALU.mult))
                factor, rest = r, xs[:, t]
                link(vtt(factor, sc_v, z, ALU.subtract))
                link(vtt(z, z, h[:, t], ALU.mult))
                link(vtt(z, z, h[:, t], ALU.add))
                link(vtt(z, z, sh_v, ALU.add))
                link(vtt(rest, rest, z, ALU.add))
                read(("in", t), lambda b: vstt(m, cn_v, count, b[:], ALU.mult, ALU.add))
                link(vtt(m, m, bz_v, ALU.add))
                vtt(n, n, m, ALU.add).then_inc(gate_in, 1)
                if t == NT - 1:
                    low_matrix(0)
                dve.wait_ge(gate_out, 3 * t + 3)
                link(vtt(n, n, factor, ALU.mult))
                link(vtt(xs[:, t], xs[:, t], n, ALU.add))
                if t == NT - 1:
                    for k in range(KT):
                        low_rows(k)
                layernorm(("h3", t), h[:, t], xs[:, t])
                vts(h[:, t], h[:, t], 0.0, None, ALU.max).then_inc(h_ready, 1)
            dve.wait_ge(vec_loaded, 96)

            def sum3(t):
                if t >= 2:
                    dve.wait_ge(for_act, A[("agg3T", t - 2)] + 1)
                read(("agg3", t), lambda b: nc.vector.tensor_copy(tiles[:, 2 + t % 2], b[:]))

            for k in range(KT, NT):
                low_rows(k)
            low_matrix(1)
            sum3(0)
            low_matrix(2)
            sum3(1)
            for t in range(NT):
                if t + 3 < NT:
                    low_matrix(t + 3)
                if t + 2 < NT:
                    sum3(t + 2)
                read(("y3", t), lambda b: vtt(xs[:, t], b[:], xs[:, t], ALU.add))
                vtt(xs[:, t], xs[:, t], vec[:, 2], ALU.add).then_inc(x_done, 1)


_INS = ["x", "src", "dst", "edge_attr_128", "edge_weight", "edge_weight1", "L0_gnn_W_self", "L0_gnn_W_neigh",
        "L0_gnn_bias", "L0_gnn_gamma", "L0_gnn_beta", "L1_gnn_W1", "L1_gnn_b1", "L1_gnn_W2", "L1_gnn_b2",
        "L2_gnn_W1", "L2_gnn_b1", "L2_gnn_W2", "L2_gnn_b2", "L2_gnn_W_ih", "L2_gnn_W_hh", "L2_gnn_b_ih",
        "L2_gnn_b_hh", "L2_gnn_gamma", "L2_gnn_beta", "L2_gnn_run_mean", "L2_gnn_run_var", "L3_gnn_W", "L3_gnn_b"]


def kernel(**inputs):
    import numpy as _np
    import concourse.bacc as _bacc
    from concourse import mybir as _mybir
    from concourse.bass_utils import run_bass_kernel_spmd as _run

    nc = _bacc.Bacc("TRN2", target_bir_lowering=False, num_devices=1)
    arrays, args = {}, []
    for name in _INS:
        a = _np.ascontiguousarray(inputs[name])
        arrays[f"in_{name}_dram"] = a
        args.append(nc.dram_tensor(f"in_{name}_dram", a.shape, _mybir.dt.from_np(a.dtype), kind="ExternalInput").ap())
    args.append(nc.dram_tensor("out_0_dram", (N, D), _mybir.dt.float32, kind="ExternalOutput").ap())
    build_gnn(nc, *args)
    r = _run(nc, [arrays], core_ids=[0])
    return r.results[0]["out_0_dram"]
```
